# Optimizing a Trainium2 kernel written in Bass

```python
import numpy as np
import jax
import jax.numpy as jnp

def _softmax(x, axis=-1):
    return jax.nn.softmax(x, axis=axis)

def _gelu(x):
    return jax.nn.gelu(x, approximate=True)

def _silu(x):
    return jax.nn.silu(x)

def _sigmoid(x):
    return jax.nn.sigmoid(x)

def _layernorm(x, axis=-1, eps=1e-05):
    m = jnp.mean(x, axis=axis, keepdims=True)
    v = jnp.var(x, axis=axis, keepdims=True)
    return (x - m) / jnp.sqrt(v + eps)

def _scatter_add(tgt, idx, src, axis=0):
    return tgt.at[idx].add(src)

def _segment_sum(src, seg, n):
    return jax.ops.segment_sum(src, seg, n)
kernel_name = 'mk_cond_seq_d2_seqx_r2_4d7d4a'

def setup_inputs(seed: int=0):
    np.random.seed(seed)
    _w = jnp.asarray

    def _rec_inputs():
        import jax
        import jax.numpy as jnp
        _rk = jax.random.key(seed)
        x = 7.22e-05 + 1 * jax.random.normal(jax.random.fold_in(_rk, 1), (8, 1024, 512), jnp.float32)
        _lenS = 1024 - jax.random.randint(jax.random.fold_in(_rk, 7), (8,), 0, max(1, 1024 // 4) + 1, jnp.int32)
        _lenS2 = 1024 - jax.random.randint(jax.random.fold_in(_rk, 8), (8,), 0, max(1, 1024 // 4) + 1, jnp.int32)
        cond_2048 = 0.00782532 + 1.00527 * jax.random.normal(jax.random.fold_in(_rk, 11), (8, 1024), jnp.float32)
        itok_S_0_1023 = jax.random.randint(jax.random.fold_in(_rk, 13), (1024,), 0, 512, jnp.int32)
        _validS = jnp.arange(1024)[None, :] < _lenS[:, None]
        _validS2 = jnp.arange(1024)[None, :] < _lenS2[:, None]
        _causal = jnp.tril(jnp.ones((1024, 1024), dtype=bool))
        mask_BxSx1_fk1 = jnp.where(jnp.ones((8, 1024, 1), dtype=bool), 1.0, 0.0).astype(jnp.float32)
        return (x, cond_2048, itok_S_0_1023, mask_BxSx1_fk1)
    x, cond_2048, itok_S_0_1023, mask_BxSx1_fk1 = _rec_inputs()

    def _L0_cond_setup():
        import jax, jax.numpy as jnp
        import numpy as np
        B, T, D, H, TE = (4, 1024, 512, 8, 1024)
        EPS = 1e-05

        def _ln(x, w, b):
            m = jnp.mean(x, axis=-1, keepdims=True)
            v = jnp.mean((x - m) ** 2, axis=-1, keepdims=True)
            return (x - m) * jax.lax.rsqrt(v + EPS) * w + b
        key = jax.random.key(seed)
        ks = jax.random.split(key, 16)
        s = 0.02
        inp = {'x': jax.random.normal(ks[0], (B, T, D), jnp.float32), 'emb': jax.random.normal(ks[1], (B, TE), jnp.float32), 'src_mask': (jax.random.uniform(ks[2], (B, T, 1)) > 0.2).astype(jnp.float32), 'num_head': H, 'ln_w': jnp.ones((D,), jnp.float32), 'ln_b': jnp.zeros((D,), jnp.float32), 'Wq': jax.random.normal(ks[3], (D, D), jnp.float32) * s, 'bq': jnp.zeros((D,), jnp.float32), 'Wk': jax.random.normal(ks[4], (D, D), jnp.float32) * s, 'bk': jnp.zeros((D,), jnp.float32), 'Wv': jax.random.normal(ks[5], (D, D), jnp.float32) * s, 'bv': jnp.zeros((D,), jnp.float32), 'W_emb': jax.random.normal(ks[6], (TE, 2 * D), jnp.float32) * s, 'b_emb': jnp.zeros((2 * D,), jnp.float32), 'ln2_w': jnp.ones((D,), jnp.float32), 'ln2_b': jnp.zeros((D,), jnp.float32), 'W_out': jax.random.normal(ks[7], (D, D), jnp.float32) * s, 'b_out': jnp.zeros((D,), jnp.float32)}
        return inp
    _L0_cond_all = _L0_cond_setup()
    _L0_cond_in = {k: v for k, v in _L0_cond_all.items() if k in ('ln_w', 'ln_b', 'Wq', 'bq', 'Wk', 'bk', 'Wv', 'bv', 'W_emb', 'b_emb', 'ln2_w', 'ln2_b', 'W_out', 'b_out')}
    del _L0_cond_all

    def _L1_cond_setup():
        import jax, jax.numpy as jnp
        import numpy as np
        B_SZ, S, D = (4, 512, 512)
        DI, DS, DTR, DC = (1024, 16, 64, 4)
        EPS = 1e-05

        def _layernorm(x, g, b):
            m = jnp.mean(x, axis=-1, keepdims=True)
            v = jnp.var(x, axis=-1, keepdims=True)
            return (x - m) * jax.lax.rsqrt(v + EPS) * g + b

        def _mamba(h, W_in, conv_w, conv_b, W_xp, W_dt, b_dt, A_log, D_param, W_out):
            bsz = h.shape[0]
            xz = h @ W_in
            xm, z = jnp.split(xz, 2, axis=-1)
            xc = jnp.transpose(xm, (0, 2, 1))
            xc = jax.lax.conv_general_dilated(xc, conv_w, (1,), [(DC - 1, 0)], feature_group_count=DI, dimension_numbers=('NCH', 'OIH', 'NCH'))
            xc = xc + conv_b[None, :, None]
            xm = jax.nn.silu(jnp.transpose(xc, (0, 2, 1)))
            xdbl = xm @ W_xp
            dtr, Bm, Cm = jnp.split(xdbl, [DTR, DTR + DS], axis=-1)
            dt = jax.nn.softplus(dtr @ W_dt + b_dt)
            A = -jnp.exp(A_log)

            def step(hst, inp):
                dt_t, B_t, C_t, x_t = inp
                dA = jnp.exp(dt_t[:, :, None] * A)
                hst = hst * dA + (dt_t * x_t)[:, :, None] * B_t[:, None, :]
                y = jnp.einsum('bds,bs->bd', hst, C_t)
                return (hst, y)
            inputs = (jnp.transpose(dt, (1, 0, 2)), jnp.transpose(Bm, (1, 0, 2)), jnp.transpose(Cm, (1, 0, 2)), jnp.transpose(xm, (1, 0, 2)))
            h0 = jnp.zeros((bsz, DI, DS), dt.dtype)
            _, ys = jax.lax.scan(step, h0, inputs)
            y = jnp.transpose(ys, (1, 0, 2)) + xm * D_param
            y = y * jax.nn.silu(z)
            return y @ W_out
        key = jax.random.key(seed)
        ks = jax.random.split(key, 12)

        def w(k, shape, scale=0.02):
            return jax.random.normal(k, shape, jnp.float32) * scale
        x = jax.random.normal(ks[0], (B_SZ, S, D), jnp.float32)
        c = jax.random.normal(ks[1], (B_SZ, 2 * D), jnp.float32)
        W_ada = w(ks[2], (2 * D, 3 * D))
        b_ada = jnp.zeros((3 * D,), jnp.float32)
        gamma = jnp.ones((D,), jnp.float32)
        beta = jnp.zeros((D,), jnp.float32)
        W_in = w(ks[3], (D, 2 * DI))
        conv_w = w(ks[4], (DI, 1, DC), 0.1)
        conv_b = jnp.zeros((DI,), jnp.float32)
        W_xp = w(ks[5], (DI, DTR + 2 * DS))
        W_dt = w(ks[6], (DTR, DI))
        b_dt = jnp.full((DI,), jnp.log(jnp.expm1(jnp.float32(0.01))), jnp.float32)
        A_log = jnp.log(jnp.broadcast_to(jnp.arange(1, DS + 1, dtype=jnp.float32), (DI, DS)))
        D_param = jnp.ones((DI,), jnp.float32)
        W_out = w(ks[7], (DI, D))
        perm = jax.random.permutation(ks[8], S)
        inv_perm = jnp.argsort(perm)
        return dict(x=x, c=c, W_ada=W_ada, b_ada=b_ada, gamma=gamma, beta=beta, W_in=W_in, conv_w=conv_w, conv_b=conv_b, W_xp=W_xp, W_dt=W_dt, b_dt=b_dt, A_log=A_log, D_param=D_param, W_out=W_out, perm=perm, inv_perm=inv_perm)
    _L1_cond_all = _L1_cond_setup()
    _L1_cond_in = {k: v for k, v in _L1_cond_all.items() if k in ('W_ada', 'b_ada', 'gamma', 'beta', 'W_in', 'conv_w', 'conv_b', 'W_xp', 'W_dt', 'b_dt', 'A_log', 'D_param', 'W_out')}
    del _L1_cond_all
    return {'x': x, 'cond_2048': cond_2048, 'itok_S_0_1023': itok_S_0_1023, 'mask_BxSx1_fk1': mask_BxSx1_fk1, 'L0_cond_ln_w': _L0_cond_in['ln_w'], 'L0_cond_ln_b': _L0_cond_in['ln_b'], 'L0_cond_Wq': _L0_cond_in['Wq'], 'L0_cond_bq': _L0_cond_in['bq'], 'L0_cond_Wk': _L0_cond_in['Wk'], 'L0_cond_bk': _L0_cond_in['bk'], 'L0_cond_Wv': _L0_cond_in['Wv'], 'L0_cond_bv': _L0_cond_in['bv'], 'L0_cond_W_emb': _L0_cond_in['W_emb'], 'L0_cond_b_emb': _L0_cond_in['b_emb'], 'L0_cond_ln2_w': _L0_cond_in['ln2_w'], 'L0_cond_ln2_b': _L0_cond_in['ln2_b'], 'L0_cond_W_out': _L0_cond_in['W_out'], 'L0_cond_b_out': _L0_cond_in['b_out'], 'L1_cond_W_ada': _L1_cond_in['W_ada'], 'L1_cond_b_ada': _L1_cond_in['b_ada'], 'L1_cond_gamma': _L1_cond_in['gamma'], 'L1_cond_beta': _L1_cond_in['beta'], 'L1_cond_W_in': _L1_cond_in['W_in'], 'L1_cond_conv_w': _L1_cond_in['conv_w'], 'L1_cond_conv_b': _L1_cond_in['conv_b'], 'L1_cond_W_xp': _L1_cond_in['W_xp'], 'L1_cond_W_dt': _L1_cond_in['W_dt'], 'L1_cond_b_dt': _L1_cond_in['b_dt'], 'L1_cond_A_log': _L1_cond_in['A_log'], 'L1_cond_D_param': _L1_cond_in['D_param'], 'L1_cond_W_out': _L1_cond_in['W_out']}

def reference(x, cond_2048, itok_S_0_1023, mask_BxSx1_fk1, L0_cond_ln_w, L0_cond_ln_b, L0_cond_Wq, L0_cond_bq, L0_cond_Wk, L0_cond_bk, L0_cond_Wv, L0_cond_bv, L0_cond_W_emb, L0_cond_b_emb, L0_cond_ln2_w, L0_cond_ln2_b, L0_cond_W_out, L0_cond_b_out, L1_cond_W_ada, L1_cond_b_ada, L1_cond_gamma, L1_cond_beta, L1_cond_W_in, L1_cond_conv_w, L1_cond_conv_b, L1_cond_W_xp, L1_cond_W_dt, L1_cond_b_dt, L1_cond_A_log, L1_cond_D_param, L1_cond_W_out):
    import jax
    import jax.numpy as jnp

    def _L0_cond_ref(x, emb, src_mask, num_head, ln_w, ln_b, Wq, bq, Wk, bk, Wv, bv, W_emb, b_emb, ln2_w, ln2_b, W_out, b_out):
        import jax, jax.numpy as jnp
        import numpy as np
        B, T, D, H, TE = (4, 1024, 512, 8, 1024)
        EPS = 1e-05

        def _ln(x, w, b):
            m = jnp.mean(x, axis=-1, keepdims=True)
            v = jnp.mean((x - m) ** 2, axis=-1, keepdims=True)
            return (x - m) * jax.lax.rsqrt(v + EPS) * w + b
        b, t, d = x.shape
        h = num_head
        dh = d // h
        xn = _ln(x, ln_w, ln_b)
        q = xn @ Wq + bq
        k = xn @ Wk + bk + (1.0 - src_mask) * -1000000.0
        q = jax.nn.softmax(q.reshape(b, t, h, dh), axis=-1)
        k = jax.nn.softmax(k.reshape(b, t, h, dh), axis=1)
        v = ((xn @ Wv + bv) * src_mask).reshape(b, t, h, dh)
        att = jnp.einsum('bnhd,bnhl->bhdl', k, v)
        y = jnp.einsum('bnhd,bhdl->bnhl', q, att).reshape(b, t, d)
        emb_out = (jax.nn.silu(emb) @ W_emb + b_emb)[:, None, :]
        scale, shift = jnp.split(emb_out, 2, axis=2)
        hh = _ln(y, ln2_w, ln2_b) * (1.0 + scale) + shift
        hh = jax.nn.silu(hh) @ W_out + b_out
        return x + hh

    def _L1_cond_ref(x, c, W_ada, b_ada, gamma, beta, W_in, conv_w, conv_b, W_xp, W_dt, b_dt, A_log, D_param, W_out, perm, inv_perm):
        import jax, jax.numpy as jnp
        import numpy as np
        B_SZ, S, D = (4, 512, 512)
        DI, DS, DTR, DC = (1024, 16, 64, 4)
        EPS = 1e-05

        def _layernorm(x, g, b):
            m = jnp.mean(x, axis=-1, keepdims=True)
            v = jnp.var(x, axis=-1, keepdims=True)
            return (x - m) * jax.lax.rsqrt(v + EPS) * g + b

        def _mamba(h, W_in, conv_w, conv_b, W_xp, W_dt, b_dt, A_log, D_param, W_out):
            bsz = h.shape[0]
            xz = h @ W_in
            xm, z = jnp.split(xz, 2, axis=-1)
            xc = jnp.transpose(xm, (0, 2, 1))
            xc = jax.lax.conv_general_dilated(xc, conv_w, (1,), [(DC - 1, 0)], feature_group_count=DI, dimension_numbers=('NCH', 'OIH', 'NCH'))
            xc = xc + conv_b[None, :, None]
            xm = jax.nn.silu(jnp.transpose(xc, (0, 2, 1)))
            xdbl = xm @ W_xp
            dtr, Bm, Cm = jnp.split(xdbl, [DTR, DTR + DS], axis=-1)
            dt = jax.nn.softplus(dtr @ W_dt + b_dt)
            A = -jnp.exp(A_log)

            def step(hst, inp):
                dt_t, B_t, C_t, x_t = inp
                dA = jnp.exp(dt_t[:, :, None] * A)
                hst = hst * dA + (dt_t * x_t)[:, :, None] * B_t[:, None, :]
                y = jnp.einsum('bds,bs->bd', hst, C_t)
                return (hst, y)
            inputs = (jnp.transpose(dt, (1, 0, 2)), jnp.transpose(Bm, (1, 0, 2)), jnp.transpose(Cm, (1, 0, 2)), jnp.transpose(xm, (1, 0, 2)))
            h0 = jnp.zeros((bsz, DI, DS), dt.dtype)
            _, ys = jax.lax.scan(step, h0, inputs)
            y = jnp.transpose(ys, (1, 0, 2)) + xm * D_param
            y = y * jax.nn.silu(z)
            return y @ W_out
        mod = jax.nn.silu(c) @ W_ada + b_ada
        shift, scale, gate = jnp.split(mod, 3, axis=1)
        h = _layernorm(x, gamma, beta)
        h = h * (1.0 + scale[:, None, :]) + shift[:, None, :]
        h = h[:, perm]
        y = _mamba(h, W_in, conv_w, conv_b, W_xp, W_dt, b_dt, A_log, D_param, W_out)
        y = y[:, inv_perm]
        return x + gate[:, None, :] * y
    x = _L0_cond_ref(x, cond_2048, mask_BxSx1_fk1, 8, L0_cond_ln_w, L0_cond_ln_b, L0_cond_Wq, L0_cond_bq, L0_cond_Wk, L0_cond_bk, L0_cond_Wv, L0_cond_bv, L0_cond_W_emb, L0_cond_b_emb, L0_cond_ln2_w, L0_cond_ln2_b, L0_cond_W_out, L0_cond_b_out)
    x = _L1_cond_ref(x, cond_2048, L1_cond_W_ada, L1_cond_b_ada, L1_cond_gamma, L1_cond_beta, L1_cond_W_in, L1_cond_conv_w, L1_cond_conv_b, L1_cond_W_xp, L1_cond_W_dt, L1_cond_b_dt, L1_cond_A_log, L1_cond_D_param, L1_cond_W_out, itok_S_0_1023, itok_S_0_1023)
    return x

_drawn_inputs = setup_inputs


def setup_inputs(seed=0):
    import zlib

    import numpy as np

    out = dict(_drawn_inputs(seed))
    spreads = {'L0_cond_ln_w': (1.0, 0.2),
     'L0_cond_ln_b': (0.0, 0.1),
     'L0_cond_bq': (0.0, 0.1),
     'L0_cond_bk': (0.0, 0.1),
     'L0_cond_bv': (0.0, 0.1),
     'L0_cond_b_emb': (0.0, 0.1),
     'L0_cond_ln2_w': (1.0, 0.2),
     'L0_cond_ln2_b': (0.0, 0.1),
     'L0_cond_b_out': (0.0, 0.1),
     'L1_cond_b_ada': (0.0, 0.1),
     'L1_cond_gamma': (1.0, 0.2),
     'L1_cond_beta': (0.0, 0.1),
     'L1_cond_conv_b': (0.0, 0.1),
     'L1_cond_b_dt': (-4.600166320800781, 0.2),
     'L1_cond_D_param': (1.0, 0.2)}
    factors = {}
    for name, (base, spread) in spreads.items():
        noise = np.random.default_rng([zlib.crc32(name.encode()), seed]).standard_normal(out[name].shape)
        drawn = base * np.exp(spread * noise) if base else spread * noise
        out[name] = jnp.asarray(drawn.astype(out[name].dtype))
    for name, factor in factors.items():
        out[name] = (out[name] * factor).astype(out[name].dtype)
    return out
```

```python
from contextlib import ExitStack

import concourse.bass as bass
from concourse import mybir

F32 = mybir.dt.float32
I32 = mybir.dt.int32
ALU = mybir.AluOpType
ACT = mybir.ActivationFunctionType
AX = mybir.AxisListType

P = 128
BATCH, SEQ, DIM = 8, 1024, 512
HEADS = 8
HEAD = DIM // HEADS
EMB = 1024
INNER, STATE, RANK, TAPS = 1024, 16, 64, 4
EPS = 1e-5
MASKED = 1e6
KD = DIM // P
KI = INNER // P
KE = EMB // P
NT = SEQ // P
CHUNK = 512
CT = CHUNK // P
CHUNKS = SEQ // CHUNK
XD = RANK + 2 * STATE
DMA = 16

VECTORS = [("L0_cond_ln_w", KD), ("L0_cond_ln_b", KD), ("L0_cond_bk", KD), ("L0_cond_ln2_w", KD), ("L0_cond_ln2_b", KD),
           ("L0_cond_b_emb", 2 * KD), ("L1_cond_b_ada", 2 * KD), ("L1_cond_gamma", KD), ("L1_cond_beta", KD),
           ("L1_cond_conv_b", KI), ("L1_cond_b_dt", KI), ("L1_cond_D_param", KI)]
COLUMN = {name: sum(n for _, n in VECTORS[:i]) for i, (name, _) in enumerate(VECTORS)}
VROWS = sum(n for _, n in VECTORS)

MM_FIRST = {"K": 0, "V": 8, "Q": 16}
MM_USES = 5 * NT
MM = {"y": 0, "K": 8, "V": 16, "Q": 24, "W": 32}
MM_LAST = {"y": 0, "W": 8}
TR_FIRST = {"z": 0, "q": 8, "k": 16}
TR_USES = 4 * NT
TR = {"z": 0, "y": 8, "q": 16, "k": 24}
TR_LAST = {"y": 0}
MM_RING, TR_RING = 4, 2

A_USE = {"h": 0, "xm": 4, "xd": 12, "dt": 13, "C": 21, "init": 22, "z": 30}
A_USES = 38
V_USE = {"y": 0, "out": 8}
V_USES = 12
RING = 4
HALVES = 2 * STATE
PIECES = 2 * HALVES


class Shared:
    pass


def need(eng, semaphore, value):
    if not (isinstance(value, int) and value <= 0):
        eng.wait_ge(semaphore, value)


def mm_use(b, stage):
    if isinstance(b, int) and b == 0:
        return MM_FIRST[stage]
    base = MM_USES * b - 2 * NT
    return base + (MM_LAST if isinstance(b, int) and b == BATCH else MM)[stage]


def tr_use(b, stage):
    if isinstance(b, int) and b == 0:
        return TR_FIRST[stage]
    base = TR_USES * b - NT
    return base + (TR_LAST if isinstance(b, int) and b == BATCH else TR)[stage]


def cond_mamba_kernel(nc, a):
    g = Shared()

    def scratch(name, shape):
        return nc.dram_tensor(name, shape, F32).ap()

    g.x1_dram = scratch("x1_rows", [BATCH * SEQ, DIM])
    g.y_dram = scratch("y_rows", [SEQ, DIM])
    g.gate_dram = scratch("gate_rows", [BATCH, DIM])
    g.b_dram = scratch("b_rows", [BATCH * CHUNKS, STATE, CHUNK])

    with ExitStack() as whole:
        def sb(name, shape, dt=F32):
            return whole.enter_context(nc.sbuf_tensor(name, shape, dt))

        g.banks = [whole.enter_context(nc.psum_tensor(f"bank{i}", [P, 512], F32)) for i in range(8)]
        g.ident = sb("ident", [P, P])
        g.cols = sb("cols", [P, VROWS])
        g.mod_l0 = sb("mod_l0", [P, BATCH, 2 * KD + NT])
        g.mod_l1 = sb("mod_l1", [P, BATCH, 2 * KD])
        g.decay = sb("decay", [P, KI, STATE])
        g.taps = sb("taps", [P, KI, TAPS])
        g.idx_first = sb("idx_first", [P, NT], I32)
        g.idx_in = sb("idx_in", [P, NT], I32)
        g.idx_max = sb("idx_max", [1, 1], I32)
        g.mhalf = sb("mhalf", [P, NT])

        with ExitStack() as weights:
            def sl(name, shape):
                return weights.enter_context(nc.sbuf_tensor(name, shape, F32))

            g.w_qkv = {n: sl(f"w_{n}", [P, KD, DIM]) for n in "qkv"}
            g.w_out = sl("w_out", [P, KD, DIM])
            g.q_bias = sl("q_bias", [P, DIM])
            g.v_bias = sl("v_bias", [P, DIM])
            g.out_bias = sl("out_bias", [P, DIM])
            g.k_bias = sl("k_bias", [P, KD])
            g.att = sl("att", [P, KD, P])
            prologue(nc, a, g)
            layer0(nc, a, g)
        layer1(nc, a, g)


def column(g, name, k):
    return g.cols[:, COLUMN[name] + k:COLUMN[name] + k + 1]


def prologue(nc, a, g):
    banks, ident, cols = g.banks, g.ident, g.cols

    with ExitStack() as ctx:
        def sb(name, shape, dt=F32):
            return ctx.enter_context(nc.sbuf_tensor(name, shape, dt))

        def sem(name):
            return ctx.enter_context(nc.semaphore(name))

        rows = sb("rows", [VROWS, P])
        idx_row = sb("idx_row", [1, SEQ], I32)
        mask_in = sb("mask_in", [BATCH * NT, P])
        cond = sb("cond", [BATCH, EMB])
        cond_silu = sb("cond_silu", [BATCH, EMB])
        cond_t = sb("cond_t", [P, KE, BATCH])
        w_emb = sb("w_emb", [P, KE, 2 * DIM])
        w_ada = sb("w_ada", [P, KE, 3 * DIM])
        ln_b_wide = sb("ln_b_wide", [P, KD, P])
        emb = sb("emb", [P, 2 * KD, BATCH])
        ada = sb("ada", [P, 2 * KD, BATCH])
        gate_bias = sb("gate_bias", [BATCH, DIM])
        gate = sb("gate", [BATCH, DIM])
        a_raw = sb("a_raw", [P, KI, STATE])
        a_exp = sb("a_exp", [P, KI, STATE])

        rows_loaded = sem("rows_loaded")
        small_loaded = sem("small_loaded")
        cond_loaded = sem("cond_loaded")
        qkv_loaded = sem("qkv_loaded")
        emb_loaded = sem("emb_loaded")
        ada_loaded = sem("ada_loaded")
        gate_stored = sem("gate_stored")
        ident_zero = sem("ident_zero")
        ident_ready = sem("ident_ready")
        silu_ready = sem("silu_ready")
        decay_exp = sem("decay_exp")
        turned = sem("turned")
        cols_ready = sem("cols_ready")
        cond_ready = sem("cond_ready")
        wide_ready = sem("wide_ready")
        bias_ready = sem("bias_ready")
        mods_ready = sem("mods_ready")
        folded = sem("folded")
        block = ctx.enter_context(nc.Block())

        @block.sync
        def _(sp):
            for name, n in VECTORS:
                at = COLUMN[name]
                sp.dma_start(rows[at:at + n, :], a[name].rearrange("(k p) -> k p", p=P)[0:n, :]).then_inc(rows_loaded, DMA)
            sp.dma_start(mask_in[:, :], a["mask_BxSx1_fk1"].rearrange("b (t p) o -> (b t) (p o)", p=P)).then_inc(rows_loaded, DMA)
            sp.dma_start(cond[:, :], a["cond_2048"]).then_inc(cond_loaded, DMA)
            for n in "qvk":
                sp.dma_start(g.w_qkv[n][:, :, :], a[f"L0_cond_W{n}"].rearrange("(k p) n -> p k n", p=P)).then_inc(qkv_loaded, DMA)
            sp.dma_start(w_emb[:, :, :], a["L0_cond_W_emb"].rearrange("(k p) n -> p k n", p=P)).then_inc(emb_loaded, DMA)
            sp.dma_start(w_ada[:, :, :], a["L1_cond_W_ada"].rearrange("(k p) n -> p k n", p=P)).then_inc(ada_loaded, DMA)
            sp.wait_ge(folded, 18)
            sp.dma_start(g.gate_dram, gate[:, :]).then_inc(gate_stored, DMA)
            sp.wait_ge(gate_stored, DMA)

        @block.scalar
        def _(act):
            act.dma_start(g.q_bias[:, :], a["L0_cond_bq"].partition_broadcast(P)).then_inc(small_loaded, DMA)
            act.dma_start(g.v_bias[:, :], a["L0_cond_bv"].partition_broadcast(P)).then_inc(small_loaded, DMA)
            act.dma_start(g.out_bias[:, :], a["L0_cond_b_out"].partition_broadcast(P)).then_inc(small_loaded, DMA)
            act.dma_start(gate_bias[:, :], a["L1_cond_b_ada"][2 * DIM:3 * DIM].partition_broadcast(BATCH)).then_inc(small_loaded, DMA)
            act.dma_start(a_raw[:, :, :], a["L1_cond_A_log"].rearrange("(k p) s -> p k s", p=P)).then_inc(small_loaded, DMA)
            act.dma_start(g.taps[:, :, :], a["L1_cond_conv_w"].rearrange("(k p) o t -> p k (o t)", p=P)).then_inc(small_loaded, DMA)
            act.dma_start(g.idx_first[:, :], a["itok_S_0_1023"].rearrange("(t p) -> p t", p=P), allow_slow_non_contiguous=True).then_inc(small_loaded, DMA)
            act.dma_start(idx_row[:, :], a["itok_S_0_1023"].rearrange("(o s) -> o s", o=1)).then_inc(small_loaded, DMA)
            act.dma_start(g.w_out[:, :, :], a["L0_cond_W_out"].rearrange("(k p) n -> p k n", p=P)).then_inc(small_loaded, DMA)
            act.wait_ge(cond_loaded, DMA)
            nc.scalar.activation(cond_silu[:, :], cond[:, :], ACT.Silu).then_inc(silu_ready, 1)
            act.wait_ge(small_loaded, 9 * DMA)
            nc.scalar.activation(a_exp[:, :, :], a_raw[:, :, :], ACT.Exp).then_inc(decay_exp, 1)

        @block.gpsimd
        def _(pool):
            nc.gpsimd.memset(ident[:, :], 0.0).then_inc(ident_zero, 1)
            nc.gpsimd.memset(g.mhalf[:, :], -0.5).then_inc(ident_zero, 1)
            pool.wait_ge(ident_zero, 1)
            nc.gpsimd.affine_select(out=ident[:, :], in_=ident[:, :], compare_op=ALU.not_equal, fill=1.0, base=0,
                                    pattern=[[-1, P]], channel_multiplier=1).then_inc(ident_ready, 1)
            pool.wait_ge(ident_zero, 2)

        @block.tensor
        def _(pe):
            pe.wait_ge(ident_ready, 1)
            pe.wait_ge(rows_loaded, (len(VECTORS) + 1) * DMA)
            nc.tensor.transpose(banks[0][:, 0:VROWS], rows[:, :], ident[0:VROWS, 0:VROWS]).then_inc(turned, 1)
            nc.tensor.transpose(banks[1][:, 0:BATCH * NT], mask_in[:, :], ident[0:BATCH * NT, 0:BATCH * NT]).then_inc(turned, 1)
            pe.wait_ge(silu_ready, 1)
            for k in range(KE):
                last = nc.tensor.transpose(banks[2][:, k * BATCH:(k + 1) * BATCH], cond_silu[:, k * P:(k + 1) * P],
                                           ident[0:BATCH, 0:BATCH])
            last.then_inc(turned, 1)
            pe.wait_ge(wide_ready, 1)
            pe.wait_ge(qkv_loaded, 3 * DMA)
            for bank, n in ((3, "q"), (4, "v")):
                for k in range(KD):
                    last = nc.tensor.matmul(banks[bank][:, :], ln_b_wide[:, k, :], g.w_qkv[n][:, k, :], start=(k == 0), stop=(k == KD - 1))
            for i in range(KD):
                for k in range(KD):
                    last = nc.tensor.matmul(banks[5][:, i:i + 1], g.w_qkv["k"][:, k, i * P:(i + 1) * P], column(g, "L0_cond_ln_b", k),
                                            start=(k == 0), stop=(k == KD - 1))
            last.then_inc(bias_ready, 1)
            pe.wait_ge(cond_ready, 1)
            for bank, w, arrived in ((6, w_emb, emb_loaded), (7, w_ada, ada_loaded)):
                pe.wait_ge(arrived, DMA)
                for m in range(2 * KD):
                    for k in range(KE):
                        last = nc.tensor.matmul(banks[bank][:, m * BATCH:(m + 1) * BATCH], w[:, k, m * P:(m + 1) * P], cond_t[:, k, :],
                                                start=(k == 0), stop=(k == KE - 1))
                last.then_inc(mods_ready, 1)
            for k in range(KE):
                last = nc.tensor.matmul(banks[0][0:BATCH, :], cond_t[:, k, :], w_ada[:, k, 2 * DIM:3 * DIM], start=(k == 0), stop=(k == KE - 1))
            last.then_inc(mods_ready, 1)

        @block.vector
        def _(dve):
            def wide(name, n):
                return cols[:, COLUMN[name]:COLUMN[name] + n].unsqueeze(2).to_broadcast([P, n, BATCH])

            nc.vector.memset(g.att[:, :, :], 0.0).then_inc(folded, 1)
            dve.wait_ge(turned, 2)
            nc.vector.tensor_copy(cols[:, :], banks[0][:, 0:VROWS]).then_inc(cols_ready, 1)
            nc.vector.tensor_copy(g.mod_l0[:, :, 2 * KD:], banks[1][:, 0:BATCH * NT].rearrange("p (b t) -> p b t", b=BATCH)).then_inc(cols_ready, 1)
            dve.wait_ge(cols_ready, 2)
            nc.vector.tensor_copy(ln_b_wide[:, :, :], cols[:, COLUMN["L0_cond_ln_b"]:COLUMN["L0_cond_ln_b"] + KD].unsqueeze(2).to_broadcast([P, KD, P])).then_inc(wide_ready, 1)
            dve.wait_ge(turned, 3)
            nc.vector.tensor_copy(cond_t[:, :, :], banks[2][:, 0:KE * BATCH].rearrange("p (k b) -> p k b", k=KE)).then_inc(cond_ready, 1)
            dve.wait_ge(small_loaded, 9 * DMA)
            dve.wait_ge(decay_exp, 1)
            nc.vector.tensor_scalar(g.decay[:, :, :], a_exp[:, :, :], -1.0, None, ALU.mult).then_inc(folded, 1)
            nc.vector.tensor_reduce(g.idx_max[:, :], idx_row[:, :], AX.X, ALU.max).then_inc(folded, 1)
            nc.vector.tensor_copy(g.idx_in[:, :], g.idx_first[:, :]).then_inc(folded, 1)
            dve.wait_ge(bias_ready, 1)
            nc.vector.tensor_tensor(g.q_bias[:, :], banks[3][:, :], g.q_bias[:, :], ALU.add).then_inc(folded, 1)
            nc.vector.tensor_tensor(g.v_bias[:, :], banks[4][:, :], g.v_bias[:, :], ALU.add).then_inc(folded, 1)
            nc.vector.tensor_tensor(g.k_bias[:, :], banks[5][:, 0:KD], cols[:, COLUMN["L0_cond_bk"]:COLUMN["L0_cond_bk"] + KD], ALU.add).then_inc(folded, 1)
            for n in "qkv":
                for k in range(KD):
                    last = nc.vector.tensor_scalar(g.w_qkv[n][:, k, :], g.w_qkv[n][:, k, :], column(g, "L0_cond_ln_w", k), None, ALU.mult)
                last.then_inc(folded, 1)
            dve.wait_ge(mods_ready, 1)
            nc.vector.tensor_tensor(emb[:, :, :], banks[6][:, 0:2 * KD * BATCH].rearrange("p (m b) -> p m b", b=BATCH), wide("L0_cond_b_emb", 2 * KD), ALU.add).then_inc(folded, 1)
            dve.wait_ge(mods_ready, 3)
            nc.vector.tensor_tensor(ada[:, :, :], banks[7][:, 0:2 * KD * BATCH].rearrange("p (m b) -> p m b", b=BATCH), wide("L1_cond_b_ada", 2 * KD), ALU.add).then_inc(folded, 1)
            dve.wait_ge(folded, 12)
            for m, mod, scale, shift, w, b in ((emb, g.mod_l0, 0, KD, "L0_cond_ln2_w", "L0_cond_ln2_b"), (ada, g.mod_l1, KD, 0, "L1_cond_gamma", "L1_cond_beta")):
                turned_mod = mod[:, :, :].rearrange("p b i -> p i b")
                nc.vector.scalar_tensor_tensor(turned_mod[:, 0:KD, :], m[:, scale:scale + KD, :], 1.0, wide(w, KD), ALU.add, ALU.mult).then_inc(folded, 1)
                nc.vector.scalar_tensor_tensor(turned_mod[:, KD:2 * KD, :], m[:, scale:scale + KD, :], 1.0, wide(b, KD), ALU.add, ALU.mult).then_inc(folded, 1)
            dve.wait_ge(folded, 16)
            for m, mod, shift, at in ((emb, g.mod_l0, KD, 15), (ada, g.mod_l1, 0, 17)):
                turned_mod = mod[:, :, :].rearrange("p b i -> p i b")[:, KD:2 * KD, :]
                last = nc.vector.tensor_tensor(turned_mod, turned_mod, m[:, shift:shift + KD, :], ALU.add)
            last.then_inc(folded, 1)
            nc.vector.tensor_tensor(gate[:, :], banks[0][0:BATCH, :], gate_bias[:, :], ALU.add).then_inc(folded, 1)
            dve.wait_ge(folded, 18)


def layer0(nc, a, g):
    banks, ident = g.banks, g.ident
    x_rows = a["x"].rearrange("b (t p) d -> b p t d", p=P)
    x1_rows = g.x1_dram.rearrange("(b t p) d -> b p t d", p=P, t=NT)
    mask_rows = a["mask_BxSx1_fk1"].rearrange("b s o -> b (s o)")

    with ExitStack() as ctx:
        def sb(name, shape):
            return ctx.enter_context(nc.sbuf_tensor(name, shape, F32))

        def sem(name):
            return ctx.enter_context(nc.semaphore(name))

        z = sb("z", [P, NT, DIM])
        z_t = sb("z_t", [P, KD, SEQ])
        k_t = sb("k_t", [P, KD, SEQ])
        k_exp = sb("k_exp", [P, NT, DIM])
        values = sb("values", [P, NT, DIM])
        qy = sb("qy", [P, NT, DIM])
        q_t = sb("q_t", [P, KD, SEQ])
        h_t = sb("h_t", [P, KD, SEQ])
        res = sb("res", [P, NT, DIM])
        mask_add = sb("mask_add", [P, SEQ])
        mod_cur = sb("mod_cur", [P, 2 * KD])
        mask_cur = sb("mask_cur", [P, NT])
        x_raw = sb("x_raw", [P, NT, 6])
        x_mv = sb("x_mv", [P, NT, 2])
        x_var = sb("x_var", [P, NT])
        x_rs = sb("x_rs", [P, NT])
        y_raw = sb("y_raw", [P, NT, 6])
        y_mv = sb("y_mv", [P, NT, 2])
        y_var = sb("y_var", [P, NT])
        y_rs = sb("y_rs", [P, NT])
        k_top = sb("k_top", [P, KD])
        k_sum = sb("k_sum", [P, KD])
        k_inv = sb("k_inv", [P, KD])
        q_top = sb("q_top", [P, NT, HEADS])
        q_sum = sb("q_sum", [P, NT, HEADS])
        q_inv = sb("q_inv", [P, NT, HEADS])

        x_loaded, res_loaded, mask_loaded, x1_stored = (sem(n) for n in ("x_loaded", "res_loaded", "mask_loaded", "x1_stored"))
        x_stats, x_aggr, x_var_ready, x_rs_ready, z_ready = (sem(n) for n in ("x_stats", "x_aggr", "x_var_ready", "x_rs_ready", "z_ready"))
        y_stats, y_aggr, y_var_ready, y_rs_ready, y_normed = (sem(n) for n in ("y_stats", "y_aggr", "y_var_ready", "y_rs_ready", "y_normed"))
        mm_ready, mm_empty, tr_ready, tr_empty = (sem(n) for n in ("mm_ready", "mm_empty", "tr_ready", "tr_empty"))
        mod_ready, mask_cur_ready, mask_ready = (sem(n) for n in ("mod_ready", "mask_cur_ready", "mask_ready"))
        k_top_ready, k_exp_ready, k_inv_ready = (sem(n) for n in ("k_top_ready", "k_exp_ready", "k_inv_ready"))
        q_top_ready, q_shifted, q_exp_ready, q_summed, q_inv_ready = (sem(n) for n in ("q_top_ready", "q_shifted", "q_exp_ready", "q_summed", "q_inv_ready"))
        kv_ready, att_ready, res_ready = (sem(n) for n in ("kv_ready", "att_ready", "res_ready"))
        started, passed = sem("started"), sem("passed")
        block = ctx.enter_context(nc.Block())

        def batch(ap, b):
            names = "p t d"[:2 * (len(ap.shape) - 1) - 1] if len(ap.shape) == 4 else "t"
            if names == "t":
                return ap[bass.ds(b, 1)]
            return ap[bass.ds(b, 1)].rearrange("o p t d -> (o p) t d")

        def iterations(eng, body):
            body(0, False, True, True)
            with eng.Fori(1, BATCH - 1) as b:
                body(b, True, True, True)
            body(BATCH - 1, True, True, False)
            body(BATCH, True, False, False)

        @block.sync
        def _(sp):
            sp.dma_start(z[:, :, :], batch(x_rows, 0)).then_inc(x_loaded, DMA)

            def body(b, prev, cur, more):
                if prev:
                    sp.wait_ge(x_loaded, DMA)
                    sp.dma_start(res[:, :, :], batch(x_rows, b - 1)).then_inc(res_loaded, DMA)
                if cur:
                    if not (isinstance(b, int) and b == 0):
                        need(sp, mm_empty, mm_use(b, "y") - 2 * NT)
                    sp.wait_ge(x_loaded, DMA)
                    sp.dma_start(mask_add[:, :], mask_rows[bass.ds(b, 1)].rearrange("o s -> (o s)").partition_broadcast(P)).then_inc(mask_loaded, DMA)
                if more:
                    need(sp, tr_ready, tr_use(b, "z") + NT)
                    sp.wait_ge(x_loaded, DMA)
                    sp.dma_start(z[:, :, :], batch(x_rows, b + 1)).then_inc(x_loaded, DMA)
                if prev:
                    need(sp, mm_empty, mm_use(b, "W") + NT)
                    sp.wait_ge(x_loaded, DMA)
                    sp.dma_start(batch(x1_rows, b - 1), res[:, :, :]).then_inc(x1_stored, DMA)
                    need(sp, x1_stored, DMA * b)
                    sp.sem_inc(passed, 1)

            iterations(sp, body)

        @block.tensor
        def _(pe):
            def product(use, stationary, moving, blocks):
                n, at = use
                need(pe, mm_empty, n + at - (MM_RING - 1))
                out = banks[at % MM_RING]
                for k in range(blocks):
                    last = nc.tensor.matmul(out[:, :], stationary(k), moving(k), start=(k == 0), stop=(k == blocks - 1))
                last.then_inc(mm_ready, 1)

            def turn(n, at, sources):
                need(pe, tr_empty, n + at - (TR_RING - 1))
                out = banks[MM_RING + at % TR_RING]
                for j, source in enumerate(sources):
                    last = nc.tensor.transpose(out[:, j * P:(j + 1) * P], source, ident[:, :])
                last.then_inc(tr_ready, 1)

            def body(b, prev, cur, more):
                if prev:
                    need(pe, tr_empty, tr_use(b - 1, "q") + NT)
                    need(pe, att_ready, 2 * b)
                    n = mm_use(b, "y")
                    for t in range(NT):
                        need(pe, mm_empty, n + t - (MM_RING - 1))
                        for i in range(KD):
                            last = nc.tensor.matmul(banks[t % MM_RING][:, i * P:(i + 1) * P], q_t[:, i, t * P:(t + 1) * P], g.att[:, i, :],
                                                    start=True, stop=True)
                        last.then_inc(mm_ready, 1)
                if cur:
                    n = tr_use(b, "z")
                    for half in range(2):
                        need(pe, z_ready, NT * b + 4 * half + 4)
                        for i in range(KD):
                            turn(n, 4 * half + i, [z[:, 4 * half + j, i * P:(i + 1) * P] for j in range(4)])
                    need(pe, tr_empty, n + NT)
                    n = mm_use(b, "K")
                    for i in range(KD):
                        for half in range(2):
                            product((n, 2 * i + half), lambda k: g.w_qkv["k"][:, k, i * P:(i + 1) * P],
                                    lambda k: z_t[:, k, half * 512:(half + 1) * 512], KD)
                    n = mm_use(b, "V")
                    for t in range(NT):
                        product((n, t), lambda k: z_t[:, k, t * P:(t + 1) * P], lambda k: g.w_qkv["v"][:, k, :], KD)
                if prev:
                    n = tr_use(b, "y")
                    for half in range(2):
                        need(pe, y_normed, NT * (b - 1) + 4 * half + 4)
                        for i in range(KD):
                            turn(n, 4 * half + i, [qy[:, 4 * half + j, i * P:(i + 1) * P] for j in range(4)])
                if cur:
                    n = mm_use(b, "Q")
                    for t in range(NT):
                        product((n, t), lambda k: z_t[:, k, t * P:(t + 1) * P], lambda k: g.w_qkv["q"][:, k, :], KD)
                if prev:
                    need(pe, tr_empty, tr_use(b, "y") + NT)
                    n = mm_use(b, "W")
                    for t in range(NT):
                        product((n, t), lambda k: h_t[:, k, t * P:(t + 1) * P], lambda k: g.w_out[:, k, :], KD)
                if cur:
                    n = tr_use(b, "q")
                    for half in range(2):
                        need(pe, q_exp_ready, NT * b + 4 * half + 4)
                        for i in range(KD):
                            turn(n, 4 * half + i, [qy[:, 4 * half + j, i * P:(i + 1) * P] for j in range(4)])
                    n = tr_use(b, "k")
                    need(pe, k_exp_ready, KD * b + KD)
                    for t in range(NT):
                        turn(n, t, [k_t[:, i, t * P:(t + 1) * P] for i in range(KD)])
                    need(pe, tr_empty, n + NT)
                    need(pe, att_ready, 2 * b)
                    for i in range(KD):
                        for t in range(NT):
                            last = nc.tensor.matmul(banks[6][:, i * P:(i + 1) * P], k_exp[:, t, i * P:(i + 1) * P], values[:, t, i * P:(i + 1) * P],
                                                    start=(t == 0), stop=(t == NT - 1))
                    last.then_inc(kv_ready, 1)

            iterations(pe, body)

        @block.scalar
        def _(act):
            def bank(at):
                return banks[MM_RING + at % TR_RING]

            def body(b, prev, cur, more):
                if cur:
                    n = tr_use(b, "z")
                    for half in range(2):
                        for i in range(KD):
                            need(act, tr_ready, n + 4 * half + i + 1)
                            nc.scalar.copy(z_t[:, i, half * 512:(half + 1) * 512], bank(i)[:, :]).then_inc(tr_empty, 1)
                    for i in range(KD):
                        need(act, k_top_ready, KD * b + i + 1)
                        nc.scalar.activation(k_t[:, i, :], k_t[:, i, :], ACT.Exp, bias=k_top[:, i:i + 1],
                                             accum_out=k_sum[:, i:i + 1]).then_inc(k_exp_ready, 1)
                if prev:
                    need(act, mod_ready, b)
                    n = tr_use(b, "y")
                    for half in range(2):
                        for i in range(KD):
                            need(act, tr_ready, n + 4 * half + i + 1)
                            nc.scalar.activation(h_t[:, i, half * 512:(half + 1) * 512], bank(i)[:, :], ACT.Silu, scale=mod_cur[:, i:i + 1],
                                                 bias=mod_cur[:, KD + i:KD + i + 1]).then_inc(tr_empty, 1)
                if cur:
                    for t in range(NT):
                        need(act, q_shifted, NT * b + t + 1)
                        nc.scalar.activation(qy[:, t, :], qy[:, t, :], ACT.Exp).then_inc(q_exp_ready, 1)
                    n = tr_use(b, "q")
                    for half in range(2):
                        for i in range(KD):
                            need(act, tr_ready, n + 4 * half + i + 1)
                            nc.scalar.copy(q_t[:, i, half * 512:(half + 1) * 512], bank(i)[:, :]).then_inc(tr_empty, 1)
                    n = tr_use(b, "k")
                    need(act, mask_cur_ready, b + 1)
                    for t in range(NT):
                        need(act, tr_ready, n + t + 1)
                        nc.scalar.mul(k_exp[:, t, :], bank(t)[:, :], mask_cur[:, t:t + 1]).then_inc(tr_empty, 1)

            iterations(act, body)

        @block.gpsimd
        def _(pool):
            nc.gpsimd.wait_ge(x_var_ready, 1)
            nc.gpsimd.tensor_tensor(x_rs[:, :], x_var[:, :], g.mhalf[:, :], ALU.pow).then_inc(x_rs_ready, 1)

            def body(b, prev, cur, more):
                if prev:
                    need(pool, y_var_ready, b)
                    nc.gpsimd.tensor_tensor(y_rs[:, :], y_var[:, :], g.mhalf[:, :], ALU.pow).then_inc(y_rs_ready, 1)
                    need(pool, res_loaded, DMA * b)
                    for t in range(NT):
                        nc.gpsimd.tensor_tensor(res[:, t, :], res[:, t, :], g.out_bias[:, :], ALU.add).then_inc(res_ready, 1)
                if more:
                    need(pool, x_var_ready, b + 2)
                    nc.gpsimd.tensor_tensor(x_rs[:, :], x_var[:, :], g.mhalf[:, :], ALU.pow).then_inc(x_rs_ready, 1)
                if cur:
                    for t in range(NT):
                        need(pool, q_top_ready, NT * b + t + 1)
                        heads = qy[:, t, :].rearrange("p (h d) -> p h d", h=HEADS)
                        nc.gpsimd.tensor_tensor(heads, heads, q_top[:, t, :].unsqueeze(2).to_broadcast([P, HEADS, HEAD]), ALU.add).then_inc(q_shifted, 1)

            iterations(pool, body)

        @block.vector
        def _(dve):
            def moments(n, src, raw, mv, var, stats, aggr, var_ready):
                for t in range(NT):
                    nc.vector.bn_stats(raw[:, t, :], src[:, t, :]).then_inc(stats, 1)
                for t in range(NT):
                    if t == 0:
                        need(dve, stats, NT * n + NT)
                        dve.sem_inc(started, 1)
                    nc.vector.bn_aggr(mv[:, t, :], raw[:, t, :]).then_inc(aggr, 1)
                need(dve, aggr, NT * n + NT)
                nc.vector.tensor_scalar(var[:, :], mv[:, :, 1], EPS, None, ALU.add).then_inc(var_ready, 1)

            def normed(src, mv, rs, ready):
                for t in range(NT):
                    nc.vector.tensor_scalar(src[:, t, :], src[:, t, :], mv[:, t, 0:1], rs[:, t:t + 1], ALU.subtract, ALU.mult).then_inc(ready, 1)

            def body(b, prev, cur, more):
                if prev:
                    need(dve, tr_empty, tr_use(b, "y") - 8)
                    dve.wait_ge(started, 1)
                    nc.vector.tensor_copy(mod_cur[:, :], g.mod_l0[:, bass.ds(b - 1, 1), 0:2 * KD].rearrange("p o i -> p (o i)")).then_inc(mod_ready, 1)
                if cur:
                    if not (isinstance(b, int) and b == 0):
                        need(dve, tr_empty, tr_use(b, "z"))
                    dve.wait_ge(started, 1)
                    nc.vector.tensor_copy(mask_cur[:, :], g.mod_l0[:, bass.ds(b, 1), 2 * KD:].rearrange("p o i -> p (o i)")).then_inc(mask_cur_ready, 1)
                if prev:
                    n = mm_use(b, "y")
                    need(dve, q_inv_ready, b)
                    for t in range(NT):
                        need(dve, mm_ready, n + t + 1)
                        nc.vector.tensor_tensor(qy[:, t, :].rearrange("p (h d) -> p h d", h=HEADS),
                                                banks[t % MM_RING][:, :].rearrange("p (h d) -> p h d", h=HEADS),
                                                q_inv[:, t, :].unsqueeze(2).to_broadcast([P, HEADS, HEAD]), ALU.mult).then_inc(mm_empty, 1)
                    need(dve, mm_empty, n + NT)
                    moments(b - 1, qy, y_raw, y_mv, y_var, y_stats, y_aggr, y_var_ready)
                if cur:
                    need(dve, mask_loaded, DMA * (b + 1))
                    nc.vector.tensor_scalar(mask_add[:, :], mask_add[:, :], 1.0, MASKED, ALU.subtract, ALU.mult).then_inc(mask_ready, 1)
                    need(dve, mask_ready, b + 1)
                    n = mm_use(b, "K")
                    for i in range(KD):
                        for half in range(2):
                            need(dve, mm_ready, n + 2 * i + half + 1)
                            nc.vector.scalar_tensor_tensor(k_t[:, i, half * 512:(half + 1) * 512], banks[(2 * i + half) % MM_RING][:, :], g.k_bias[:, i:i + 1],
                                                           mask_add[:, half * 512:(half + 1) * 512], ALU.add, ALU.add).then_inc(mm_empty, 1)
                        need(dve, mm_empty, n + 2 * i + 2)
                        nc.vector.tensor_reduce(k_top[:, i:i + 1], k_t[:, i, :], AX.X, ALU.max, negate=True).then_inc(k_top_ready, 1)
                if prev:
                    need(dve, y_rs_ready, b)
                    normed(qy, y_mv, y_rs, y_normed)
                if cur:
                    n = mm_use(b, "V")
                    for t in range(NT):
                        need(dve, mm_ready, n + t + 1)
                        nc.vector.tensor_tensor(values[:, t, :], banks[t % MM_RING][:, :], g.v_bias[:, :], ALU.add).then_inc(mm_empty, 1)
                if more:
                    need(dve, x_loaded, DMA * (b + 2))
                    moments(b + 1, z, x_raw, x_mv, x_var, x_stats, x_aggr, x_var_ready)
                if cur:
                    n = mm_use(b, "Q")
                    for t in range(NT):
                        need(dve, mm_ready, n + t + 1)
                        nc.vector.tensor_tensor(qy[:, t, :], banks[t % MM_RING][:, :], g.q_bias[:, :], ALU.add).then_inc(mm_empty, 1)
                        need(dve, mm_empty, n + t + 1)
                        nc.vector.tensor_reduce(q_top[:, t, :], qy[:, t, :].rearrange("p (h d) -> p h d", h=HEADS), AX.X, ALU.max,
                                                negate=True).then_inc(q_top_ready, 1)
                    need(dve, k_exp_ready, KD * b + KD)
                    nc.vector.reciprocal(k_inv[:, :], k_sum[:, :]).then_inc(k_inv_ready, 1)
                if more:
                    need(dve, x_rs_ready, b + 2)
                    normed(z, x_mv, x_rs, z_ready)
                if prev:
                    n = mm_use(b, "W")
                    for t in range(NT):
                        need(dve, mm_ready, n + t + 1)
                        need(dve, res_ready, NT * (b - 1) + t + 1)
                        nc.vector.tensor_tensor(res[:, t, :], banks[t % MM_RING][:, :], res[:, t, :], ALU.add).then_inc(mm_empty, 1)
                if cur:
                    for t in range(NT):
                        need(dve, q_exp_ready, NT * b + t + 1)
                        nc.vector.tensor_reduce(q_sum[:, t, :], qy[:, t, :].rearrange("p (h d) -> p h d", h=HEADS), AX.X, ALU.add).then_inc(q_summed, 1)
                    need(dve, q_summed, NT * b + NT)
                    nc.vector.reciprocal(q_inv[:, :, :], q_sum[:, :, :]).then_inc(q_inv_ready, 1)
                    need(dve, kv_ready, b + 1)
                    need(dve, k_inv_ready, b + 1)
                    for h in range(2):
                        at = slice(h * HEAD, (h + 1) * HEAD)
                        nc.vector.tensor_tensor(g.att[at, :, at], banks[6][at, :].rearrange("p (i d) -> p i d", i=KD)[:, :, at],
                                                k_inv[at, :].unsqueeze(2).to_broadcast([HEAD, KD, HEAD]), ALU.mult).then_inc(att_ready, 1)

            nc.vector.memset(k_sum[:, :], 0.0).then_inc(started, 1)
            dve.wait_ge(x_loaded, DMA)
            moments(0, z, x_raw, x_mv, x_var, x_stats, x_aggr, x_var_ready)
            dve.wait_ge(x_rs_ready, 1)
            normed(z, x_mv, x_rs, z_ready)
            iterations(dve, body)


def layer1(nc, a, g):
    banks, ident = g.banks, g.ident
    x1_rows = g.x1_dram.rearrange("(b t p) d -> b t p d", p=P, t=NT)
    y_rows = g.y_dram.rearrange("(k t p) d -> k p t d", p=P, t=CT)
    out_rows = a["out"].rearrange("b (t p) d -> b t p d", p=P)
    w_in_dram = a["L1_cond_W_in"].rearrange("(k p) n -> p k n", p=P)

    with ExitStack() as ctx:
        def sb(name, shape):
            return ctx.enter_context(nc.sbuf_tensor(name, shape, F32))

        def sem(name):
            return ctx.enter_context(nc.semaphore(name))

        w_xp = sb("w_xp", [P, KI, XD])
        w_dt = sb("w_dt", [RANK, INNER])
        w_y = sb("w_y", [P, KI, DIM])
        w_in = sb("w_in", [P, 2, KD, P])
        rows = sb("rows1", [P, CT, DIM])
        h_t = sb("h1_t", [P, KD, CHUNK])
        pad = sb("pad", [P, 2, TAPS - 1 + CHUNK])
        xd = pad[0:XD, 0, TAPS - 1:]
        xm = sb("xm", [P, KI, CHUNK])
        zs = sb("zs", [P, KI, CHUNK])
        dt = sb("dt", [P, 2, KI, CHUNK])
        u = sb("u", [P, KI, CHUNK])
        acc = sb("acc", [P, CT, INNER])
        da = sb("da", [P, RING, 2, CHUNK])
        db = sb("db", [P, RING, 2, CHUNK])
        hs = sb("hs", [P, RING, 2, CHUNK])
        b_wide = sb("b_wide", [P, 2, CHUNK])
        c_t = sb("c_t", [P, 2, CT, STATE])
        gate = sb("gate_wide", [P, DIM])
        fin = sb("fin", [P, 2, DIM])
        mod_cur = sb("mod1_cur", [P, 2 * KD])
        raw = sb("raw1", [P, CT, 6])
        mv = sb("mv1", [P, CT, 2])
        var = sb("var1", [P, CT])
        rs = sb("rs1", [P, CT])
        halo = sb("halo", [P, KI, TAPS - 1])
        carry = sb("carry", [P, KI, STATE])

        weights_loaded, cleared = sem("weights1_loaded"), sem("cleared")
        w_in_loaded = [sem(f"w_in_loaded{i}") for i in range(2)]
        rows_loaded, gate_loaded, b_stored, y_stored = (sem(n) for n in ("rows1_loaded", "gate_loaded", "b_stored", "y_stored"))
        b_loaded = [sem(f"b_loaded{i}") for i in range(2)]
        fin_loaded, fin_added, fin_stored = ([sem(f"fin_{n}{i}") for i in range(2)] for n in ("loaded", "added", "stored"))
        idx_in_ready, mod_ready = (sem(n) for n in ("idx_in_ready", "mod1_ready"))
        stats, aggr, var_ready, rs_ready, normed = (sem(n) for n in ("stats1", "aggr1", "var1_ready", "rs1_ready", "normed1"))
        a_ready, a_empty, v_ready, v_empty = (sem(n) for n in ("a_ready", "a_empty", "v_ready", "v_empty"))
        tap_done, halo_set, halo_kept = (sem(n) for n in ("tap_done", "halo_set", "halo_kept"))
        xm_ready, zs_ready, dt_exp, dt_log, dt_ready, u_ready, xm_scaled = (
            sem(n) for n in ("xm_ready", "zs_ready", "dt_exp", "dt_log", "dt_ready", "u_ready", "xm_scaled"))
        da_ready, db_ready, scanned, turned, summed, carried = (sem(n) for n in ("da_ready", "db_ready", "scanned", "turned1", "summed", "carried"))
        passed = sem("passed1")
        block = ctx.enter_context(nc.Block())

        def apart(eng, semaphore, value):
            need(eng, semaphore, value)
            if not isinstance(value, int):
                eng.sem_inc(passed, 1)

        def either(eng, first_chunk, both_chunks):
            largest = eng.value_load(g.idx_max[0:1, 0:1], min_val=0, max_val=SEQ - 1)
            with eng.If(largest < CHUNK):
                first_chunk()
            with eng.Else():
                both_chunks()

        def batches(eng, body):
            body(0)
            with eng.Fori(1, BATCH) as b:
                body(b)

        def turns(eng, turn, end):
            turn(0, 0, False, True)
            with eng.Fori(0, BATCH // 2 - 1) as pair:
                turn(2 * pair + 1, 1, True, True)
                turn(2 * pair + 2, 0, True, True)
            turn(BATCH - 1, 1, True, False)
            end()

        @block.sync
        def _(sp):
            sp.dma_start(w_xp[:, :, :], a["L1_cond_W_xp"].rearrange("(k p) n -> p k n", p=P)).then_inc(weights_loaded, DMA)
            sp.dma_start(w_dt[:, :], a["L1_cond_W_dt"]).then_inc(weights_loaded, DMA)
            sp.dma_start(w_y[:, :, :], a["L1_cond_W_out"].rearrange("(k p) n -> p k n", p=P)).then_inc(weights_loaded, DMA)

            def load_w_in(it, m):
                if m < 2:
                    need(sp, a_ready, A_USES * (it - 1) + A_USE["z"] + 6 + m + 1)
                elif m < KI + 2:
                    need(sp, a_ready, A_USES * it + A_USE["xm"] + m - 2 + 1)
                else:
                    need(sp, a_ready, A_USES * it + A_USE["z"] + m - KI - 2 + 1)
                sp.dma_start(w_in[:, m % 2, :, :], w_in_dram[:, :, m * P:(m + 1) * P]).then_inc(w_in_loaded[m % 2], DMA)

            def store_b(it):
                apart(sp, a_empty, A_USES * it + A_USE["xd"] + 1)
                sp.dma_start(g.b_dram[bass.ds(it, 1)].rearrange("o s t -> (o s) t"), xd[RANK:RANK + STATE, :]).then_inc(b_stored, DMA)

            def load_b(it, s):
                apart(sp, b_stored, DMA * (it + 1))
                apart(sp, db_ready, PIECES * it + 4 * (s - 1))
                sp.dma_start(b_wide[:, s % 2, :], g.b_dram[bass.ds(it, 1), s, :].rearrange("o t -> (o t)").partition_broadcast(P)).then_inc(b_loaded[s % 2], DMA)

            def load_gate(it, b):
                apart(sp, v_empty, V_USES * it)
                sp.dma_start(gate[:, :], g.gate_dram[bass.ds(b, 1)].rearrange("o d -> (o d)").partition_broadcast(P)).then_inc(gate_loaded, DMA)

            def store_y(it, c):
                apart(sp, v_empty, V_USES * it + V_USES)
                sp.dma_start(y_rows[c], rows[:, :, :]).then_inc(y_stored, DMA)

            def load_fin(b, k):
                if k >= 2:
                    apart(sp, fin_stored[k % 2], DMA * (NT // 2 * b + k // 2))
                sp.dma_start(fin[:, k % 2, :], x1_rows[bass.ds(b, 1), k].rearrange("o p d -> (o p) d")).then_inc(fin_loaded[k % 2], DMA)

            def store_fin(b, k):
                apart(sp, fin_added[k % 2], DMA * (NT // 2 * b + k // 2 + 1))
                sp.dma_start(out_rows[bass.ds(b, 1), k].rearrange("o p d -> (o p) d"), fin[:, k % 2, :]).then_inc(fin_stored[k % 2], DMA)

            def all_stored(b):
                for i in range(2):
                    apart(sp, fin_stored[i], DMA * NT // 2 * (b + 1))

            def finish(b):
                load_fin(b, 0)
                for k in range(NT):
                    if k + 1 < NT:
                        load_fin(b, k + 1)
                    store_fin(b, k)
                all_stored(b)

            def turn(b, par, prev, more):
                for s in range(STATE):
                    if s == 0:
                        load_w_in(b, KI)
                        load_w_in(b, KI + 1)
                    if s == 4:
                        load_gate(b, b)
                    if prev and s == 4:
                        store_y(b - 1, 0)
                    for m in {4: (2, 3, 4), 5: (5, 6, 7)}.get(s, ()):
                        load_w_in(b, KI + m)
                    if more:
                        for m in {6: (0, 1), 7: (2, 3), 8: (4, 5), 9: (6, 7)}.get(s, ()):
                            load_w_in(b + 1, m)
                        if s == 13:
                            store_b(b + 1)
                    if prev and s >= 8:
                        k = s - 8
                        if k == 0:
                            load_fin(b - 1, 0)
                        if k:
                            store_fin(b - 1, k - 1)
                        if k + 1 < NT:
                            load_fin(b - 1, k + 1)
                    if s + 2 < STATE:
                        load_b(b, s + 2)
                    elif more:
                        load_b(b + 1, s + 2 - STATE)
                if prev:
                    store_fin(b - 1, NT - 1)
                    all_stored(b - 1)

            def first_chunk():
                for m in range(KI):
                    load_w_in(0, m)
                store_b(0)
                load_b(0, 0)
                load_b(0, 1)

                def end():
                    store_y(BATCH - 1, 0)
                    finish(BATCH - 1)

                turns(sp, turn, end)

            def both_chunks():
                def body(b):
                    for c in range(CHUNKS):
                        it = CHUNKS * b + c
                        for m in range(KI):
                            load_w_in(it, m)
                        store_b(it)
                        for s in range(STATE):
                            load_b(it, s)
                        load_gate(it, b)
                        for m in range(KI, 2 * KI):
                            load_w_in(it, m)
                        store_y(it, c)
                    finish(b)

                batches(sp, body)

            either(sp, first_chunk, both_chunks)
            for s in fin_stored:
                sp.wait_ge(s, DMA * NT // 2 * BATCH)

        @block.tensor
        def _(pe):
            pe.wait_ge(weights_loaded, 3 * DMA)

            def a_bank(it, at):
                need(pe, a_empty, A_USES * it + at - 1)
                return banks[4 + at % 2]

            def v_bank(it, at):
                need(pe, v_empty, V_USES * it + at - 1)
                return banks[6 + at % 2]

            def norm_turned(it):
                need(pe, normed, CT * it + CT)
                for i in range(KD):
                    out = a_bank(it, A_USE["h"] + i)
                    for t in range(CT):
                        last = nc.tensor.transpose(out[:, t * P:(t + 1) * P], rows[:, t, i * P:(i + 1) * P], ident[:, :])
                    last.then_inc(a_ready, 1)
                need(pe, a_empty, A_USES * it + A_USE["h"] + KD)

            def project_in(it, m):
                out = a_bank(it, A_USE["xm"] + m if m < KI else A_USE["z"] + m - KI)
                need(pe, w_in_loaded[m % 2], DMA * (KI * it + m // 2 + 1))
                for k in range(KD):
                    last = nc.tensor.matmul(out[:, :], w_in[:, m % 2, k, :], h_t[:, k, :], start=(k == 0), stop=(k == KD - 1))
                last.then_inc(a_ready, 1)

            def project_xd(it):
                out = a_bank(it, A_USE["xd"])
                for j in range(KI):
                    need(pe, xm_ready, 2 * it + j // 4 + 1)
                    last = nc.tensor.matmul(out[0:XD, :], w_xp[:, j, :], xm[:, j, :], start=(j == 0), stop=(j == KI - 1))
                last.then_inc(a_ready, 1)

            def project_dt(it, j):
                need(pe, a_empty, A_USES * it + A_USE["xd"] + 1)
                out = a_bank(it, A_USE["dt"] + j)
                nc.tensor.matmul(out[:, :], w_dt[:, j * P:(j + 1) * P], xd[0:RANK, :], start=True, stop=True).then_inc(a_ready, 1)

            def c_turned(it):
                out = a_bank(it, A_USE["C"])
                for t in range(CT):
                    last = nc.tensor.transpose(out[:, t * XD:(t + 1) * XD], xd[:, t * P:(t + 1) * P], ident[0:XD, 0:XD])
                last.then_inc(a_ready, 1)

            def x_turned(it):
                for j in range(KI):
                    need(pe, xm_scaled, KI * it + j + 1)
                    out = a_bank(it, A_USE["init"] + j)
                    for t in range(CT):
                        last = nc.tensor.transpose(out[:, t * P:(t + 1) * P], xm[:, j, t * P:(t + 1) * P], ident[:, :])
                    last.then_inc(a_ready, 1)

            def states_turned(it, q):
                need(pe, scanned, PIECES * it + 2 * q + 2)
                for t in range(CT):
                    need(pe, summed, CT * HALVES * it + CT * (q - 1) + t + 1)
                    for j in range(4):
                        last = nc.tensor.transpose(banks[t][:, j * P:(j + 1) * P], hs[:, (2 * q + j // 2) % RING, j % 2, t * P:(t + 1) * P], ident[:, :])
                    last.then_inc(turned, 1)

            def y_turned(it):
                need(pe, summed, CT * HALVES * it + CT * HALVES)
                for j in range(KI):
                    out = v_bank(it, V_USE["y"] + j)
                    for t in range(CT):
                        last = nc.tensor.transpose(out[:, t * P:(t + 1) * P], acc[:, t, j * P:(j + 1) * P], ident[:, :])
                    last.then_inc(v_ready, 1)

            def project_out(it, t):
                need(pe, v_empty, V_USES * it + KI)
                out = v_bank(it, V_USE["out"] + t)
                for j in range(KI):
                    last = nc.tensor.matmul(out[:, :], zs[:, j, t * P:(t + 1) * P], w_y[:, j, :], start=(j == 0), stop=(j == KI - 1))
                last.then_inc(v_ready, 1)

            def turn(b, par, prev, more):
                for s in range(STATE):
                    states_turned(b, 2 * s)
                    if prev and s < CT:
                        project_out(b - 1, s)
                    for m in {4: (0, 1, 2), 5: (3, 4, 5), 6: (6, 7)}.get(s, ()):
                        project_in(b, KI + m)
                    if more:
                        if s == 7:
                            norm_turned(b + 1)
                        if 7 <= s < 11:
                            project_in(b + 1, 2 * (s - 7))
                            project_in(b + 1, 2 * (s - 7) + 1)
                        if s == 12:
                            project_xd(b + 1)
                        if s in (13, 14):
                            for j in range(4):
                                project_dt(b + 1, 4 * (s - 13) + j)
                        if s == 14:
                            c_turned(b + 1)
                    states_turned(b, 2 * s + 1)
                y_turned(b)
                if more:
                    x_turned(b + 1)

            def front(it):
                norm_turned(it)
                for m in range(KI):
                    project_in(it, m)
                project_xd(it)
                for j in range(KI):
                    project_dt(it, j)
                c_turned(it)
                x_turned(it)

            def first_chunk():
                def end():
                    for t in range(CT):
                        project_out(BATCH - 1, t)

                front(0)
                turns(pe, turn, end)

            def both_chunks():
                def body(b):
                    for c in range(CHUNKS):
                        it = CHUNKS * b + c
                        front(it)
                        for q in range(HALVES):
                            states_turned(it, q)
                        for m in range(KI):
                            project_in(it, KI + m)
                        y_turned(it)
                        for t in range(CT):
                            project_out(it, t)

                batches(pe, body)

            pe.wait_ge(cleared, 4)
            either(pe, first_chunk, both_chunks)

        @block.scalar
        def _(act):
            def bank(it, at):
                need(act, a_ready, A_USES * it + at + 1)
                return banks[4 + at % 2]

            def norm_modulated(it):
                need(act, mod_ready, it + 1)
                for i in range(KD):
                    src = bank(it, A_USE["h"] + i)
                    nc.scalar.activation(h_t[:, i, :], src[:, :], ACT.Identity, scale=mod_cur[:, i:i + 1], bias=mod_cur[:, KD + i:KD + i + 1]).then_inc(a_empty, 1)

            def keep_x(it, m):
                if m < 2:
                    need(act, a_ready, A_USES * (it - 1) + A_USE["C"] + 1)
                    need(act, b_stored, DMA * it)
                need(act, tap_done, KI * TAPS * it + TAPS * 2 * (m // 2))
                src = bank(it, A_USE["xm"] + m)
                nc.scalar.copy(pad[:, m % 2, TAPS - 1:], src[:, :]).then_inc(a_empty, 1)

            def silu_x(it, half):
                need(act, tap_done, KI * TAPS * it + KI * TAPS // 2 * (half + 1))
                part = xm[:, 4 * half:4 * half + 4, :]
                nc.scalar.activation(part, part, ACT.Silu).then_inc(xm_ready, 1)

            def keep_z(it, m):
                need(act, v_ready, V_USES * it)
                src = bank(it, A_USE["z"] + m)
                nc.scalar.copy(zs[:, m, :], src[:, :]).then_inc(a_empty, 1)

            def silu_z(it, half):
                need(act, a_empty, A_USES * it + A_USE["z"] + 4 * half + 4)
                part = zs[:, 4 * half:4 * half + 4, :]
                nc.scalar.activation(part, part, ACT.Silu).then_inc(zs_ready, 1)

            def keep_xd(it):
                need(act, tap_done, KI * TAPS * it + KI * TAPS)
                src = bank(it, A_USE["xd"])
                nc.scalar.copy(xd, src[0:XD, :]).then_inc(a_empty, 1)

            def log_dt(it, par, half):
                if half:
                    need(act, dt_ready, 2 * it + 1)
                for j in range(4 * half, 4 * half + 4):
                    src = bank(it, A_USE["dt"] + j)
                    nc.scalar.activation(rows[:, j % 4, :], src[:, :], ACT.Relu, bias=column(g, "L1_cond_b_dt", j))
                    nc.scalar.activation(dt[:, par, j, :], src[:, :], ACT.Abs, bias=column(g, "L1_cond_b_dt", j)).then_inc(a_empty, 1)
                part = dt[:, par, 4 * half:4 * half + 4, :]
                need(act, a_empty, A_USES * it + A_USE["dt"] + 4 * half + 4)
                nc.scalar.activation(part, part, ACT.Exp, scale=-1.0).then_inc(dt_exp, 1)
                need(act, dt_exp, 2 * it + half + 1)
                nc.scalar.activation(part, part, ACT.Ln, bias=1.0).then_inc(dt_log, 1)

            def keep_c(it, par):
                src = bank(it, A_USE["C"])
                nc.scalar.copy(c_t[:, par, :, :], src[:, 0:CT * XD].rearrange("p (t x) -> p t x", x=XD)[:, :, RANK + STATE:]).then_inc(a_empty, 1)

            def start_sum(it):
                need(act, v_ready, V_USES * (it - 1) + KI)
                for j in range(KI):
                    src = bank(it, A_USE["init"] + j)
                    nc.scalar.copy(acc[:, :, j * P:(j + 1) * P], src[:, :].rearrange("p (t d) -> p t d", t=CT)).then_inc(a_empty, 1)

            def decays(it, par, k, first):
                s, jc = k // 4, k % 4
                if k < 4:
                    need(act, dt_ready, 2 * it + jc // 2 + 1)
                need(act, scanned, PIECES * it + k - (RING - 1))
                for e in range(2):
                    j = 2 * jc + e
                    last = nc.scalar.activation(da[:, k % RING, e, first:], dt[:, par, j, first:], ACT.Exp, scale=g.decay[:, j, s:s + 1])
                last.then_inc(da_ready, 1)

            def turn(b, par, prev, more):
                for s in range(STATE):
                    for k in range(4 * s, 4 * s + 4):
                        decays(b, par, k, 1)
                    for m in {4: (0, 1, 2), 5: (3, 4, 5), 6: (6, 7)}.get(s, ()):
                        keep_z(b, m)
                    if s == 12:
                        silu_z(b, 0)
                        silu_z(b, 1)
                    if more:
                        if s == 7:
                            norm_modulated(b + 1)
                        if 7 <= s < 11:
                            keep_x(b + 1, 2 * (s - 7))
                            keep_x(b + 1, 2 * (s - 7) + 1)
                        if s == 12:
                            silu_x(b + 1, 0)
                            silu_x(b + 1, 1)
                            keep_xd(b + 1)
                        if s in (13, 14):
                            log_dt(b + 1, 1 - par, s - 13)
                        if s == 14:
                            keep_c(b + 1, 1 - par)
                if more:
                    start_sum(b + 1)

            def front(it, par):
                norm_modulated(it)
                for m in range(KI):
                    keep_x(it, m)
                silu_x(it, 0)
                silu_x(it, 1)
                keep_xd(it)
                log_dt(it, par, 0)
                log_dt(it, par, 1)
                keep_c(it, par)
                start_sum(it)

            def first_chunk():
                front(0, 0)
                turns(act, turn, lambda: None)

            def both_chunks():
                def body(b):
                    for c in range(CHUNKS):
                        it = CHUNKS * b + c
                        front(it, c)
                        for k in range(PIECES):
                            decays(it, c, k, 0)
                        for m in range(KI):
                            keep_z(it, m)
                        silu_z(it, 0)
                        silu_z(it, 1)

                batches(act, body)

            act.wait_ge(cleared, 4)
            either(act, first_chunk, both_chunks)

        @block.gpsimd
        def _(pool):
            def gather_rows(it, b, c, stores):
                need(pool, y_stored, DMA * stores)
                need(pool, dt_ready, 2 * it)
                apart(pool, idx_in_ready, b)
                for t in range(CT):
                    nc.gpsimd.indirect_dma_start(rows[:, t, :], None, g.x1_dram, bass.IndirectOffsetOnAxis(g.idx_in[:, c * CT + t:c * CT + t + 1], axis=0)).then_inc(rows_loaded, DMA)

            def rsqrt(it):
                need(pool, var_ready, it + 1)
                nc.gpsimd.tensor_tensor(rs[:, :], var[:, :], g.mhalf[:, 0:CT], ALU.pow).then_inc(rs_ready, 1)

            def add_dt(it, par, half):
                need(pool, dt_log, 2 * it + half + 1)
                part = dt[:, par, 4 * half:4 * half + 4, :]
                nc.gpsimd.tensor_tensor(part, part, rows[:, :, :], ALU.add).then_inc(dt_ready, 1)

            def dt_x(it, par, jc):
                need(pool, dt_ready, 2 * it + jc // 2 + 1)
                need(pool, xm_ready, 2 * it + jc // 2 + 1)
                need(pool, db_ready, PIECES * it - 4 + jc + 1)
                nc.gpsimd.tensor_tensor(u[:, 2 * jc:2 * jc + 2, :], dt[:, par, 2 * jc:2 * jc + 2, :], xm[:, 2 * jc:2 * jc + 2, :], ALU.mult).then_inc(u_ready, 1)

            def inputs(it, k):
                s, jc = k // 4, k % 4
                if k < 4:
                    need(pool, u_ready, 4 * it + jc + 1)
                if jc == 0:
                    need(pool, b_loaded[s % 2], DMA * (STATE // 2 * it + s // 2 + 1))
                need(pool, scanned, PIECES * it + k - (RING - 1))
                nc.gpsimd.tensor_tensor(db[:, k % RING, :, :], u[:, 2 * jc:2 * jc + 2, :], b_wide[:, s % 2, :].unsqueeze(1).to_broadcast([P, 2, CHUNK]),
                                        ALU.mult).then_inc(db_ready, 1)

            def add_y(b, k, reach):
                apart(pool, fin_loaded[k % 2], DMA * (NT // 2 * b + k // 2 + 1))
                nc.gpsimd.indirect_dma_start(fin[:, k % 2, :], None, g.y_dram[0:reach, :], bass.IndirectOffsetOnAxis(g.idx_first[:, k:k + 1], axis=0),
                                             compute_op=ALU.add).then_inc(fin_added[k % 2], DMA)

            def turn(b, par, prev, more):
                for s in range(STATE):
                    for k in range(4 * s, 4 * s + 4):
                        inputs(b, k)
                    if more:
                        if s == 4:
                            gather_rows(b + 1, b + 1, 0, b)
                        if s == 6:
                            rsqrt(b + 1)
                        if s in (13, 14):
                            add_dt(b + 1, 1 - par, s - 13)
                    if prev and s >= 8:
                        if s == 8:
                            apart(pool, y_stored, DMA * b)
                        add_y(b - 1, s - 8, CHUNK)
                if more:
                    for jc in range(4):
                        dt_x(b + 1, 1 - par, jc)

            def front(it, b, c, stores, par):
                gather_rows(it, b, c, stores)
                rsqrt(it)
                add_dt(it, par, 0)
                add_dt(it, par, 1)
                for jc in range(4):
                    dt_x(it, par, jc)

            def finish(b, stores, reach):
                apart(pool, y_stored, DMA * stores)
                for k in range(NT):
                    add_y(b, k, reach)

            def first_chunk():
                front(0, 0, 0, 0, 0)
                turns(pool, turn, lambda: finish(BATCH - 1, BATCH, CHUNK))

            def both_chunks():
                def body(b):
                    for c in range(CHUNKS):
                        it = CHUNKS * b + c
                        pool.wait_ge(cleared, 4)
                        front(it, b, c, it, c)
                        for k in range(PIECES):
                            inputs(it, k)
                    finish(b, CHUNKS * b + CHUNKS, SEQ)

                batches(pool, body)

            pool.wait_ge(cleared, 4)
            either(pool, first_chunk, both_chunks)

        @block.vector
        def _(dve):
            def norm(it, b):
                apart(dve, a_empty, A_USES * (it - 1) + A_USE["h"] + KD)
                nc.vector.tensor_copy(mod_cur[:, :], g.mod_l1[:, bass.ds(b, 1), :].rearrange("p o i -> p (o i)")).then_inc(mod_ready, 1)
                need(dve, rows_loaded, CT * DMA * (it + 1))
                for t in range(CT):
                    nc.vector.bn_stats(raw[:, t, :], rows[:, t, :]).then_inc(stats, 1)
                apart(dve, stats, CT * it + CT)
                for t in range(CT):
                    nc.vector.bn_aggr(mv[:, t, :], raw[:, t, :]).then_inc(aggr, 1)
                need(dve, aggr, CT * it + CT)
                nc.vector.tensor_scalar(var[:, :], mv[:, :, 1], EPS, None, ALU.add).then_inc(var_ready, 1)
                need(dve, rs_ready, it + 1)
                for t in range(CT):
                    nc.vector.tensor_scalar(rows[:, t, :], rows[:, t, :], mv[:, t, 0:1], rs[:, t:t + 1], ALU.subtract, ALU.mult).then_inc(normed, 1)

            def convolve(it, pair):
                n = KI * TAPS * it + 2 * TAPS * pair
                for tap in range(TAPS):
                    for e in range(2):
                        m = 2 * pair + e
                        need(dve, a_empty, A_USES * it + A_USE["xm"] + m + 1)
                        src, w = pad[:, e, tap:tap + CHUNK], g.taps[:, m, tap:tap + 1]
                        if tap == 0:
                            nc.vector.tensor_scalar(xm[:, m, :], src, w, column(g, "L1_cond_conv_b", m), ALU.mult, ALU.add).then_inc(tap_done, 1)
                        else:
                            need(dve, tap_done, n + 2 * (tap - 1) + e + 1)
                            nc.vector.scalar_tensor_tensor(xm[:, m, :], src, w, xm[:, m, :], ALU.mult, ALU.add).then_inc(tap_done, 1)

            def scan(it, k):
                need(dve, da_ready, PIECES * it + k + 1)
                need(dve, db_ready, PIECES * it + k + 1)
                need(dve, turned, CT * HALVES * it + CT * ((k - RING) // 2 + 1))
                flat = [r[:, k % RING, :, :].rearrange("p e t -> p (e t)") for r in (hs, da, db)]
                nc.vector.tensor_tensor_scan(flat[0], flat[1], flat[2], 0.0, ALU.mult, ALU.add).then_inc(scanned, 1)

            def scan_on(it, b, k):
                s, jc = k // 4, k % 4
                need(dve, da_ready, PIECES * it + k + 1)
                need(dve, db_ready, PIECES * it + k + 1)
                need(dve, turned, CT * HALVES * it + CT * ((k - RING) // 2 + 1))
                if k == 0:
                    need(dve, carried, PIECES * it + b + 1)
                for e in range(2):
                    last = nc.vector.tensor_tensor_scan(hs[:, k % RING, e, :], da[:, k % RING, e, :], db[:, k % RING, e, :],
                                                        carry[:, 2 * jc + e, s:s + 1], ALU.mult, ALU.add)
                last.then_inc(scanned, 1)
                need(dve, scanned, PIECES * it + k + 1)
                nc.vector.tensor_copy(carry[:, 2 * jc:2 * jc + 2, s:s + 1], hs[:, k % RING, :, CHUNK - 1:CHUNK]).then_inc(carried, 1)

            def add_states(it, par, q):
                s, jg = q // 2, q % 2
                for t in range(CT):
                    if q < 2:
                        need(dve, a_empty, A_USES * it + A_USE["init"] + 4 * jg + 4)
                    else:
                        need(dve, summed, CT * HALVES * it + CT * (q - 2) + t + 1)
                    need(dve, turned, CT * HALVES * it + CT * q + t + 1)
                    part = acc[:, t, jg * 512:(jg + 1) * 512]
                    nc.vector.scalar_tensor_tensor(part, banks[t][:, :], c_t[:, par, t, s:s + 1], part, ALU.mult, ALU.add).then_inc(summed, 1)

            def gate_y(it):
                need(dve, zs_ready, 2 * it + 2)
                for j in range(KI):
                    need(dve, v_ready, V_USES * it + j + 1)
                    nc.vector.tensor_tensor(zs[:, j, :], banks[6 + j % 2][:, :], zs[:, j, :], ALU.mult).then_inc(v_empty, 1)

            def gate_out(it, t, dts):
                if t == 0:
                    need(dve, gate_loaded, DMA * (it + 1))
                    need(dve, dt_ready, dts)
                need(dve, v_ready, V_USES * it + KI + t + 1)
                nc.vector.tensor_tensor(rows[:, t, :], banks[6 + t % 2][:, :], gate[:, :], ALU.mult).then_inc(v_empty, 1)

            def scale_x(it):
                for j in range(KI):
                    need(dve, u_ready, 4 * it + j // 2 + 1)
                    nc.vector.tensor_scalar(xm[:, j, :], xm[:, j, :], column(g, "L1_cond_D_param", j), None, ALU.mult).then_inc(xm_scaled, 1)

            def next_rows():
                nc.vector.tensor_scalar(g.idx_in[:, :], g.idx_in[:, :], SEQ, None, ALU.add).then_inc(idx_in_ready, 1)

            def turn(b, par, prev, more):
                for q in range(HALVES):
                    scan(b, 2 * q)
                    scan(b, 2 * q + 1)
                    if q:
                        add_states(b, par, q - 1)
                    s = q // 2
                    if q % 2 == 0:
                        continue
                    if prev and s < CT:
                        gate_out(b - 1, s, 2 * (b + 1))
                    if more:
                        if s == 6:
                            norm(b + 1, b + 1)
                        if 8 <= s < 12:
                            convolve(b + 1, s - 8)
                        if s == 12:
                            next_rows()
                add_states(b, par, HALVES - 1)
                gate_y(b)
                if more:
                    scale_x(b + 1)

            def first_chunk():
                norm(0, 0)
                for pair in range(KI // 2):
                    convolve(0, pair)
                scale_x(0)
                next_rows()

                def end():
                    for t in range(CT):
                        gate_out(BATCH - 1, t, 2 * BATCH)

                turns(dve, turn, end)

            def both_chunks():
                def body(b):
                    for c in range(CHUNKS):
                        it = CHUNKS * b + c
                        norm(it, b)
                        if c == 0:
                            need(dve, halo_kept, (KI // 2 + 1) * b)
                            need(dve, carried, PIECES * it + b)
                            nc.vector.memset(halo[:, :, :], 0.0).then_inc(halo_kept, 1)
                            nc.vector.memset(carry[:, :, :], 0.0).then_inc(carried, 1)
                        for pair in range(KI // 2):
                            need(dve, halo_kept, 5 * b + (KI // 2 * c) + 1)
                            nc.vector.tensor_copy(pad[:, :, 0:TAPS - 1], halo[:, 2 * pair:2 * pair + 2, :]).then_inc(halo_set, 1)
                            need(dve, halo_set, KI // 2 * it + pair + 1)
                            if c == 0:
                                need(dve, a_empty, A_USES * it + A_USE["xm"] + 2 * pair + 2)
                                nc.vector.tensor_copy(halo[:, 2 * pair:2 * pair + 2, :], pad[:, :, CHUNK:]).then_inc(halo_kept, 1)
                            convolve(it, pair)
                        scale_x(it)
                        for q in range(HALVES):
                            scan_on(it, b, 2 * q)
                            scan_on(it, b, 2 * q + 1)
                            add_states(it, c, q)
                        gate_y(it)
                        for t in range(CT):
                            gate_out(it, t, 2 * (it + 1))
                    next_rows()

                batches(dve, body)

            nc.vector.memset(da[:, :, :, 0:1], 0.0).then_inc(cleared, 1)
            nc.vector.memset(pad[:, :, 0:TAPS - 1], 0.0).then_inc(cleared, 1)
            nc.vector.memset(halo[:, :, :], 0.0).then_inc(cleared, 1)
            nc.vector.memset(carry[:, :, :], 0.0).then_inc(cleared, 1)
            dve.wait_ge(cleared, 4)
            either(dve, first_chunk, both_chunks)


INPUTS = ["x", "cond_2048", "itok_S_0_1023", "mask_BxSx1_fk1"] + [
    f"L0_cond_{n}" for n in ("ln_w", "ln_b", "Wq", "bq", "Wk", "bk", "Wv", "bv", "W_emb", "b_emb", "ln2_w", "ln2_b", "W_out", "b_out")] + [
    f"L1_cond_{n}" for n in ("W_ada", "b_ada", "gamma", "beta", "W_in", "conv_w", "conv_b", "W_xp", "W_dt", "b_dt", "A_log", "D_param", "W_out")]


def kernel(**inputs):
    import numpy as np
    import concourse.bacc as bacc
    from concourse.bass_utils import run_bass_kernel_spmd

    nc = bacc.Bacc("TRN2", target_bir_lowering=False, num_devices=1)
    arrays, aps = {}, {}
    for name in INPUTS:
        arrays[f"in_{name}"] = np.ascontiguousarray(inputs[name])
        aps[name] = nc.dram_tensor(f"in_{name}", arrays[f"in_{name}"].shape, mybir.dt.from_np(arrays[f"in_{name}"].dtype), kind="ExternalInput").ap()
    aps["out"] = nc.dram_tensor("out", (BATCH, SEQ, DIM), F32, kind="ExternalOutput").ap()
    cond_mamba_kernel(nc, aps)
    result = run_bass_kernel_spmd(nc, [arrays], core_ids=[0])
    return result.results[0]["out"]
```

```python
from contextlib import ExitStack

import concourse.bass as bass
from concourse import mybir

F32 = mybir.dt.float32
I32 = mybir.dt.int32
ALU = mybir.AluOpType
ACT = mybir.ActivationFunctionType
AX = mybir.AxisListType

P = 128
BATCH, SEQ, DIM = 8, 1024, 512
HEADS = 8
HEAD = DIM // HEADS
EMB = 1024
INNER, STATE, RANK, TAPS = 1024, 16, 64, 4
EPS = 1e-5
MASKED = 1e6
KD = DIM // P
KI = INNER // P
KE = EMB // P
NT = SEQ // P
CHUNK = 512
CT = CHUNK // P
CHUNKS = SEQ // CHUNK
XD = RANK + 2 * STATE
DMA = 16

VECTORS = [("L0_cond_ln_w", KD), ("L0_cond_ln_b", KD), ("L0_cond_bk", KD), ("L0_cond_ln2_w", KD), ("L0_cond_ln2_b", KD),
           ("L0_cond_b_emb", 2 * KD), ("L1_cond_b_ada", 2 * KD), ("L1_cond_gamma", KD), ("L1_cond_beta", KD),
           ("L1_cond_conv_b", KI), ("L1_cond_b_dt", KI), ("L1_cond_D_param", KI)]
COLUMN = {name: sum(n for _, n in VECTORS[:i]) for i, (name, _) in enumerate(VECTORS)}
VROWS = sum(n for _, n in VECTORS)

MM_FIRST = {"K": 0, "V": 8, "Q": 16}
MM_USES = 5 * NT
MM = {"y": 0, "K": 8, "V": 16, "Q": 24, "W": 32}
MM_LAST = {"y": 0, "W": 8}
TR_FIRST = {"z": 0, "q": 8, "k": 16}
TR_USES = 4 * NT
TR = {"z": 0, "y": 8, "q": 16, "k": 24}
TR_LAST = {"y": 0}
MM_RING, TR_RING = 4, 2

RING = 4
BLOCKS = STATE * KI
PIECES = BLOCKS // 2
HALVES = BLOCKS // 4
W_IN_RING = 4


def work_order(*stages):
    uses, seen = {}, {}
    for stage, n in stages:
        for _ in range(n):
            i = seen.get(stage, 0)
            uses[stage, i], seen[stage] = len(uses), i + 1
    return uses


FRONT = work_order(("h", KD), ("xm", KI), ("xd", 1), ("C", 1), ("dt", KI))
PREPARE = (("h", KD), ("xm", KI), ("z", 2), ("xd", 1), ("z", 1), ("C", 1), ("dt", 4), ("z", 2), ("dt", 4), ("z", 3))
FIRST_TURN = work_order(("init", KI), *PREPARE)
TURN = work_order(*[("y", 1), ("init", 1)] * KI, *PREPARE)
LAST_TURN = work_order(*[("y", 1), ("init", 1)] * KI, ("z", KI))
END = work_order(("y", KI))
CHUNK_ORDER = work_order(("h", KD), ("xm", KI), ("xd", 1), ("C", 1), ("dt", KI), ("init", KI), ("z", KI), ("y", KI))


def turn_place(b):
    first = len(FRONT) // 2
    if isinstance(b, int) and b == 0:
        return first, FIRST_TURN
    start = first + len(FIRST_TURN) // 2 + len(TURN) // 2 * (b - 1)
    return start, LAST_TURN if isinstance(b, int) and b == BATCH - 1 else TURN


class Shared:
    pass


def need(eng, semaphore, value):
    if not (isinstance(value, int) and value <= 0):
        eng.wait_ge(semaphore, value)


def mm_use(b, stage):
    if isinstance(b, int) and b == 0:
        return MM_FIRST[stage]
    base = MM_USES * b - 2 * NT
    return base + (MM_LAST if isinstance(b, int) and b == BATCH else MM)[stage]


def tr_use(b, stage):
    if isinstance(b, int) and b == 0:
        return TR_FIRST[stage]
    base = TR_USES * b - NT
    return base + (TR_LAST if isinstance(b, int) and b == BATCH else TR)[stage]


def cond_mamba_kernel(nc, a):
    g = Shared()

    def scratch(name, shape):
        return nc.dram_tensor(name, shape, F32).ap()

    g.x1_dram = scratch("x1_rows", [BATCH * SEQ, DIM])
    g.y_dram = scratch("y_rows", [SEQ, DIM])
    g.gate_dram = scratch("gate_rows", [BATCH, DIM])
    g.b_dram = scratch("b_rows", [BATCH * CHUNKS, STATE, CHUNK])

    with ExitStack() as whole:
        def sb(name, shape, dt=F32):
            return whole.enter_context(nc.sbuf_tensor(name, shape, dt))

        g.banks = [whole.enter_context(nc.psum_tensor(f"bank{i}", [P, 512], F32)) for i in range(8)]
        g.ident = sb("ident", [P, P])
        g.cols = sb("cols", [P, VROWS])
        g.mod_l0 = sb("mod_l0", [P, BATCH, 2 * KD + NT])
        g.mod_l1 = sb("mod_l1", [P, BATCH, 2 * KD])
        g.decay = sb("decay", [P, KI, STATE])
        g.taps = sb("taps", [P, KI, TAPS])
        g.idx_first = sb("idx_first", [P, NT], I32)
        g.idx_in = sb("idx_in", [P, NT], I32)
        g.idx_max = sb("idx_max", [1, 1], I32)
        g.mhalf = sb("mhalf", [P, NT])

        with ExitStack() as weights:
            def sl(name, shape):
                return weights.enter_context(nc.sbuf_tensor(name, shape, F32))

            g.w_qkv = {n: sl(f"w_{n}", [P, KD, DIM]) for n in "qkv"}
            g.w_out = sl("w_out", [P, KD, DIM])
            g.q_bias = sl("q_bias", [P, DIM])
            g.v_bias = sl("v_bias", [P, DIM])
            g.out_bias = sl("out_bias", [P, DIM])
            g.k_bias = sl("k_bias", [P, KD])
            g.att = sl("att", [P, KD, P])
            prologue(nc, a, g)
            layer0(nc, a, g)
        layer1(nc, a, g)


def column(g, name, k):
    return g.cols[:, COLUMN[name] + k:COLUMN[name] + k + 1]


def prologue(nc, a, g):
    banks, ident, cols = g.banks, g.ident, g.cols

    with ExitStack() as ctx:
        def sb(name, shape, dt=F32):
            return ctx.enter_context(nc.sbuf_tensor(name, shape, dt))

        def sem(name):
            return ctx.enter_context(nc.semaphore(name))

        rows = sb("rows", [VROWS, P])
        idx_row = sb("idx_row", [1, SEQ], I32)
        mask_in = sb("mask_in", [BATCH * NT, P])
        cond = sb("cond", [BATCH, EMB])
        cond_silu = sb("cond_silu", [BATCH, EMB])
        cond_t = sb("cond_t", [P, KE, BATCH])
        w_emb = sb("w_emb", [P, KE, 2 * DIM])
        w_ada = sb("w_ada", [P, KE, 3 * DIM])
        ln_b_wide = sb("ln_b_wide", [P, KD, P])
        emb = sb("emb", [P, 2 * KD, BATCH])
        ada = sb("ada", [P, 2 * KD, BATCH])
        gate_bias = sb("gate_bias", [BATCH, DIM])
        gate = sb("gate", [BATCH, DIM])
        a_raw = sb("a_raw", [P, KI, STATE])
        a_exp = sb("a_exp", [P, KI, STATE])

        rows_loaded = sem("rows_loaded")
        small_loaded = sem("small_loaded")
        cond_loaded = sem("cond_loaded")
        qkv_loaded = sem("qkv_loaded")
        emb_loaded = sem("emb_loaded")
        ada_loaded = sem("ada_loaded")
        gate_stored = sem("gate_stored")
        ident_zero = sem("ident_zero")
        ident_ready = sem("ident_ready")
        silu_ready = sem("silu_ready")
        decay_exp = sem("decay_exp")
        turned = sem("turned")
        cols_ready = sem("cols_ready")
        cond_ready = sem("cond_ready")
        wide_ready = sem("wide_ready")
        bias_ready = sem("bias_ready")
        mods_ready = sem("mods_ready")
        folded = sem("folded")
        block = ctx.enter_context(nc.Block())

        @block.sync
        def _(sp):
            for name, n in VECTORS:
                at = COLUMN[name]
                sp.dma_start(rows[at:at + n, :], a[name].rearrange("(k p) -> k p", p=P)[0:n, :]).then_inc(rows_loaded, DMA)
            sp.dma_start(mask_in[:, :], a["mask_BxSx1_fk1"].rearrange("b (t p) o -> (b t) (p o)", p=P)).then_inc(rows_loaded, DMA)
            sp.dma_start(cond[:, :], a["cond_2048"]).then_inc(cond_loaded, DMA)
            for n in "qvk":
                sp.dma_start(g.w_qkv[n][:, :, :], a[f"L0_cond_W{n}"].rearrange("(k p) n -> p k n", p=P)).then_inc(qkv_loaded, DMA)
            sp.dma_start(w_emb[:, :, :], a["L0_cond_W_emb"].rearrange("(k p) n -> p k n", p=P)).then_inc(emb_loaded, DMA)
            sp.dma_start(w_ada[:, :, :], a["L1_cond_W_ada"].rearrange("(k p) n -> p k n", p=P)).then_inc(ada_loaded, DMA)
            sp.wait_ge(folded, 18)
            sp.dma_start(g.gate_dram, gate[:, :]).then_inc(gate_stored, DMA)
            sp.wait_ge(gate_stored, DMA)

        @block.scalar
        def _(act):
            act.dma_start(g.q_bias[:, :], a["L0_cond_bq"].partition_broadcast(P)).then_inc(small_loaded, DMA)
            act.dma_start(g.v_bias[:, :], a["L0_cond_bv"].partition_broadcast(P)).then_inc(small_loaded, DMA)
            act.dma_start(g.out_bias[:, :], a["L0_cond_b_out"].partition_broadcast(P)).then_inc(small_loaded, DMA)
            act.dma_start(gate_bias[:, :], a["L1_cond_b_ada"][2 * DIM:3 * DIM].partition_broadcast(BATCH)).then_inc(small_loaded, DMA)
            act.dma_start(a_raw[:, :, :], a["L1_cond_A_log"].rearrange("(k p) s -> p k s", p=P)).then_inc(small_loaded, DMA)
            act.dma_start(g.taps[:, :, :], a["L1_cond_conv_w"].rearrange("(k p) o t -> p k (o t)", p=P)).then_inc(small_loaded, DMA)
            act.dma_start(g.idx_first[:, :], a["itok_S_0_1023"].rearrange("(t p) -> p t", p=P), allow_slow_non_contiguous=True).then_inc(small_loaded, DMA)
            act.dma_start(idx_row[:, :], a["itok_S_0_1023"].rearrange("(o s) -> o s", o=1)).then_inc(small_loaded, DMA)
            act.dma_start(g.w_out[:, :, :], a["L0_cond_W_out"].rearrange("(k p) n -> p k n", p=P)).then_inc(small_loaded, DMA)
            act.wait_ge(cond_loaded, DMA)
            nc.scalar.activation(cond_silu[:, :], cond[:, :], ACT.Silu).then_inc(silu_ready, 1)
            act.wait_ge(small_loaded, 9 * DMA)
            nc.scalar.activation(a_exp[:, :, :], a_raw[:, :, :], ACT.Exp).then_inc(decay_exp, 1)

        @block.gpsimd
        def _(pool):
            nc.gpsimd.memset(ident[:, :], 0.0).then_inc(ident_zero, 1)
            nc.gpsimd.memset(g.mhalf[:, :], -0.5).then_inc(ident_zero, 1)
            pool.wait_ge(ident_zero, 1)
            nc.gpsimd.affine_select(out=ident[:, :], in_=ident[:, :], compare_op=ALU.not_equal, fill=1.0, base=0,
                                    pattern=[[-1, P]], channel_multiplier=1).then_inc(ident_ready, 1)
            pool.wait_ge(ident_zero, 2)

        @block.tensor
        def _(pe):
            pe.wait_ge(ident_ready, 1)
            pe.wait_ge(rows_loaded, (len(VECTORS) + 1) * DMA)
            nc.tensor.transpose(banks[0][:, 0:VROWS], rows[:, :], ident[0:VROWS, 0:VROWS]).then_inc(turned, 1)
            nc.tensor.transpose(banks[1][:, 0:BATCH * NT], mask_in[:, :], ident[0:BATCH * NT, 0:BATCH * NT]).then_inc(turned, 1)
            pe.wait_ge(silu_ready, 1)
            for k in range(KE):
                last = nc.tensor.transpose(banks[2][:, k * BATCH:(k + 1) * BATCH], cond_silu[:, k * P:(k + 1) * P],
                                           ident[0:BATCH, 0:BATCH])
            last.then_inc(turned, 1)
            pe.wait_ge(wide_ready, 1)
            pe.wait_ge(qkv_loaded, 3 * DMA)
            for bank, n in ((3, "q"), (4, "v")):
                for k in range(KD):
                    last = nc.tensor.matmul(banks[bank][:, :], ln_b_wide[:, k, :], g.w_qkv[n][:, k, :], start=(k == 0), stop=(k == KD - 1))
            for i in range(KD):
                for k in range(KD):
                    last = nc.tensor.matmul(banks[5][:, i:i + 1], g.w_qkv["k"][:, k, i * P:(i + 1) * P], column(g, "L0_cond_ln_b", k),
                                            start=(k == 0), stop=(k == KD - 1))
            last.then_inc(bias_ready, 1)
            pe.wait_ge(cond_ready, 1)
            for bank, w, arrived in ((6, w_emb, emb_loaded), (7, w_ada, ada_loaded)):
                pe.wait_ge(arrived, DMA)
                for m in range(2 * KD):
                    for k in range(KE):
                        last = nc.tensor.matmul(banks[bank][:, m * BATCH:(m + 1) * BATCH], w[:, k, m * P:(m + 1) * P], cond_t[:, k, :],
                                                start=(k == 0), stop=(k == KE - 1))
                last.then_inc(mods_ready, 1)
            for k in range(KE):
                last = nc.tensor.matmul(banks[0][0:BATCH, :], cond_t[:, k, :], w_ada[:, k, 2 * DIM:3 * DIM], start=(k == 0), stop=(k == KE - 1))
            last.then_inc(mods_ready, 1)

        @block.vector
        def _(dve):
            def wide(name, n):
                return cols[:, COLUMN[name]:COLUMN[name] + n].unsqueeze(2).to_broadcast([P, n, BATCH])

            nc.vector.memset(g.att[:, :, :], 0.0).then_inc(folded, 1)
            dve.wait_ge(turned, 2)
            nc.vector.tensor_copy(cols[:, :], banks[0][:, 0:VROWS]).then_inc(cols_ready, 1)
            nc.vector.tensor_copy(g.mod_l0[:, :, 2 * KD:], banks[1][:, 0:BATCH * NT].rearrange("p (b t) -> p b t", b=BATCH)).then_inc(cols_ready, 1)
            dve.wait_ge(cols_ready, 2)
            nc.vector.tensor_copy(ln_b_wide[:, :, :], cols[:, COLUMN["L0_cond_ln_b"]:COLUMN["L0_cond_ln_b"] + KD].unsqueeze(2).to_broadcast([P, KD, P])).then_inc(wide_ready, 1)
            dve.wait_ge(turned, 3)
            nc.vector.tensor_copy(cond_t[:, :, :], banks[2][:, 0:KE * BATCH].rearrange("p (k b) -> p k b", k=KE)).then_inc(cond_ready, 1)
            dve.wait_ge(small_loaded, 9 * DMA)
            dve.wait_ge(decay_exp, 1)
            nc.vector.tensor_scalar(g.decay[:, :, :], a_exp[:, :, :], -1.0, None, ALU.mult).then_inc(folded, 1)
            nc.vector.tensor_reduce(g.idx_max[:, :], idx_row[:, :], AX.X, ALU.max).then_inc(folded, 1)
            nc.vector.tensor_copy(g.idx_in[:, :], g.idx_first[:, :]).then_inc(folded, 1)
            dve.wait_ge(bias_ready, 1)
            nc.vector.tensor_tensor(g.q_bias[:, :], banks[3][:, :], g.q_bias[:, :], ALU.add).then_inc(folded, 1)
            nc.vector.tensor_tensor(g.v_bias[:, :], banks[4][:, :], g.v_bias[:, :], ALU.add).then_inc(folded, 1)
            nc.vector.tensor_tensor(g.k_bias[:, :], banks[5][:, 0:KD], cols[:, COLUMN["L0_cond_bk"]:COLUMN["L0_cond_bk"] + KD], ALU.add).then_inc(folded, 1)
            for n in "qkv":
                for k in range(KD):
                    last = nc.vector.tensor_scalar(g.w_qkv[n][:, k, :], g.w_qkv[n][:, k, :], column(g, "L0_cond_ln_w", k), None, ALU.mult)
                last.then_inc(folded, 1)
            dve.wait_ge(mods_ready, 1)
            nc.vector.tensor_tensor(emb[:, :, :], banks[6][:, 0:2 * KD * BATCH].rearrange("p (m b) -> p m b", b=BATCH), wide("L0_cond_b_emb", 2 * KD), ALU.add).then_inc(folded, 1)
            dve.wait_ge(mods_ready, 3)
            nc.vector.tensor_tensor(ada[:, :, :], banks[7][:, 0:2 * KD * BATCH].rearrange("p (m b) -> p m b", b=BATCH), wide("L1_cond_b_ada", 2 * KD), ALU.add).then_inc(folded, 1)
            dve.wait_ge(folded, 12)
            for m, mod, scale, shift, w, b in ((emb, g.mod_l0, 0, KD, "L0_cond_ln2_w", "L0_cond_ln2_b"), (ada, g.mod_l1, KD, 0, "L1_cond_gamma", "L1_cond_beta")):
                turned_mod = mod[:, :, :].rearrange("p b i -> p i b")
                nc.vector.scalar_tensor_tensor(turned_mod[:, 0:KD, :], m[:, scale:scale + KD, :], 1.0, wide(w, KD), ALU.add, ALU.mult).then_inc(folded, 1)
                nc.vector.scalar_tensor_tensor(turned_mod[:, KD:2 * KD, :], m[:, scale:scale + KD, :], 1.0, wide(b, KD), ALU.add, ALU.mult).then_inc(folded, 1)
            dve.wait_ge(folded, 16)
            for m, mod, shift, at in ((emb, g.mod_l0, KD, 15), (ada, g.mod_l1, 0, 17)):
                turned_mod = mod[:, :, :].rearrange("p b i -> p i b")[:, KD:2 * KD, :]
                last = nc.vector.tensor_tensor(turned_mod, turned_mod, m[:, shift:shift + KD, :], ALU.add)
            last.then_inc(folded, 1)
            nc.vector.tensor_tensor(gate[:, :], banks[0][0:BATCH, :], gate_bias[:, :], ALU.add).then_inc(folded, 1)
            dve.wait_ge(folded, 18)


def layer0(nc, a, g):
    banks, ident = g.banks, g.ident
    x_rows = a["x"].rearrange("b (t p) d -> b p t d", p=P)
    x1_rows = g.x1_dram.rearrange("(b t p) d -> b p t d", p=P, t=NT)
    mask_rows = a["mask_BxSx1_fk1"].rearrange("b s o -> b (s o)")

    with ExitStack() as ctx:
        def sb(name, shape):
            return ctx.enter_context(nc.sbuf_tensor(name, shape, F32))

        def sem(name):
            return ctx.enter_context(nc.semaphore(name))

        z = sb("z", [P, NT, DIM])
        z_t = sb("z_t", [P, KD, SEQ])
        k_t = sb("k_t", [P, KD, SEQ])
        k_exp = sb("k_exp", [P, NT, DIM])
        values = sb("values", [P, NT, DIM])
        qy = sb("qy", [P, NT, DIM])
        q_t = sb("q_t", [P, KD, SEQ])
        h_t = sb("h_t", [P, KD, SEQ])
        res = sb("res", [P, NT, DIM])
        mask_add = sb("mask_add", [P, SEQ])
        mod_cur = sb("mod_cur", [P, 2 * KD])
        mask_cur = sb("mask_cur", [P, NT])
        x_raw = sb("x_raw", [P, NT, 6])
        x_mv = sb("x_mv", [P, NT, 2])
        x_var = sb("x_var", [P, NT])
        x_rs = sb("x_rs", [P, NT])
        y_raw = sb("y_raw", [P, NT, 6])
        y_mv = sb("y_mv", [P, NT, 2])
        y_var = sb("y_var", [P, NT])
        y_rs = sb("y_rs", [P, NT])
        k_top = sb("k_top", [P, KD])
        k_sum = sb("k_sum", [P, KD])
        k_inv = sb("k_inv", [P, KD])
        q_top = sb("q_top", [P, NT, HEADS])
        q_sum = sb("q_sum", [P, NT, HEADS])
        q_inv = sb("q_inv", [P, NT, HEADS])

        x_loaded, res_loaded, mask_loaded, x1_stored = (sem(n) for n in ("x_loaded", "res_loaded", "mask_loaded", "x1_stored"))
        x_stats, x_aggr, x_var_ready, x_rs_ready, z_ready = (sem(n) for n in ("x_stats", "x_aggr", "x_var_ready", "x_rs_ready", "z_ready"))
        y_stats, y_aggr, y_var_ready, y_rs_ready, y_normed = (sem(n) for n in ("y_stats", "y_aggr", "y_var_ready", "y_rs_ready", "y_normed"))
        mm_ready, mm_empty, tr_ready, tr_empty = (sem(n) for n in ("mm_ready", "mm_empty", "tr_ready", "tr_empty"))
        mod_ready, mask_cur_ready, mask_ready = (sem(n) for n in ("mod_ready", "mask_cur_ready", "mask_ready"))
        k_top_ready, k_exp_ready, k_inv_ready = (sem(n) for n in ("k_top_ready", "k_exp_ready", "k_inv_ready"))
        q_top_ready, q_shifted, q_exp_ready, q_summed, q_inv_ready = (sem(n) for n in ("q_top_ready", "q_shifted", "q_exp_ready", "q_summed", "q_inv_ready"))
        kv_ready, att_ready, res_ready = (sem(n) for n in ("kv_ready", "att_ready", "res_ready"))
        started, passed = sem("started"), sem("passed")
        block = ctx.enter_context(nc.Block())

        def batch(ap, b):
            names = "p t d"[:2 * (len(ap.shape) - 1) - 1] if len(ap.shape) == 4 else "t"
            if names == "t":
                return ap[bass.ds(b, 1)]
            return ap[bass.ds(b, 1)].rearrange("o p t d -> (o p) t d")

        def iterations(eng, body):
            body(0, False, True, True)
            with eng.Fori(1, BATCH - 1) as b:
                body(b, True, True, True)
            body(BATCH - 1, True, True, False)
            body(BATCH, True, False, False)

        @block.sync
        def _(sp):
            sp.dma_start(z[:, :, :], batch(x_rows, 0)).then_inc(x_loaded, DMA)

            def body(b, prev, cur, more):
                if prev:
                    sp.wait_ge(x_loaded, DMA)
                    sp.dma_start(res[:, :, :], batch(x_rows, b - 1)).then_inc(res_loaded, DMA)
                if cur:
                    if not (isinstance(b, int) and b == 0):
                        need(sp, mm_empty, mm_use(b, "y") - 2 * NT)
                    sp.wait_ge(x_loaded, DMA)
                    sp.dma_start(mask_add[:, :], mask_rows[bass.ds(b, 1)].rearrange("o s -> (o s)").partition_broadcast(P)).then_inc(mask_loaded, DMA)
                if more:
                    need(sp, tr_ready, tr_use(b, "z") + NT)
                    sp.wait_ge(x_loaded, DMA)
                    sp.dma_start(z[:, :, :], batch(x_rows, b + 1)).then_inc(x_loaded, DMA)
                if prev:
                    need(sp, mm_empty, mm_use(b, "W") + NT)
                    sp.wait_ge(x_loaded, DMA)
                    sp.dma_start(batch(x1_rows, b - 1), res[:, :, :]).then_inc(x1_stored, DMA)
                    need(sp, x1_stored, DMA * b)
                    sp.sem_inc(passed, 1)

            iterations(sp, body)

        @block.tensor
        def _(pe):
            def product(use, stationary, moving, blocks):
                n, at = use
                need(pe, mm_empty, n + at - (MM_RING - 1))
                out = banks[at % MM_RING]
                for k in range(blocks):
                    last = nc.tensor.matmul(out[:, :], stationary(k), moving(k), start=(k == 0), stop=(k == blocks - 1))
                last.then_inc(mm_ready, 1)

            def turn(n, at, sources):
                need(pe, tr_empty, n + at - (TR_RING - 1))
                out = banks[MM_RING + at % TR_RING]
                for j, source in enumerate(sources):
                    last = nc.tensor.transpose(out[:, j * P:(j + 1) * P], source, ident[:, :])
                last.then_inc(tr_ready, 1)

            def body(b, prev, cur, more):
                if prev:
                    need(pe, tr_empty, tr_use(b - 1, "q") + NT)
                    need(pe, att_ready, 2 * b)
                    n = mm_use(b, "y")
                    for t in range(NT):
                        need(pe, mm_empty, n + t - (MM_RING - 1))
                        for i in range(KD):
                            last = nc.tensor.matmul(banks[t % MM_RING][:, i * P:(i + 1) * P], q_t[:, i, t * P:(t + 1) * P], g.att[:, i, :],
                                                    start=True, stop=True)
                        last.then_inc(mm_ready, 1)
                if cur:
                    n = tr_use(b, "z")
                    for half in range(2):
                        need(pe, z_ready, NT * b + 4 * half + 4)
                        for i in range(KD):
                            turn(n, 4 * half + i, [z[:, 4 * half + j, i * P:(i + 1) * P] for j in range(4)])
                    need(pe, tr_empty, n + NT)
                    n = mm_use(b, "K")
                    for i in range(KD):
                        for half in range(2):
                            product((n, 2 * i + half), lambda k: g.w_qkv["k"][:, k, i * P:(i + 1) * P],
                                    lambda k: z_t[:, k, half * 512:(half + 1) * 512], KD)
                    n = mm_use(b, "V")
                    for t in range(NT):
                        product((n, t), lambda k: z_t[:, k, t * P:(t + 1) * P], lambda k: g.w_qkv["v"][:, k, :], KD)
                if prev:
                    n = tr_use(b, "y")
                    for half in range(2):
                        need(pe, y_normed, NT * (b - 1) + 4 * half + 4)
                        for i in range(KD):
                            turn(n, 4 * half + i, [qy[:, 4 * half + j, i * P:(i + 1) * P] for j in range(4)])
                if cur:
                    n = mm_use(b, "Q")
                    for t in range(NT):
                        product((n, t), lambda k: z_t[:, k, t * P:(t + 1) * P], lambda k: g.w_qkv["q"][:, k, :], KD)
                if prev:
                    need(pe, tr_empty, tr_use(b, "y") + NT)
                    n = mm_use(b, "W")
                    for t in range(NT):
                        product((n, t), lambda k: h_t[:, k, t * P:(t + 1) * P], lambda k: g.w_out[:, k, :], KD)
                if cur:
                    n = tr_use(b, "q")
                    for half in range(2):
                        need(pe, q_exp_ready, NT * b + 4 * half + 4)
                        for i in range(KD):
                            turn(n, 4 * half + i, [qy[:, 4 * half + j, i * P:(i + 1) * P] for j in range(4)])
                    n = tr_use(b, "k")
                    need(pe, k_exp_ready, KD * b + KD)
                    for t in range(NT):
                        turn(n, t, [k_t[:, i, t * P:(t + 1) * P] for i in range(KD)])
                    need(pe, tr_empty, n + NT)
                    need(pe, att_ready, 2 * b)
                    for i in range(KD):
                        for t in range(NT):
                            last = nc.tensor.matmul(banks[6][:, i * P:(i + 1) * P], k_exp[:, t, i * P:(i + 1) * P], values[:, t, i * P:(i + 1) * P],
                                                    start=(t == 0), stop=(t == NT - 1))
                    last.then_inc(kv_ready, 1)

            iterations(pe, body)

        @block.scalar
        def _(act):
            def bank(at):
                return banks[MM_RING + at % TR_RING]

            def body(b, prev, cur, more):
                if cur:
                    n = tr_use(b, "z")
                    for half in range(2):
                        for i in range(KD):
                            need(act, tr_ready, n + 4 * half + i + 1)
                            nc.scalar.copy(z_t[:, i, half * 512:(half + 1) * 512], bank(i)[:, :]).then_inc(tr_empty, 1)
                    for i in range(KD):
                        need(act, k_top_ready, KD * b + i + 1)
                        nc.scalar.activation(k_t[:, i, :], k_t[:, i, :], ACT.Exp, bias=k_top[:, i:i + 1],
                                             accum_out=k_sum[:, i:i + 1]).then_inc(k_exp_ready, 1)
                if prev:
                    need(act, mod_ready, b)
                    n = tr_use(b, "y")
                    for half in range(2):
                        for i in range(KD):
                            need(act, tr_ready, n + 4 * half + i + 1)
                            nc.scalar.activation(h_t[:, i, half * 512:(half + 1) * 512], bank(i)[:, :], ACT.Silu, scale=mod_cur[:, i:i + 1],
                                                 bias=mod_cur[:, KD + i:KD + i + 1]).then_inc(tr_empty, 1)
                if cur:
                    for t in range(NT):
                        need(act, q_shifted, NT * b + t + 1)
                        nc.scalar.activation(qy[:, t, :], qy[:, t, :], ACT.Exp).then_inc(q_exp_ready, 1)
                    n = tr_use(b, "q")
                    for half in range(2):
                        for i in range(KD):
                            need(act, tr_ready, n + 4 * half + i + 1)
                            nc.scalar.copy(q_t[:, i, half * 512:(half + 1) * 512], bank(i)[:, :]).then_inc(tr_empty, 1)
                    n = tr_use(b, "k")
                    need(act, mask_cur_ready, b + 1)
                    for t in range(NT):
                        need(act, tr_ready, n + t + 1)
                        nc.scalar.mul(k_exp[:, t, :], bank(t)[:, :], mask_cur[:, t:t + 1]).then_inc(tr_empty, 1)

            iterations(act, body)

        @block.gpsimd
        def _(pool):
            nc.gpsimd.wait_ge(x_var_ready, 1)
            nc.gpsimd.tensor_tensor(x_rs[:, :], x_var[:, :], g.mhalf[:, :], ALU.pow).then_inc(x_rs_ready, 1)

            def body(b, prev, cur, more):
                if prev:
                    need(pool, y_var_ready, b)
                    nc.gpsimd.tensor_tensor(y_rs[:, :], y_var[:, :], g.mhalf[:, :], ALU.pow).then_inc(y_rs_ready, 1)
                    need(pool, res_loaded, DMA * b)
                    for t in range(NT):
                        nc.gpsimd.tensor_tensor(res[:, t, :], res[:, t, :], g.out_bias[:, :], ALU.add).then_inc(res_ready, 1)
                if more:
                    need(pool, x_var_ready, b + 2)
                    nc.gpsimd.tensor_tensor(x_rs[:, :], x_var[:, :], g.mhalf[:, :], ALU.pow).then_inc(x_rs_ready, 1)
                if cur:
                    for t in range(NT):
                        need(pool, q_top_ready, NT * b + t + 1)
                        heads = qy[:, t, :].rearrange("p (h d) -> p h d", h=HEADS)
                        nc.gpsimd.tensor_tensor(heads, heads, q_top[:, t, :].unsqueeze(2).to_broadcast([P, HEADS, HEAD]), ALU.add).then_inc(q_shifted, 1)

            iterations(pool, body)

        @block.vector
        def _(dve):
            def moments(n, src, raw, mv, var, stats, aggr, var_ready):
                for t in range(NT):
                    nc.vector.bn_stats(raw[:, t, :], src[:, t, :]).then_inc(stats, 1)
                for t in range(NT):
                    if t == 0:
                        need(dve, stats, NT * n + NT)
                        dve.sem_inc(started, 1)
                    nc.vector.bn_aggr(mv[:, t, :], raw[:, t, :]).then_inc(aggr, 1)
                need(dve, aggr, NT * n + NT)
                nc.vector.tensor_scalar(var[:, :], mv[:, :, 1], EPS, None, ALU.add).then_inc(var_ready, 1)

            def normed(src, mv, rs, ready):
                for t in range(NT):
                    nc.vector.tensor_scalar(src[:, t, :], src[:, t, :], mv[:, t, 0:1], rs[:, t:t + 1], ALU.subtract, ALU.mult).then_inc(ready, 1)

            def body(b, prev, cur, more):
                if prev:
                    need(dve, tr_empty, tr_use(b, "y") - 8)
                    dve.wait_ge(started, 1)
                    nc.vector.tensor_copy(mod_cur[:, :], g.mod_l0[:, bass.ds(b - 1, 1), 0:2 * KD].rearrange("p o i -> p (o i)")).then_inc(mod_ready, 1)
                if cur:
                    if not (isinstance(b, int) and b == 0):
                        need(dve, tr_empty, tr_use(b, "z"))
                    dve.wait_ge(started, 1)
                    nc.vector.tensor_copy(mask_cur[:, :], g.mod_l0[:, bass.ds(b, 1), 2 * KD:].rearrange("p o i -> p (o i)")).then_inc(mask_cur_ready, 1)
                if prev:
                    n = mm_use(b, "y")
                    need(dve, q_inv_ready, b)
                    for t in range(NT):
                        need(dve, mm_ready, n + t + 1)
                        nc.vector.tensor_tensor(qy[:, t, :].rearrange("p (h d) -> p h d", h=HEADS),
                                                banks[t % MM_RING][:, :].rearrange("p (h d) -> p h d", h=HEADS),
                                                q_inv[:, t, :].unsqueeze(2).to_broadcast([P, HEADS, HEAD]), ALU.mult).then_inc(mm_empty, 1)
                    need(dve, mm_empty, n + NT)
                    moments(b - 1, qy, y_raw, y_mv, y_var, y_stats, y_aggr, y_var_ready)
                if cur:
                    need(dve, mask_loaded, DMA * (b + 1))
                    nc.vector.tensor_scalar(mask_add[:, :], mask_add[:, :], 1.0, MASKED, ALU.subtract, ALU.mult).then_inc(mask_ready, 1)
                    need(dve, mask_ready, b + 1)
                    n = mm_use(b, "K")
                    for i in range(KD):
                        for half in range(2):
                            need(dve, mm_ready, n + 2 * i + half + 1)
                            nc.vector.scalar_tensor_tensor(k_t[:, i, half * 512:(half + 1) * 512], banks[(2 * i + half) % MM_RING][:, :], g.k_bias[:, i:i + 1],
                                                           mask_add[:, half * 512:(half + 1) * 512], ALU.add, ALU.add).then_inc(mm_empty, 1)
                        need(dve, mm_empty, n + 2 * i + 2)
                        nc.vector.tensor_reduce(k_top[:, i:i + 1], k_t[:, i, :], AX.X, ALU.max, negate=True).then_inc(k_top_ready, 1)
                if prev:
                    need(dve, y_rs_ready, b)
                    normed(qy, y_mv, y_rs, y_normed)
                if cur:
                    n = mm_use(b, "V")
                    for t in range(NT):
                        need(dve, mm_ready, n + t + 1)
                        nc.vector.tensor_tensor(values[:, t, :], banks[t % MM_RING][:, :], g.v_bias[:, :], ALU.add).then_inc(mm_empty, 1)
                if more:
                    need(dve, x_loaded, DMA * (b + 2))
                    moments(b + 1, z, x_raw, x_mv, x_var, x_stats, x_aggr, x_var_ready)
                if cur:
                    n = mm_use(b, "Q")
                    for t in range(NT):
                        need(dve, mm_ready, n + t + 1)
                        nc.vector.tensor_tensor(qy[:, t, :], banks[t % MM_RING][:, :], g.q_bias[:, :], ALU.add).then_inc(mm_empty, 1)
                        need(dve, mm_empty, n + t + 1)
                        nc.vector.tensor_reduce(q_top[:, t, :], qy[:, t, :].rearrange("p (h d) -> p h d", h=HEADS), AX.X, ALU.max,
                                                negate=True).then_inc(q_top_ready, 1)
                    need(dve, k_exp_ready, KD * b + KD)
                    nc.vector.reciprocal(k_inv[:, :], k_sum[:, :]).then_inc(k_inv_ready, 1)
                if more:
                    need(dve, x_rs_ready, b + 2)
                    normed(z, x_mv, x_rs, z_ready)
                if prev:
                    n = mm_use(b, "W")
                    for t in range(NT):
                        need(dve, mm_ready, n + t + 1)
                        need(dve, res_ready, NT * (b - 1) + t + 1)
                        nc.vector.tensor_tensor(res[:, t, :], banks[t % MM_RING][:, :], res[:, t, :], ALU.add).then_inc(mm_empty, 1)
                if cur:
                    for t in range(NT):
                        need(dve, q_exp_ready, NT * b + t + 1)
                        nc.vector.tensor_reduce(q_sum[:, t, :], qy[:, t, :].rearrange("p (h d) -> p h d", h=HEADS), AX.X, ALU.add).then_inc(q_summed, 1)
                    need(dve, q_summed, NT * b + NT)
                    nc.vector.reciprocal(q_inv[:, :, :], q_sum[:, :, :]).then_inc(q_inv_ready, 1)
                    need(dve, kv_ready, b + 1)
                    need(dve, k_inv_ready, b + 1)
                    for h in range(2):
                        at = slice(h * HEAD, (h + 1) * HEAD)
                        nc.vector.tensor_tensor(g.att[at, :, at], banks[6][at, :].rearrange("p (i d) -> p i d", i=KD)[:, :, at],
                                                k_inv[at, :].unsqueeze(2).to_broadcast([HEAD, KD, HEAD]), ALU.mult).then_inc(att_ready, 1)

            nc.vector.memset(k_sum[:, :], 0.0).then_inc(started, 1)
            dve.wait_ge(x_loaded, DMA)
            moments(0, z, x_raw, x_mv, x_var, x_stats, x_aggr, x_var_ready)
            dve.wait_ge(x_rs_ready, 1)
            normed(z, x_mv, x_rs, z_ready)
            iterations(dve, body)


def layer1(nc, a, g):
    banks, ident = g.banks, g.ident
    x1_rows = g.x1_dram.rearrange("(b t p) d -> b t p d", p=P, t=NT)
    y_rows = g.y_dram.rearrange("(t p) d -> t p d", p=P)
    out_rows = a["out"].rearrange("b (t p) d -> b t p d", p=P)
    w_in_dram = a["L1_cond_W_in"].rearrange("(k p) n -> p k n", p=P)

    with ExitStack() as ctx:
        def sb(name, shape):
            return ctx.enter_context(nc.sbuf_tensor(name, shape, F32))

        def sem(name):
            return ctx.enter_context(nc.semaphore(name))

        w_xp = sb("w_xp", [P, KI, XD])
        w_dt = sb("w_dt", [RANK, INNER])
        w_y = sb("w_y", [P, KI, DIM])
        w_in = sb("w_in", [P, W_IN_RING, KD, P])
        d_diag = sb("d_diag", [P, KI, P])
        rows = sb("rows1", [P, CT, DIM])
        h_t = sb("h1_t", [P, 2, KD, CHUNK])
        xd = sb("xd", [XD, CHUNK])
        xm = sb("xm", [P, KI, CHUNK])
        zs = sb("zs", [P, KI, CHUNK])
        dt = sb("dt", [P, 2, KI, CHUNK])
        u = sb("u", [P, KI, CHUNK])
        acc = sb("acc", [P, CT, INNER])
        db = sb("db", [P, RING, 2, CHUNK])
        hs = sb("hs", [P, RING, 2, CHUNK])
        b_wide = sb("b_wide", [P, 2, CHUNK])
        c_t = sb("c_t", [P, 2, CT, STATE])
        gate = sb("gate_wide", [P, DIM])
        fin = sb("fin", [P, 2, DIM])
        mod_cur = sb("mod1_cur", [P, 2 * KD])
        raw = sb("raw1", [P, CT, 6])
        mv = sb("mv1", [P, CT, 2])
        var = sb("var1", [P, CT])
        rs = sb("rs1", [P, CT])
        halo = sb("halo", [P, KI, TAPS - 1])
        carry = sb("carry", [P, KI, STATE])
        state_banks, out_bank, decay_banks, work_banks = banks[0:2], banks[2], banks[3:6], banks[6:8]

        weights_loaded, d_ready = sem("weights1_loaded"), sem("d_ready")
        w_in_loaded = [sem(f"w_in_loaded{i}") for i in range(W_IN_RING)]
        rows_loaded, gate_loaded, b_stored = (sem(n) for n in ("rows1_loaded", "gate_loaded", "b_stored"))
        b_loaded, y_stored = ([sem(f"{n}{i}") for i in range(2)] for n in ("b_loaded", "y_stored"))
        fin_loaded, fin_added, fin_stored = ([sem(f"fin_{n}{i}") for i in range(2)] for n in ("loaded", "added", "stored"))
        fin_free, idx_in_ready, mod_ready = (sem(n) for n in ("fin_free", "idx_in_ready", "mod1_ready"))
        stats, aggr, var_ready, rs_ready, normed = (sem(n) for n in ("stats1", "aggr1", "var1_ready", "rs1_ready", "normed1"))
        work_ready, work_empty = ([sem(f"work_{n}{i}") for i in range(2)] for n in ("ready", "empty"))
        out_ready, out_empty = sem("out_ready"), sem("out_empty")
        tap_done, halo_done = sem("tap_done"), sem("halo_done")
        xm_ready, zs_ready, dt_exp, dt_log, dt_ready, u_ready = (sem(n) for n in ("xm_ready", "zs_ready", "dt_exp", "dt_log", "dt_ready", "u_ready"))
        da_ready, db_ready, scanned, turned, summed, carried = (sem(n) for n in ("da_ready", "db_ready", "scanned", "turned1", "summed", "carried"))
        passed = sem("passed1")
        block = ctx.enter_context(nc.Block())

        def apart(eng, semaphore, value):
            need(eng, semaphore, value)
            if not isinstance(value, int):
                eng.sem_inc(passed, 1)

        def work_bank(place, stage, i):
            return work_banks[place[1][stage, i] % 2]

        def claimed(pe, place, stage, i):
            n = place[1][stage, i]
            need(pe, work_empty[n % 2], place[0] + n // 2)
            return work_banks[n % 2]

        def filled_by(place, stage, i):
            n = place[1][stage, i]
            return work_ready[n % 2], place[0] + n // 2 + 1

        def read_by(place, stage, i):
            n = place[1][stage, i]
            return work_empty[n % 2], place[0] + n // 2 + 1

        def last_z(place, m):
            n = (m - KI // 2) if m else -2 * KI // 2
            return work_ready[n % 2], place[0] + n // 2 + 1

        def fills(place, stage, i):
            return work_ready[place[1][stage, i] % 2]

        def empties(place, stage, i):
            return work_empty[place[1][stage, i] % 2]

        def either(eng, first_chunk, both_chunks):
            largest = eng.value_load(g.idx_max[0:1, 0:1], min_val=0, max_val=SEQ - 1)
            with eng.If(largest < CHUNK):
                first_chunk()
            with eng.Else():
                both_chunks()

        def batches(eng, body):
            body(0)
            with eng.Fori(1, BATCH) as b:
                body(b)

        def turns(eng, turn, end):
            turn(0, 0, False, True)
            with eng.Fori(0, BATCH // 2 - 1) as pair:
                turn(2 * pair + 1, 1, True, True)
                turn(2 * pair + 2, 0, True, True)
            turn(BATCH - 1, 1, True, False)
            end()

        front_place = (0, FRONT)
        end_place = (turn_place(BATCH - 1)[0] + len(LAST_TURN) // 2, END)

        def chunk_place(it):
            return len(CHUNK_ORDER) // 2 * it, CHUNK_ORDER

        def w_in_uses(b, stage):
            n = KI // W_IN_RING
            if stage == "xm":
                return 0 if isinstance(b, int) and b == 0 else n + 2 * n * (b - 1)
            return 2 * n * b + (n if isinstance(b, int) and b == BATCH - 1 else 2 * n)

        @block.sync
        def _(sp):
            sp.dma_start(w_xp[:, :, :], a["L1_cond_W_xp"].rearrange("(k p) n -> p k n", p=P)).then_inc(weights_loaded, DMA)
            sp.dma_start(w_dt[:, :], a["L1_cond_W_dt"]).then_inc(weights_loaded, DMA)
            sp.dma_start(w_y[:, :, :], a["L1_cond_W_out"].rearrange("(k p) n -> p k n", p=P)).then_inc(weights_loaded, DMA)

            def load_w_in(m, stage, before):
                if before is not None:
                    need(sp, *before)
                at = m if stage == "xm" else KI + m
                sp.dma_start(w_in[:, m % W_IN_RING, :, :], w_in_dram[:, :, at * P:(at + 1) * P]).then_inc(w_in_loaded[m % W_IN_RING], DMA)

            def store_b(it, place):
                apart(sp, *read_by(place, "xd", 0))
                sp.dma_start(g.b_dram[bass.ds(it, 1)].rearrange("o s t -> (o s) t"), xd[RANK:RANK + STATE, :]).then_inc(b_stored, DMA)

            def load_b(it, s):
                apart(sp, b_stored, DMA * (it + 1))
                apart(sp, db_ready, PIECES * it + 4 * (s - 1))
                sp.dma_start(b_wide[:, s % 2, :], g.b_dram[bass.ds(it, 1), s, :].rearrange("o t -> (o t)").partition_broadcast(P)).then_inc(b_loaded[s % 2], DMA)

            def load_gate(b):
                sp.dma_start(gate[:, :], g.gate_dram[bass.ds(b, 1)].rearrange("o d -> (o d)").partition_broadcast(P)).then_inc(gate_loaded, DMA)

            def store_y(it, c, t):
                need(sp, out_empty, CT * it + t + 1)
                sp.dma_start(y_rows[c * CT + t], fin[:, t % 2, :]).then_inc(y_stored[t % 2], DMA)

            def load_fin(b, k, stores):
                if k < 2:
                    apart(sp, y_stored[k % 2], DMA * CT // 2 * stores)
                else:
                    apart(sp, fin_stored[k % 2], DMA * (NT // 2 * b + k // 2))
                sp.dma_start(fin[:, k % 2, :], x1_rows[bass.ds(b, 1), k].rearrange("o p d -> (o p) d")).then_inc(fin_loaded[k % 2], DMA)

            def store_fin(b, k):
                apart(sp, fin_added[k % 2], DMA * (NT // 2 * b + k // 2 + 1))
                sp.dma_start(out_rows[bass.ds(b, 1), k].rearrange("o p d -> (o p) d"), fin[:, k % 2, :]).then_inc(fin_stored[k % 2], DMA)

            def all_stored(b):
                for i in range(2):
                    apart(sp, fin_stored[i], DMA * NT // 2 * (b + 1))

            def finish(b, stores):
                for k in range(2):
                    load_fin(b, k, stores)
                for k in range(NT):
                    store_fin(b, k)
                    if k + 2 < NT:
                        load_fin(b, k + 2, stores)
                all_stored(b)

            def turn(b, par, prev, more):
                place = turn_place(b)
                for s in range(STATE):
                    if more:
                        if s == 0:
                            for m in range(W_IN_RING):
                                load_w_in(m, "xm", last_z(place, m) if prev else filled_by(front_place, "xm", m + W_IN_RING))
                        for m in {3: (4, 5), 4: (6, 7)}.get(s, ()):
                            load_w_in(m, "xm", filled_by(place, "xm", m - W_IN_RING))
                        if s == 9:
                            store_b(b + 1, place)
                    for m in {6: (0, 1), 7: (2, 3)}.get(s, ()):
                        load_w_in(m, "z", filled_by(place, "xm", m + W_IN_RING) if more else last_z(place, m))
                    for m in {9: (4, 5), 11: (6, 7)}.get(s, ()):
                        load_w_in(m, "z", filled_by(place, "z", m - W_IN_RING))
                    if prev:
                        if s in (3, 5, 6, 8):
                            store_y(b - 1, 0, (3, 5, 6, 8).index(s))
                        if s == 10:
                            load_fin(b - 1, 0, b)
                            load_fin(b - 1, 1, b)
                        if 11 <= s < 15:
                            for k in (2 * (s - 11), 2 * (s - 11) + 1):
                                store_fin(b - 1, k)
                                if k + 2 < NT:
                                    load_fin(b - 1, k + 2, b)
                    if s == 9:
                        load_gate(b)
                    if s + 2 < STATE:
                        load_b(b, s + 2)
                    elif more:
                        load_b(b + 1, s + 2 - STATE)
                if prev:
                    all_stored(b - 1)
                sp.sem_inc(fin_free, 1)

            def first_chunk():
                for m in range(KI):
                    load_w_in(m, "xm", filled_by(front_place, "xm", m - W_IN_RING) if m >= W_IN_RING else None)
                store_b(0, front_place)
                load_b(0, 0)
                load_b(0, 1)

                def end():
                    for t in range(CT):
                        store_y(BATCH - 1, 0, t)
                    finish(BATCH - 1, BATCH)

                turns(sp, turn, end)

            def both_chunks():
                def body(b):
                    for c in range(CHUNKS):
                        it = CHUNKS * b + c
                        place = chunk_place(it)
                        for m in range(KI):
                            load_w_in(m, "xm", filled_by(place, "xm", m - W_IN_RING) if m >= W_IN_RING else None)
                        store_b(it, place)
                        for s in range(STATE):
                            load_b(it, s)
                        load_gate(b)
                        for m in range(KI):
                            load_w_in(m, "z", filled_by(place, "z", m - W_IN_RING) if m >= W_IN_RING else filled_by(place, "xm", m + W_IN_RING))
                        for t in range(CT):
                            store_y(it, c, t)
                    finish(b, CHUNKS * (b + 1))
                    sp.sem_inc(fin_free, 1)

                batches(sp, body)

            either(sp, first_chunk, both_chunks)
            for s in fin_stored:
                sp.wait_ge(s, DMA * NT // 2 * BATCH)

        @block.tensor
        def _(pe):
            pe.wait_ge(weights_loaded, 3 * DMA)
            pe.wait_ge(d_ready, KI)

            def norm_turned(it, place, i):
                need(pe, normed, CT * it + CT)
                out = claimed(pe, place, "h", i)
                for t in range(CT):
                    last = nc.tensor.transpose(out[:, t * P:(t + 1) * P], rows[:, t, i * P:(i + 1) * P], ident[:, :])
                last.then_inc(fills(place, "h", i), 1)

            def project_in(par, place, loads, stage, m, ks, norm_place):
                if ks[0] == 0:
                    out = claimed(pe, place, stage, m)
                    need(pe, w_in_loaded[m % W_IN_RING], DMA * (loads + m // W_IN_RING + 1))
                    if norm_place is not None:
                        for i in (KD - 2, KD - 1):
                            need(pe, *read_by(norm_place, "h", i))
                for k in ks:
                    last = nc.tensor.matmul(work_bank(place, stage, m)[:, :], w_in[:, m % W_IN_RING, k, :], h_t[:, par, k, :],
                                            start=(k == 0), stop=(k == KD - 1))
                if ks[-1] == KD - 1:
                    last.then_inc(fills(place, stage, m), 1)

            def project_xd(it, place, js):
                if js[0] == 0:
                    claimed(pe, place, "xd", 0)
                for j in js:
                    need(pe, xm_ready, KI // 2 * it + j // 2 + 1)
                    last = nc.tensor.matmul(work_bank(place, "xd", 0)[0:XD, :], w_xp[:, j, :], xm[:, j, :], start=(j == 0), stop=(j == KI - 1))
                if js[-1] == KI - 1:
                    last.then_inc(fills(place, "xd", 0), 1)

            def c_turned(place):
                out = claimed(pe, place, "C", 0)
                need(pe, *read_by(place, "xd", 0))
                for t in range(CT):
                    last = nc.tensor.transpose(out[:, t * XD:(t + 1) * XD], xd[:, t * P:(t + 1) * P], ident[0:XD, 0:XD])
                last.then_inc(fills(place, "C", 0), 1)

            def project_dt(place, j):
                out = claimed(pe, place, "dt", j)
                nc.tensor.matmul(out[:, :], w_dt[:, j * P:(j + 1) * P], xd[0:RANK, :], start=True, stop=True).then_inc(fills(place, "dt", j), 1)

            def x_turned(place, j):
                out = claimed(pe, place, "init", j)
                for t in range(CT):
                    last = nc.tensor.matmul(out[:, t * P:(t + 1) * P], xm[:, j, t * P:(t + 1) * P], d_diag[:, j, :], start=True, stop=True)
                last.then_inc(fills(place, "init", j), 1)

            def states_turned(it, q, t):
                n = CT * q + t
                if t == 0:
                    need(pe, scanned, BLOCKS * it + 4 * (q + 1))
                need(pe, summed, CT * HALVES * it + max(n - len(state_banks) + 1, 0))
                for j in range(4):
                    last = nc.tensor.transpose(state_banks[n % len(state_banks)][:, j * P:(j + 1) * P], hs[:, (2 * q + j // 2) % RING, j % 2, t * P:(t + 1) * P], ident[:, :])
                last.then_inc(turned, 1)

            def y_turned(it, place, j):
                need(pe, summed, CT * HALVES * it + CT * HALVES)
                out = claimed(pe, place, "y", j)
                for t in range(CT):
                    last = nc.tensor.transpose(out[:, t * P:(t + 1) * P], acc[:, t, j * P:(j + 1) * P], ident[:, :])
                last.then_inc(fills(place, "y", j), 1)

            def project_out(it, place, t, js):
                if js[0] == 0:
                    need(pe, out_empty, CT * it + t)
                    if t == 0:
                        for j in (KI - 2, KI - 1):
                            apart(pe, *read_by(place, "y", j))
                for j in js:
                    last = nc.tensor.matmul(out_bank[:, :], zs[:, j, t * P:(t + 1) * P], w_y[:, j, :], start=(j == 0), stop=(j == KI - 1))
                if js[-1] == KI - 1:
                    last.then_inc(out_ready, 1)

            def turn(b, par, prev, more):
                place = turn_place(b)
                def swap_sums(j):
                    if prev:
                        y_turned(b - 1, place, j)
                    x_turned(place, j)

                for j in range(KI // 2):
                    swap_sums(j)
                for q in range(HALVES):
                    for t in range(CT):
                        states_turned(b, q, t)
                        if q == 0:
                            swap_sums(KI // 2 + t)
                        n = CT * q + t
                        if prev:
                            for tile, first in enumerate((4, 22, 32, 43)):
                                if first <= n < first + KI:
                                    project_out(b - 1, place, tile, [n - first])
                        if more:
                            if 12 <= n < 12 + KD:
                                norm_turned(b + 1, place, n - 12)
                            if 17 <= n < 17 + KI * KD:
                                project_in(1 - par, place, w_in_uses(b + 1, "xm"), "xm", (n - 17) // KD, [(n - 17) % KD], place)
                            if 59 <= n < 59 + KI:
                                project_xd(b + 1, place, [n - 59])
                            if n == 71:
                                c_turned(place)
                            for j, at in enumerate((73, 75, 77, 79, 95, 97, 99, 101)):
                                if n == at:
                                    project_dt(place, j)
                        for m, first in enumerate((51, 55, 67, 81, 85, 103, 107, 111)):
                            if first <= n < first + KD:
                                project_in(par, place, w_in_uses(b, "z"), "z", m, [n - first], None)

            def front(it, par, place, loads):
                for i in range(KD):
                    norm_turned(it, place, i)
                for m in range(KI):
                    project_in(par, place, loads, "xm", m, range(KD), place)
                project_xd(it, place, range(KI))
                c_turned(place)
                for j in range(KI):
                    project_dt(place, j)

            def first_chunk():
                def end():
                    for j in range(KI):
                        y_turned(BATCH - 1, end_place, j)
                    for t in range(CT):
                        project_out(BATCH - 1, end_place, t, range(KI))

                front(0, 0, front_place, 0)
                turns(pe, turn, end)

            def both_chunks():
                def body(b):
                    for c in range(CHUNKS):
                        it = CHUNKS * b + c
                        place, loads = chunk_place(it), 2 * KI // W_IN_RING * it
                        front(it, c, place, loads)
                        for j in range(KI):
                            x_turned(place, j)
                        for q in range(HALVES):
                            for t in range(CT):
                                states_turned(it, q, t)
                        for m in range(KI):
                            project_in(c, place, loads + KI // W_IN_RING, "z", m, range(KD), None)
                        for j in range(KI):
                            y_turned(it, place, j)
                        for t in range(CT):
                            project_out(it, place, t, range(KI))

                batches(pe, body)

            either(pe, first_chunk, both_chunks)

        @block.scalar
        def _(act):
            def filled(place, stage, i):
                need(act, *filled_by(place, stage, i))
                return work_bank(place, stage, i)

            def norm_modulated(it, par, place, i):
                need(act, mod_ready, it + 1)
                src = filled(place, "h", i)
                nc.scalar.activation(h_t[:, par, i, :], src[:, :], ACT.Identity, scale=mod_cur[:, i:i + 1],
                                     bias=mod_cur[:, KD + i:KD + i + 1]).then_inc(empties(place, "h", i), 1)

            def silu_x(place, pair):
                for m in (2 * pair, 2 * pair + 1):
                    need(act, *read_by(place, "xm", m))
                part = xm[:, 2 * pair:2 * pair + 2, :]
                nc.scalar.activation(part, part, ACT.Silu).then_inc(xm_ready, 1)

            def keep_z(place, m):
                src = filled(place, "z", m)
                nc.scalar.copy(zs[:, m, :], src[:, :]).then_inc(empties(place, "z", m), 1)

            def silu_z(place, half):
                for m in (4 * half + 2, 4 * half + 3):
                    need(act, *read_by(place, "z", m))
                part = zs[:, 4 * half:4 * half + 4, :]
                nc.scalar.activation(part, part, ACT.Silu).then_inc(zs_ready, 1)

            def keep_xd(it, place):
                need(act, b_stored, DMA * it)
                src = filled(place, "xd", 0)
                nc.scalar.copy(xd[:, :], src[0:XD, :]).then_inc(empties(place, "xd", 0), 1)

            def keep_c(par, place):
                src = filled(place, "C", 0)
                nc.scalar.copy(c_t[:, par, :, :], src[:, 0:CT * XD].rearrange("p (t x) -> p t x", x=XD)[:, :, RANK + STATE:]).then_inc(empties(place, "C", 0), 1)

            def split_dt(it, par, place, j):
                if j == 4:
                    need(act, dt_ready, 2 * it + 1)
                src = filled(place, "dt", j)
                nc.scalar.activation(rows[:, j % 4, :], src[:, :], ACT.Relu, bias=column(g, "L1_cond_b_dt", j))
                nc.scalar.activation(dt[:, par, j, :], src[:, :], ACT.Abs, bias=column(g, "L1_cond_b_dt", j)).then_inc(empties(place, "dt", j), 1)

            def exp_dt(par, place, half):
                for j in (4 * half + 2, 4 * half + 3):
                    need(act, *read_by(place, "dt", j))
                part = dt[:, par, 4 * half:4 * half + 4, :]
                nc.scalar.activation(part, part, ACT.Exp, scale=-1.0).then_inc(dt_exp, 1)

            def log_dt(it, par, half):
                need(act, dt_exp, 2 * it + half + 1)
                part = dt[:, par, 4 * half:4 * half + 4, :]
                nc.scalar.activation(part, part, ACT.Ln, bias=1.0).then_inc(dt_log, 1)

            def start_sum(place, j):
                src = filled(place, "init", j)
                nc.scalar.copy(acc[:, :, j * P:(j + 1) * P], src[:, :].rearrange("p (t d) -> p t d", t=CT)).then_inc(empties(place, "init", j), 1)

            def decays(it, par, k):
                s, j = k // KI, k % KI
                if k < KI:
                    need(act, dt_ready, 2 * it + j // 4 + 1)
                need(act, scanned, BLOCKS * it + (k - len(decay_banks) + 1 if k >= 2 else k - 1))
                nc.scalar.activation(decay_banks[k % len(decay_banks)][:, :], dt[:, par, j, :], ACT.Exp, scale=g.decay[:, j, s:s + 1]).then_inc(da_ready, 1)

            def turn(b, par, prev, more):
                place = turn_place(b)
                ahead = len(decay_banks)
                for k in range(ahead):
                    decays(b, par, k)
                for n in range(BLOCKS):
                    if n + ahead < BLOCKS:
                        decays(b, par, n + ahead)
                    if n < KI:
                        start_sum(place, n)
                    if more:
                        if 17 <= n < 17 + KD:
                            norm_modulated(b + 1, 1 - par, place, n - 17)
                        if n in (33, 41, 49, 57):
                            silu_x(place, (n - 33) // 8)
                        if n == 71:
                            keep_xd(b + 1, place)
                        if n == 76:
                            keep_c(1 - par, place)
                        for j, at in enumerate((78, 80, 82, 84, 101, 103, 105, 107)):
                            if n == at:
                                split_dt(b + 1, 1 - par, place, j)
                        if n in (87, 109):
                            exp_dt(1 - par, place, n // 109)
                        if n in (91, 113):
                            log_dt(b + 1, 1 - par, n // 113)
                    for m, at in enumerate((59, 63, 75, 89, 93, 111, 115, 119)):
                        if n == at:
                            keep_z(place, m)
                    if n in (95, 121):
                        silu_z(place, n // 121)

            def front(it, par, place):
                for i in range(KD):
                    norm_modulated(it, par, place, i)
                for pair in range(KI // 2):
                    silu_x(place, pair)
                keep_xd(it, place)
                keep_c(par, place)
                for half in range(2):
                    for j in range(4 * half, 4 * half + 4):
                        split_dt(it, par, place, j)
                    exp_dt(par, place, half)
                    log_dt(it, par, half)

            def first_chunk():
                front(0, 0, front_place)
                turns(act, turn, lambda: None)

            def both_chunks():
                def body(b):
                    for c in range(CHUNKS):
                        it = CHUNKS * b + c
                        place = chunk_place(it)
                        front(it, c, place)
                        for j in range(KI):
                            start_sum(place, j)
                        for k in range(BLOCKS):
                            decays(it, c, k)
                        for m in range(KI):
                            keep_z(place, m)
                        silu_z(place, 0)
                        silu_z(place, 1)

                batches(act, body)

            either(act, first_chunk, both_chunks)

        @block.gpsimd
        def _(pool):
            def gather_rows(it, b, c):
                need(pool, dt_ready, 2 * it)
                apart(pool, idx_in_ready, b)
                for t in range(CT):
                    nc.gpsimd.indirect_dma_start(rows[:, t, :], None, g.x1_dram, bass.IndirectOffsetOnAxis(g.idx_in[:, c * CT + t:c * CT + t + 1], axis=0)).then_inc(rows_loaded, DMA)

            def rsqrt(it):
                need(pool, var_ready, it + 1)
                nc.gpsimd.tensor_tensor(rs[:, :], var[:, :], g.mhalf[:, 0:CT], ALU.pow).then_inc(rs_ready, 1)

            def add_dt(it, par, half):
                need(pool, dt_log, 2 * it + half + 1)
                part = dt[:, par, 4 * half:4 * half + 4, :]
                nc.gpsimd.tensor_tensor(part, part, rows[:, :, :], ALU.add).then_inc(dt_ready, 1)

            def dt_x(it, par, jc):
                need(pool, dt_ready, 2 * it + jc // 2 + 1)
                need(pool, xm_ready, KI // 2 * it + jc + 1)
                need(pool, db_ready, PIECES * it - 4 + jc + 1)
                nc.gpsimd.tensor_tensor(u[:, 2 * jc:2 * jc + 2, :], dt[:, par, 2 * jc:2 * jc + 2, :], xm[:, 2 * jc:2 * jc + 2, :], ALU.mult).then_inc(u_ready, 1)

            def inputs(it, k):
                s, jc = k // 4, k % 4
                if k < 4:
                    need(pool, u_ready, 4 * it + jc + 1)
                if jc == 0:
                    need(pool, b_loaded[s % 2], DMA * (STATE // 2 * it + s // 2 + 1))
                need(pool, scanned, BLOCKS * it + 2 * (k - RING + 1))
                nc.gpsimd.tensor_tensor(db[:, k % RING, :, :], u[:, 2 * jc:2 * jc + 2, :], b_wide[:, s % 2, :].unsqueeze(1).to_broadcast([P, 2, CHUNK]),
                                        ALU.mult).then_inc(db_ready, 1)

            def y_complete(stores):
                for i in range(2):
                    apart(pool, y_stored[i], DMA * CT // 2 * stores)

            def add_y(b, k, reach):
                apart(pool, fin_loaded[k % 2], DMA * (NT // 2 * b + k // 2 + 1))
                nc.gpsimd.indirect_dma_start(fin[:, k % 2, :], None, g.y_dram[0:reach, :], bass.IndirectOffsetOnAxis(g.idx_first[:, k:k + 1], axis=0),
                                             compute_op=ALU.add).then_inc(fin_added[k % 2], DMA)

            def turn(b, par, prev, more):
                for q in range(HALVES):
                    for k in (2 * q, 2 * q + 1):
                        inputs(b, k)
                        if more and k >= PIECES - 4:
                            dt_x(b + 1, 1 - par, k - (PIECES - 4))
                    if more:
                        if q == 1:
                            gather_rows(b + 1, b + 1, 0)
                        if q == 3:
                            rsqrt(b + 1)
                        if q == 24:
                            add_dt(b + 1, 1 - par, 0)
                        if q == 29:
                            add_dt(b + 1, 1 - par, 1)
                    if prev and 22 <= q < 22 + NT:
                        if q == 22:
                            y_complete(b)
                        add_y(b - 1, q - 22, CHUNK)

            def front(it, b, c):
                gather_rows(it, b, c)
                rsqrt(it)
                add_dt(it, c, 0)
                add_dt(it, c, 1)
                for jc in range(4):
                    dt_x(it, c, jc)

            def finish(b, stores, reach):
                y_complete(stores)
                for k in range(NT):
                    add_y(b, k, reach)

            def first_chunk():
                front(0, 0, 0)
                turns(pool, turn, lambda: finish(BATCH - 1, BATCH, CHUNK))

            def both_chunks():
                def body(b):
                    for c in range(CHUNKS):
                        it = CHUNKS * b + c
                        front(it, b, c)
                        for k in range(PIECES):
                            inputs(it, k)
                    finish(b, CHUNKS * (b + 1), SEQ)

                batches(pool, body)

            either(pool, first_chunk, both_chunks)

        @block.vector
        def _(dve):
            def moments(it, b):
                dve.sem_inc(passed, 1)
                nc.vector.tensor_copy(mod_cur[:, :], g.mod_l1[:, bass.ds(b, 1), :].rearrange("p o i -> p (o i)")).then_inc(mod_ready, 1)
                need(dve, rows_loaded, CT * DMA * (it + 1))
                for t in range(CT):
                    nc.vector.bn_stats(raw[:, t, :], rows[:, t, :]).then_inc(stats, 1)
                apart(dve, stats, CT * it + CT)
                for t in range(CT):
                    nc.vector.bn_aggr(mv[:, t, :], raw[:, t, :]).then_inc(aggr, 1)
                need(dve, aggr, CT * it + CT)
                nc.vector.tensor_scalar(var[:, :], mv[:, :, 1], EPS, None, ALU.add).then_inc(var_ready, 1)

            def norm(it):
                need(dve, rs_ready, it + 1)
                for t in range(CT):
                    nc.vector.tensor_scalar(rows[:, t, :], rows[:, t, :], mv[:, t, 0:1], rs[:, t:t + 1], ALU.subtract, ALU.mult).then_inc(normed, 1)

            def tap(it, place, m, back):
                bank, w = work_bank(place, "xm", m), g.taps[:, m, TAPS - 1 - back:TAPS - back]
                if back == 0:
                    need(dve, *filled_by(place, "xm", m))
                    nc.vector.tensor_scalar(xm[:, m, :], bank[:, :], w, column(g, "L1_cond_conv_b", m), ALU.mult, ALU.add).then_inc(tap_done, 1)
                else:
                    need(dve, tap_done, (TAPS - 1) * (KI * it + m) + back)
                    last = back == TAPS - 1
                    nc.vector.scalar_tensor_tensor(xm[:, m, back:], bank[:, 0:CHUNK - back], w, xm[:, m, back:], ALU.mult,
                                                   ALU.add).then_inc(empties(place, "xm", m) if last else tap_done, 1)

            def halo_taps(it, m, done):
                need(dve, tap_done, (TAPS - 1) * (KI * it + m) + 1)
                for back in range(1, TAPS):
                    need(dve, halo_done, done + back - 1)
                    nc.vector.scalar_tensor_tensor(xm[:, m, 0:back], halo[:, m, TAPS - 1 - back:], g.taps[:, m, TAPS - 1 - back:TAPS - back],
                                                   xm[:, m, 0:back], ALU.mult, ALU.add).then_inc(halo_done, 1)
                need(dve, halo_done, done + TAPS - 1)

            def scan(it, k):
                need(dve, da_ready, BLOCKS * it + k + 1)
                if k % 2 == 0:
                    need(dve, db_ready, PIECES * it + k // 2 + 1)
                    need(dve, turned, CT * HALVES * it + CT * (k // 4 - 1))
                nc.vector.tensor_tensor_scan(hs[:, k // 2 % RING, k % 2, :], decay_banks[k % len(decay_banks)][:, :], db[:, k // 2 % RING, k % 2, :], 0.0,
                                             ALU.mult, ALU.add).then_inc(scanned, 1)

            def scan_on(it, b, c, q):
                for k in range(4 * q, 4 * q + 4):
                    s, j = k // KI, k % KI
                    need(dve, da_ready, BLOCKS * it + k + 1)
                    need(dve, db_ready, PIECES * it + k // 2 + 1)
                    need(dve, turned, CT * HALVES * it + CT * (q - 1))
                    need(dve, carried, BLOCKS * (b + c))
                    out = hs[:, k // 2 % RING, k % 2, :]
                    nc.vector.tensor_tensor_scan(out, decay_banks[k % len(decay_banks)][:, :], db[:, k // 2 % RING, k % 2, :], carry[:, j, s:s + 1] if c else 0.0,
                                                 ALU.mult, ALU.add).then_inc(scanned, 1)
                    if c == 0:
                        need(dve, scanned, BLOCKS * it + k + 1)
                        nc.vector.tensor_copy(carry[:, j, s:s + 1], out[:, CHUNK - 1:CHUNK]).then_inc(carried, 1)

            def add_states(it, par, place, q, t):
                s, jg = q // 2, q % 2
                if q < 2:
                    for j in (4 * jg + 2, 4 * jg + 3):
                        need(dve, *read_by(place, "init", j))
                else:
                    need(dve, summed, CT * HALVES * it + CT * (q - 2) + t + 1)
                need(dve, turned, CT * HALVES * it + CT * q + t + 1)
                part = acc[:, t, jg * 512:(jg + 1) * 512]
                nc.vector.scalar_tensor_tensor(part, state_banks[(CT * q + t) % len(state_banks)][:, :], c_t[:, par, t, s:s + 1], part, ALU.mult, ALU.add).then_inc(summed, 1)

            def gate_y(it, place, j):
                need(dve, zs_ready, 2 * it + j // 4 + 1)
                need(dve, *filled_by(place, "y", j))
                nc.vector.tensor_tensor(zs[:, j, :], work_bank(place, "y", j)[:, :], zs[:, j, :], ALU.mult).then_inc(empties(place, "y", j), 1)

            def gate_out(it, t, finals):
                if t == 0:
                    need(dve, gate_loaded, DMA * (it + 1))
                    need(dve, fin_free, finals)
                if t >= 2:
                    need(dve, y_stored[t % 2], DMA * (CT // 2 * it + t // 2))
                need(dve, out_ready, CT * it + t + 1)
                nc.vector.tensor_tensor(fin[:, t % 2, :], out_bank[:, :], gate[:, :], ALU.mult).then_inc(out_empty, 1)

            def next_rows():
                nc.vector.tensor_scalar(g.idx_in[:, :], g.idx_in[:, :], SEQ, None, ALU.add).then_inc(idx_in_ready, 1)

            def turn(b, par, prev, more):
                place = turn_place(b)
                for q in range(HALVES):
                    for t in range(CT):
                        n = CT * q + t
                        scan(b, n)
                        if q:
                            add_states(b, par, place, q - 1, t)
                        if prev:
                            if q < 2:
                                gate_y(b - 1, place, 4 * q + t)
                            for tile, at in enumerate((17, 35, 45, 56)):
                                if n == at:
                                    gate_out(b - 1, tile, b)
                        if more and 25 <= n < 25 + KI * TAPS:
                            tap(b + 1, place, (n - 25) // TAPS, (n - 25) % TAPS)
                    if more:
                        if q == 2:
                            moments(b + 1, b + 1)
                        if q == 3:
                            norm(b + 1)
                        if q == 4:
                            next_rows()
                for t in range(CT):
                    add_states(b, par, place, HALVES - 1, t)

            def first_chunk():
                moments(0, 0)
                norm(0)
                next_rows()
                for m in range(KI):
                    for back in range(TAPS):
                        tap(0, front_place, m, back)

                def end():
                    for j in range(KI):
                        gate_y(BATCH - 1, end_place, j)
                    for t in range(CT):
                        gate_out(BATCH - 1, t, BATCH)

                turns(dve, turn, end)

            def both_chunks():
                def body(b):
                    for c in range(CHUNKS):
                        it = CHUNKS * b + c
                        place = chunk_place(it)
                        halos = KI * (1 + TAPS - 1) * b
                        moments(it, b)
                        norm(it)
                        for m in range(KI):
                            tap(it, place, m, 0)
                            if c:
                                halo_taps(it, m, halos + KI + (TAPS - 1) * m)
                            else:
                                need(dve, halo_done, halos)
                                nc.vector.tensor_copy(halo[:, m, :], work_bank(place, "xm", m)[:, CHUNK - TAPS + 1:]).then_inc(halo_done, 1)
                            for back in range(1, TAPS):
                                tap(it, place, m, back)
                        for q in range(HALVES):
                            scan_on(it, b, c, q)
                            for t in range(CT):
                                add_states(it, c, place, q, t)
                        for j in range(KI):
                            gate_y(it, place, j)
                        for t in range(CT):
                            gate_out(it, t, b)
                    next_rows()

                batches(dve, body)

            for j in range(KI):
                nc.vector.tensor_scalar(d_diag[:, j, :], ident[:, :], column(g, "L1_cond_D_param", j), None, ALU.mult).then_inc(d_ready, 1)
            dve.wait_ge(d_ready, KI)
            either(dve, first_chunk, both_chunks)


INPUTS = ["x", "cond_2048", "itok_S_0_1023", "mask_BxSx1_fk1"] + [
    f"L0_cond_{n}" for n in ("ln_w", "ln_b", "Wq", "bq", "Wk", "bk", "Wv", "bv", "W_emb", "b_emb", "ln2_w", "ln2_b", "W_out", "b_out")] + [
    f"L1_cond_{n}" for n in ("W_ada", "b_ada", "gamma", "beta", "W_in", "conv_w", "conv_b", "W_xp", "W_dt", "b_dt", "A_log", "D_param", "W_out")]


def kernel(**inputs):
    import numpy as np
    import concourse.bacc as bacc
    from concourse.bass_utils import run_bass_kernel_spmd

    nc = bacc.Bacc("TRN2", target_bir_lowering=False, num_devices=1)
    arrays, aps = {}, {}
    for name in INPUTS:
        arrays[f"in_{name}"] = np.ascontiguousarray(inputs[name])
        aps[name] = nc.dram_tensor(f"in_{name}", arrays[f"in_{name}"].shape, mybir.dt.from_np(arrays[f"in_{name}"].dtype), kind="ExternalInput").ap()
    aps["out"] = nc.dram_tensor("out", (BATCH, SEQ, DIM), F32, kind="ExternalOutput").ap()
    cond_mamba_kernel(nc, aps)
    result = run_bass_kernel_spmd(nc, [arrays], core_ids=[0])
    return result.results[0]["out"]
```

```python
from contextlib import ExitStack

import concourse.bass as bass
from concourse import mybir

F32 = mybir.dt.float32
I32 = mybir.dt.int32
ALU = mybir.AluOpType
ACT = mybir.ActivationFunctionType
AX = mybir.AxisListType

P = 128
BATCH, SEQ, DIM = 8, 1024, 512
HEADS = 8
HEAD = DIM // HEADS
EMB = 1024
INNER, STATE, RANK, TAPS = 1024, 16, 64, 4
EPS = 1e-5
MASKED = 1e6
KD = DIM // P
KI = INNER // P
KE = EMB // P
NT = SEQ // P
CHUNK = 512
CT = CHUNK // P
CHUNKS = SEQ // CHUNK
XD = RANK + 2 * STATE
DMA = 16

VECTORS = [("L0_cond_ln_w", KD), ("L0_cond_ln_b", KD), ("L0_cond_bk", KD), ("L0_cond_ln2_w", KD), ("L0_cond_ln2_b", KD),
           ("L0_cond_b_emb", 2 * KD), ("L1_cond_b_ada", 2 * KD), ("L1_cond_gamma", KD), ("L1_cond_beta", KD),
           ("L1_cond_conv_b", KI), ("L1_cond_b_dt", KI), ("L1_cond_D_param", KI)]
COLUMN = {name: sum(n for _, n in VECTORS[:i]) for i, (name, _) in enumerate(VECTORS)}
VROWS = sum(n for _, n in VECTORS)

MM_FIRST = {"K": 0, "V": 8, "Q": 16}
MM_USES = 5 * NT
MM = {"y": 0, "K": 8, "V": 16, "Q": 24, "W": 32}
MM_LAST = {"y": 0, "W": 8}
TR_FIRST = {"z": 0, "q": 8, "k": 16}
TR_USES = 4 * NT
TR = {"z": 0, "y": 8, "q": 16, "k": 24}
TR_LAST = {"y": 0}
MM_RING, TR_RING = 4, 2

RING = 4
BLOCKS = STATE * KI
HALVES = BLOCKS // 4
W_IN_RING = 4
FOUR_BANKS = 60
assert FOUR_BANKS % 3 == 0 and (BLOCKS - FOUR_BANKS) % 4 == 0


def work_order(*stages):
    uses, seen = {}, {}
    for stage, n in stages:
        for _ in range(n):
            i = seen.get(stage, 0)
            uses[stage, i], seen[stage] = len(uses), i + 1
    return uses


FRONT = work_order(("h", KD), ("xm", KI), ("xd", 1), ("C", 1), ("dt", KI))
PREPARE = (("h", KD), ("xm", KI), ("z", 1), ("xd", 1), ("z", 2), ("C", 1), ("dt", 4), ("z", 2), ("dt", 4), ("z", 3))
FIRST_TURN = work_order(("init", KI), *PREPARE)
TURN = work_order(*[("y", 1), ("init", 1)] * KI, *PREPARE)
LAST_TURN = work_order(*[("y", 1), ("init", 1)] * KI, ("z", KI))
END = work_order(("y", KI))
CHUNK_ORDER = work_order(("h", KD), ("xm", KI), ("xd", 1), ("C", 1), ("dt", KI), ("init", KI), ("z", KI), ("y", KI))


def turn_place(b):
    first = len(FRONT) // 2
    if isinstance(b, int) and b == 0:
        return first, FIRST_TURN
    start = first + len(FIRST_TURN) // 2 + len(TURN) // 2 * (b - 1)
    return start, LAST_TURN if isinstance(b, int) and b == BATCH - 1 else TURN


class Shared:
    pass


def need(eng, semaphore, value):
    if not (isinstance(value, int) and value <= 0):
        eng.wait_ge(semaphore, value)


def mm_use(b, stage):
    if isinstance(b, int) and b == 0:
        return MM_FIRST[stage]
    base = MM_USES * b - 2 * NT
    return base + (MM_LAST if isinstance(b, int) and b == BATCH else MM)[stage]


def tr_use(b, stage):
    if isinstance(b, int) and b == 0:
        return TR_FIRST[stage]
    base = TR_USES * b - NT
    return base + (TR_LAST if isinstance(b, int) and b == BATCH else TR)[stage]


def cond_mamba_kernel(nc, a):
    g = Shared()

    def scratch(name, shape):
        return nc.dram_tensor(name, shape, F32).ap()

    g.x1_dram = scratch("x1_rows", [BATCH * SEQ, DIM])
    g.y_dram = scratch("y_rows", [SEQ, DIM])
    g.gate_dram = scratch("gate_rows", [BATCH, DIM])
    g.b_dram = scratch("b_rows", [BATCH * CHUNKS, STATE, CHUNK])

    with ExitStack() as whole:
        def sb(name, shape, dt=F32):
            return whole.enter_context(nc.sbuf_tensor(name, shape, dt))

        g.banks = [whole.enter_context(nc.psum_tensor(f"bank{i}", [P, 512], F32)) for i in range(8)]
        g.ident = sb("ident", [P, P])
        g.cols = sb("cols", [P, VROWS])
        g.mod_l0 = sb("mod_l0", [P, BATCH, 2 * KD + NT])
        g.mod_l1 = sb("mod_l1", [P, BATCH, 2 * KD])
        g.decay = sb("decay", [P, KI, STATE])
        g.taps = sb("taps", [P, KI, TAPS])
        g.idx_first = sb("idx_first", [P, NT], I32)
        g.idx_in = sb("idx_in", [P, NT], I32)
        g.idx_max = sb("idx_max", [1, 1], I32)
        g.mhalf = sb("mhalf", [P, NT])
        g.rows = sb("rows1", [P, CT, DIM])
        g.raw = sb("raw1", [P, CT, 6])
        g.mv = sb("mv1", [P, CT, 2])
        g.var = sb("var1", [P, CT])
        g.rs = sb("rs1", [P, CT])
        g.rows_loaded, g.stats, g.aggr, g.var_ready, g.rs_ready, g.normed = (
            whole.enter_context(nc.semaphore(n)) for n in ("rows1_loaded", "stats1", "aggr1", "var1_ready", "rs1_ready", "normed1"))

        with ExitStack() as weights:
            def sl(name, shape):
                return weights.enter_context(nc.sbuf_tensor(name, shape, F32))

            g.w_qkv = {"q": g.rows, "k": sl("w_k", [P, KD, DIM]), "v": sl("w_v", [P, KD, DIM])}
            g.w_out = sl("w_out", [P, KD, DIM])
            g.q_bias = sl("q_bias", [P, DIM])
            g.v_bias = sl("v_bias", [P, DIM])
            g.out_bias = sl("out_bias", [P, DIM])
            g.k_bias = sl("k_bias", [P, KD])
            g.cond_t = sl("cond_t", [P, KE, BATCH])
            g.att = sl("att", [P, KD, P])
            g.z = sl("z", [P, NT, DIM])
            g.x_raw = sl("x_raw", [P, NT, 6])
            g.x_mv = sl("x_mv", [P, NT, 2])
            g.x_var = sl("x_var", [P, NT])
            g.x_rs = sl("x_rs", [P, NT])
            prologue(nc, a, g)
            layer0(nc, a, g)
        layer1(nc, a, g)


def column(g, name, k):
    return g.cols[:, COLUMN[name] + k:COLUMN[name] + k + 1]


def moments(nc, src, raw, mv, var, stats, aggr, var_ready, n, apart):
    for t in range(NT):
        nc.vector.bn_stats(raw[:, t, :], src[:, t, :]).then_inc(stats, 1)
    need(nc.vector, stats, NT * n + NT)
    nc.vector.sem_inc(apart, 1)
    for t in range(NT):
        nc.vector.bn_aggr(mv[:, t, :], raw[:, t, :]).then_inc(aggr, 1)
    need(nc.vector, aggr, NT * n + NT)
    nc.vector.tensor_scalar(var[:, :], mv[:, :, 1], EPS, None, ALU.add).then_inc(var_ready, 1)


def normed(nc, src, mv, rs, ready):
    for t in range(NT):
        nc.vector.tensor_scalar(src[:, t, :], src[:, t, :], mv[:, t, 0:1], rs[:, t:t + 1], ALU.subtract, ALU.mult).then_inc(ready, 1)


def vector_wide(g, name, n):
    return g.cols[:, COLUMN[name]:COLUMN[name] + n].unsqueeze(2).to_broadcast([P, n, BATCH])


def rows_product(nc, g, bank, w):
    for k in range(KE):
        last = nc.tensor.matmul(g.banks[bank][0:BATCH, :], g.cond_t[:, k, :], w[:, k, :], start=(k == 0), stop=(k == KE - 1))
    return last


def rows_turned(nc, g, bank, rows):
    for m in range(2 * KD):
        last = nc.tensor.transpose(g.banks[bank][:, m * BATCH:(m + 1) * BATCH], rows[:, m * P:(m + 1) * P], g.ident[0:BATCH, 0:BATCH])
    return last


def turned_bias(nc, g, out, bank, name):
    return nc.vector.tensor_tensor(out, g.banks[bank][:, 0:2 * KD * BATCH].rearrange("p (m b) -> p m b", b=BATCH),
                                   vector_wide(g, name, 2 * KD), ALU.add)


def modulation(nc, g, out, rows, scale, shift, w, b, done, n):
    out = out.rearrange("p b i -> p i b")
    nc.vector.scalar_tensor_tensor(out[:, 0:KD, :], rows[:, scale:scale + KD, :], 1.0, vector_wide(g, w, KD), ALU.add, ALU.mult).then_inc(done, 1)
    nc.vector.scalar_tensor_tensor(out[:, KD:2 * KD, :], rows[:, scale:scale + KD, :], 1.0, vector_wide(g, b, KD), ALU.add, ALU.mult).then_inc(done, 1)
    nc.vector.wait_ge(done, n + 2)
    nc.vector.tensor_tensor(out[:, KD:2 * KD, :], out[:, KD:2 * KD, :], rows[:, shift:shift + KD, :], ALU.add).then_inc(done, 1)


def gather_rows(nc, g, x1, c):
    for t in range(CT):
        nc.gpsimd.indirect_dma_start(g.rows[:, t, :], None, x1, bass.IndirectOffsetOnAxis(g.idx_in[:, c * CT + t:c * CT + t + 1], axis=0)).then_inc(g.rows_loaded, DMA)


def rows_rsqrt(nc, g, it):
    need(nc.gpsimd, g.var_ready, it + 1)
    nc.gpsimd.tensor_tensor(g.rs[:, :], g.var[:, :], g.mhalf[:, 0:CT], ALU.pow).then_inc(g.rs_ready, 1)


def rows_moments(nc, g, it, apart):
    need(nc.vector, g.rows_loaded, CT * DMA * (it + 1))
    for t in range(CT):
        nc.vector.bn_stats(g.raw[:, t, :], g.rows[:, t, :]).then_inc(g.stats, 1)
    need(nc.vector, g.stats, CT * it + CT)
    nc.vector.sem_inc(apart, 1)
    for t in range(CT):
        nc.vector.bn_aggr(g.mv[:, t, :], g.raw[:, t, :]).then_inc(g.aggr, 1)
    need(nc.vector, g.aggr, CT * it + CT)
    nc.vector.tensor_scalar(g.var[:, :], g.mv[:, :, 1], EPS, None, ALU.add).then_inc(g.var_ready, 1)


def rows_normed(nc, g, it):
    need(nc.vector, g.rs_ready, it + 1)
    for t in range(CT):
        nc.vector.tensor_scalar(g.rows[:, t, :], g.rows[:, t, :], g.mv[:, t, 0:1], g.rs[:, t:t + 1], ALU.subtract, ALU.mult).then_inc(g.normed, 1)


def prologue(nc, a, g):
    banks, ident, cols = g.banks, g.ident, g.cols

    with ExitStack() as ctx:
        def sb(name, shape, dt=F32):
            return ctx.enter_context(nc.sbuf_tensor(name, shape, dt))

        def sem(name):
            return ctx.enter_context(nc.semaphore(name))

        rows = sb("rows", [VROWS, P])
        idx_row = sb("idx_row", [1, SEQ], I32)
        mask_in = sb("mask_in", [BATCH * NT, P])
        cond = sb("cond", [BATCH, EMB])
        cond_silu = sb("cond_silu", [BATCH, EMB])
        w_emb = sb("w_emb", [P, KE, 2 * DIM])
        ln_b_wide = sb("ln_b_wide", [P, KD, P])
        emb_rows = sb("emb_rows", [BATCH, 2 * DIM])
        emb = sb("emb", [P, 2 * KD, BATCH])
        a_raw = sb("a_raw", [P, KI, STATE])
        a_exp = sb("a_exp", [P, KI, STATE])

        rows_loaded = sem("rows_loaded")
        small_loaded = sem("small_loaded")
        cond_loaded = sem("cond_loaded")
        qkv_loaded = sem("qkv_loaded")
        emb_loaded = [sem(f"emb_loaded{i}") for i in range(2)]
        ident_zero = sem("ident_zero")
        ident_ready = sem("ident_ready")
        silu_ready = sem("silu_ready")
        decay_exp = sem("decay_exp")
        turned = sem("turned")
        cols_ready = sem("cols_ready")
        cond_ready = sem("cond_ready")
        wide_ready = sem("wide_ready")
        bias_ready = sem("bias_ready")
        mods_ready = sem("mods_ready")
        rows_kept = sem("rows_kept")
        x0_loaded, x0_stats, x0_aggr, x0_var_ready, x0_rs_ready, x0_normed, x0_apart = (
            sem(n) for n in ("x0_loaded", "x0_stats", "x0_aggr", "x0_var_ready", "x0_rs_ready", "x0_normed", "x0_apart"))
        folded = sem("folded")
        block = ctx.enter_context(nc.Block())

        @block.sync
        def _(sp):
            for name, n in VECTORS:
                at = COLUMN[name]
                sp.dma_start(rows[at:at + n, :], a[name].rearrange("(k p) -> k p", p=P)[0:n, :]).then_inc(rows_loaded, DMA)
            sp.dma_start(mask_in[:, :], a["mask_BxSx1_fk1"].rearrange("b (t p) o -> (b t) (p o)", p=P)).then_inc(rows_loaded, DMA)
            sp.dma_start(cond[:, :], a["cond_2048"]).then_inc(cond_loaded, DMA)
            for n in "qvk":
                sp.dma_start(g.w_qkv[n][:, :, :], a[f"L0_cond_W{n}"].rearrange("(k p) n -> p k n", p=P)).then_inc(qkv_loaded, DMA)
            sp.dma_start(g.z[:, :, :], a["x"].rearrange("b (t p) d -> b p t d", p=P)[0]).then_inc(x0_loaded, DMA)
            for half in range(2):
                at = slice(half * DIM, (half + 1) * DIM)
                sp.dma_start(w_emb[:, :, at], a["L0_cond_W_emb"].rearrange("(k p) n -> p k n", p=P)[:, :, at]).then_inc(emb_loaded[half], DMA)

        @block.scalar
        def _(act):
            act.dma_start(g.q_bias[:, :], a["L0_cond_bq"].partition_broadcast(P)).then_inc(small_loaded, DMA)
            act.dma_start(g.v_bias[:, :], a["L0_cond_bv"].partition_broadcast(P)).then_inc(small_loaded, DMA)
            act.dma_start(g.out_bias[:, :], a["L0_cond_b_out"].partition_broadcast(P)).then_inc(small_loaded, DMA)
            act.dma_start(a_raw[:, :, :], a["L1_cond_A_log"].rearrange("(k p) s -> p k s", p=P)).then_inc(small_loaded, DMA)
            act.dma_start(g.taps[:, :, :], a["L1_cond_conv_w"].rearrange("(k p) o t -> p k (o t)", p=P)).then_inc(small_loaded, DMA)
            act.dma_start(g.idx_first[:, :], a["itok_S_0_1023"].rearrange("(t p) -> p t", p=P), allow_slow_non_contiguous=True).then_inc(small_loaded, DMA)
            act.dma_start(idx_row[:, :], a["itok_S_0_1023"].rearrange("(o s) -> o s", o=1)).then_inc(small_loaded, DMA)
            act.wait_ge(cond_loaded, DMA)
            nc.scalar.activation(cond_silu[:, :], cond[:, :], ACT.Silu).then_inc(silu_ready, 1)
            act.wait_ge(small_loaded, 7 * DMA)
            nc.scalar.activation(a_exp[:, :, :], a_raw[:, :, :], ACT.Exp).then_inc(decay_exp, 1)
            for half in range(2):
                act.wait_ge(mods_ready, half + 1)
                nc.scalar.copy(emb_rows[:, half * DIM:(half + 1) * DIM], banks[6 + half][0:BATCH, :]).then_inc(rows_kept, 1)

        @block.gpsimd
        def _(pool):
            nc.gpsimd.memset(ident[:, :], 0.0).then_inc(ident_zero, 1)
            nc.gpsimd.memset(g.mhalf[:, :], -0.5).then_inc(ident_zero, 1)
            pool.wait_ge(ident_zero, 1)
            nc.gpsimd.affine_select(out=ident[:, :], in_=ident[:, :], compare_op=ALU.not_equal, fill=1.0, base=0,
                                    pattern=[[-1, P]], channel_multiplier=1).then_inc(ident_ready, 1)
            pool.wait_ge(ident_zero, 2)
            pool.wait_ge(x0_var_ready, 1)
            nc.gpsimd.tensor_tensor(g.x_rs[:, :], g.x_var[:, :], g.mhalf[:, :], ALU.pow).then_inc(x0_rs_ready, 1)

        @block.tensor
        def _(pe):
            pe.wait_ge(ident_ready, 1)
            pe.wait_ge(rows_loaded, (len(VECTORS) + 1) * DMA)
            nc.tensor.transpose(banks[0][:, 0:VROWS], rows[:, :], ident[0:VROWS, 0:VROWS]).then_inc(turned, 1)
            nc.tensor.transpose(banks[1][:, 0:BATCH * NT], mask_in[:, :], ident[0:BATCH * NT, 0:BATCH * NT]).then_inc(turned, 1)
            pe.wait_ge(silu_ready, 1)
            for k in range(KE):
                last = nc.tensor.transpose(banks[2][:, k * BATCH:(k + 1) * BATCH], cond_silu[:, k * P:(k + 1) * P],
                                           ident[0:BATCH, 0:BATCH])
            last.then_inc(turned, 1)
            pe.wait_ge(wide_ready, 1)
            pe.wait_ge(qkv_loaded, 3 * DMA)
            for bank, n in ((3, "q"), (4, "v")):
                for k in range(KD):
                    last = nc.tensor.matmul(banks[bank][:, :], ln_b_wide[:, k, :], g.w_qkv[n][:, k, :], start=(k == 0), stop=(k == KD - 1))
            for i in range(KD):
                for k in range(KD):
                    last = nc.tensor.matmul(banks[5][:, i:i + 1], g.w_qkv["k"][:, k, i * P:(i + 1) * P], column(g, "L0_cond_ln_b", k),
                                            start=(k == 0), stop=(k == KD - 1))
            last.then_inc(bias_ready, 1)
            pe.wait_ge(cond_ready, 1)
            for half in range(2):
                pe.wait_ge(emb_loaded[half], DMA)
                rows_product(nc, g, 6 + half, w_emb[:, :, half * DIM:(half + 1) * DIM]).then_inc(mods_ready, 1)
            pe.wait_ge(rows_kept, 2)
            rows_turned(nc, g, 6, emb_rows).then_inc(mods_ready, 1)

        @block.vector
        def _(dve):
            nc.vector.memset(g.att[:, :, :], 0.0).then_inc(folded, 1)
            dve.wait_ge(turned, 2)
            nc.vector.tensor_copy(cols[:, :], banks[0][:, 0:VROWS]).then_inc(cols_ready, 1)
            nc.vector.tensor_copy(g.mod_l0[:, :, 2 * KD:], banks[1][:, 0:BATCH * NT].rearrange("p (b t) -> p b t", b=BATCH)).then_inc(cols_ready, 1)
            dve.wait_ge(cols_ready, 2)
            nc.vector.tensor_copy(ln_b_wide[:, :, :], cols[:, COLUMN["L0_cond_ln_b"]:COLUMN["L0_cond_ln_b"] + KD].unsqueeze(2).to_broadcast([P, KD, P])).then_inc(wide_ready, 1)
            dve.wait_ge(turned, 3)
            nc.vector.tensor_copy(g.cond_t[:, :, :], banks[2][:, 0:KE * BATCH].rearrange("p (k b) -> p k b", k=KE)).then_inc(cond_ready, 1)
            dve.wait_ge(small_loaded, 7 * DMA)
            dve.wait_ge(decay_exp, 1)
            nc.vector.tensor_scalar(g.decay[:, :, :], a_exp[:, :, :], -1.0, None, ALU.mult).then_inc(folded, 1)
            nc.vector.tensor_reduce(g.idx_max[:, :], idx_row[:, :], AX.X, ALU.max).then_inc(folded, 1)
            nc.vector.tensor_copy(g.idx_in[:, :], g.idx_first[:, :]).then_inc(folded, 1)
            dve.wait_ge(bias_ready, 1)
            nc.vector.tensor_tensor(g.q_bias[:, :], banks[3][:, :], g.q_bias[:, :], ALU.add).then_inc(folded, 1)
            nc.vector.tensor_tensor(g.v_bias[:, :], banks[4][:, :], g.v_bias[:, :], ALU.add).then_inc(folded, 1)
            nc.vector.tensor_tensor(g.k_bias[:, :], banks[5][:, 0:KD], cols[:, COLUMN["L0_cond_bk"]:COLUMN["L0_cond_bk"] + KD], ALU.add).then_inc(folded, 1)
            for n in "qkv":
                for k in range(KD):
                    last = nc.vector.tensor_scalar(g.w_qkv[n][:, k, :], g.w_qkv[n][:, k, :], column(g, "L0_cond_ln_w", k), None, ALU.mult)
                last.then_inc(folded, 1)
            dve.wait_ge(x0_loaded, DMA)
            moments(nc, g.z, g.x_raw, g.x_mv, g.x_var, x0_stats, x0_aggr, x0_var_ready, 0, x0_apart)
            dve.wait_ge(x0_rs_ready, 1)
            normed(nc, g.z, g.x_mv, g.x_rs, x0_normed)
            dve.wait_ge(mods_ready, 3)
            turned_bias(nc, g, emb[:, :, :], 6, "L0_cond_b_emb").then_inc(folded, 1)
            dve.wait_ge(folded, 11)
            modulation(nc, g, g.mod_l0[:, :, 0:2 * KD], emb, 0, KD, "L0_cond_ln2_w", "L0_cond_ln2_b", folded, 11)
            dve.wait_ge(folded, 14)
            dve.wait_ge(x0_normed, NT)


def layer0(nc, a, g):
    banks, ident = g.banks, g.ident
    x_rows = a["x"].rearrange("b (t p) d -> b p t d", p=P)
    x1_rows = g.x1_dram.rearrange("(b t p) d -> b p t d", p=P, t=NT)
    mask_rows = a["mask_BxSx1_fk1"].rearrange("b s o -> b (s o)")

    with ExitStack() as ctx:
        def sb(name, shape):
            return ctx.enter_context(nc.sbuf_tensor(name, shape, F32))

        def sem(name):
            return ctx.enter_context(nc.semaphore(name))

        z, x_raw, x_mv, x_var, x_rs = g.z, g.x_raw, g.x_mv, g.x_var, g.x_rs
        z_t = sb("z_t", [P, KD, SEQ])
        k_t = sb("k_t", [P, KD, SEQ])
        k_exp = sb("k_exp", [P, NT, DIM])
        values = sb("values", [P, NT, DIM])
        qy = sb("qy", [P, NT, DIM])
        q_t = sb("q_t", [P, KD, SEQ])
        h_t = sb("h_t", [P, KD, SEQ])
        res = sb("res", [P, NT, DIM])
        mask_add = sb("mask_add", [P, SEQ])
        mod_cur = sb("mod_cur", [P, 2 * KD])
        mask_cur = sb("mask_cur", [P, NT])
        y_raw = sb("y_raw", [P, NT, 6])
        y_mv = sb("y_mv", [P, NT, 2])
        y_var = sb("y_var", [P, NT])
        y_rs = sb("y_rs", [P, NT])
        k_top = sb("k_top", [P, KD])
        k_sum = sb("k_sum", [P, KD])
        k_inv = sb("k_inv", [P, KD])
        q_top = sb("q_top", [P, NT, HEADS])
        q_sum = sb("q_sum", [P, NT, HEADS])
        q_inv = sb("q_inv", [P, NT, HEADS])
        w_ada_third = [z[:, :, :], z_t[:, :, :].rearrange("p k (h n) -> p (k h) n", n=DIM), values[:, :, :]]
        ada_rows = k_t[0:BATCH, 0, 0:2 * DIM]
        gate, gate_bias = k_t[0:BATCH, 1, 0:DIM], k_t[0:BATCH, 1, DIM:2 * DIM]
        ada = k_t[:, 2, 0:2 * KD * BATCH].rearrange("p (m b) -> p m b", b=BATCH)
        w_ada_rows = a["L1_cond_W_ada"].rearrange("(k p) n -> p k n", p=P)

        x_loaded, res_loaded, mask_loaded, x1_stored = (sem(n) for n in ("x_loaded", "res_loaded", "mask_loaded", "x1_stored"))
        x_stats, x_aggr, x_var_ready, x_rs_ready, z_ready = (sem(n) for n in ("x_stats", "x_aggr", "x_var_ready", "x_rs_ready", "z_ready"))
        y_stats, y_aggr, y_var_ready, y_rs_ready, y_normed = (sem(n) for n in ("y_stats", "y_aggr", "y_var_ready", "y_rs_ready", "y_normed"))
        mm_ready, mm_empty, tr_ready, tr_empty = (sem(n) for n in ("mm_ready", "mm_empty", "tr_ready", "tr_empty"))
        mod_ready, mask_cur_ready, mask_ready = (sem(n) for n in ("mod_ready", "mask_cur_ready", "mask_ready"))
        k_top_ready, k_exp_ready, k_inv_ready = (sem(n) for n in ("k_top_ready", "k_exp_ready", "k_inv_ready"))
        q_top_ready, q_shifted, q_exp_ready, q_summed, q_inv_ready = (sem(n) for n in ("q_top_ready", "q_shifted", "q_exp_ready", "q_summed", "q_inv_ready"))
        kv_ready, att_ready, res_ready = (sem(n) for n in ("kv_ready", "att_ready", "res_ready"))
        started, passed = sem("started"), sem("passed")
        w_out_loaded, gate_bias_loaded, gate_stored = (sem(n) for n in ("w_out_loaded", "gate_bias_loaded", "gate_stored"))
        ada_loaded = [sem(f"ada_loaded{i}") for i in range(3)]
        ada_ready = sem("ada_ready")
        ada_kept = sem("ada_kept")
        ada_folded = sem("ada_folded")
        block = ctx.enter_context(nc.Block())

        def batch(ap, b):
            names = "p t d"[:2 * (len(ap.shape) - 1) - 1] if len(ap.shape) == 4 else "t"
            if names == "t":
                return ap[bass.ds(b, 1)]
            return ap[bass.ds(b, 1)].rearrange("o p t d -> (o p) t d")

        def iterations(eng, body):
            body(0, False, True, True)
            with eng.Fori(1, BATCH - 1) as b:
                body(b, True, True, True)
            body(BATCH - 1, True, True, False)
            body(BATCH, True, False, False)

        @block.sync
        def _(sp):
            def load_ada(i):
                sp.dma_start(w_ada_third[i], w_ada_rows[:, :, i * DIM:(i + 1) * DIM]).then_inc(ada_loaded[i], DMA)

            def body(b, prev, cur, more):
                if prev:
                    sp.dma_start(res[:, :, :], batch(x_rows, b - 1)).then_inc(res_loaded, DMA)
                if not cur:
                    sp.wait_ge(tr_ready, tr_use(b - 1, "k") + NT)
                    sp.wait_ge(kv_ready, b)
                    load_ada(2)
                    sp.dma_start(gate_bias, a["L1_cond_b_ada"][2 * DIM:3 * DIM].partition_broadcast(BATCH)).then_inc(gate_bias_loaded, DMA)
                if cur:
                    if not (isinstance(b, int) and b == 0):
                        need(sp, mm_empty, mm_use(b, "y") - 2 * NT)
                    sp.sem_inc(passed, 1)
                    sp.dma_start(mask_add[:, :], mask_rows[bass.ds(b, 1)].rearrange("o s -> (o s)").partition_broadcast(P)).then_inc(mask_loaded, DMA)
                if more:
                    need(sp, tr_ready, tr_use(b, "z") + NT)
                    sp.sem_inc(passed, 1)
                    sp.dma_start(z[:, :, :], batch(x_rows, b + 1)).then_inc(x_loaded, DMA)
                if cur and not more:
                    sp.wait_ge(tr_ready, tr_use(b, "z") + NT)
                    load_ada(0)
                    sp.wait_ge(mm_ready, mm_use(b, "Q") + NT)
                    load_ada(1)
                if not cur:
                    sp.wait_ge(ada_folded, 5)
                    sp.dma_start(g.gate_dram, gate).then_inc(gate_stored, DMA)
                    for t in range(0, NT, 2):
                        sp.wait_ge(mm_empty, mm_use(b, "W") + t + 2)
                        sp.dma_start(batch(x1_rows, b - 1)[:, t:t + 2, :], res[:, t:t + 2, :]).then_inc(x1_stored, DMA)
                    sp.wait_ge(gate_stored, DMA)
                    sp.wait_ge(x1_stored, DMA * (b - 1 + NT // 2))
                elif prev:
                    need(sp, mm_empty, mm_use(b, "W") + NT)
                    sp.sem_inc(passed, 1)
                    sp.dma_start(batch(x1_rows, b - 1), res[:, :, :]).then_inc(x1_stored, DMA)
                    need(sp, x1_stored, DMA * b)
                    sp.sem_inc(passed, 1)

            sp.dma_start(g.w_out[:, :, :], a["L0_cond_W_out"].rearrange("(k p) n -> p k n", p=P)).then_inc(w_out_loaded, DMA)
            iterations(sp, body)

        @block.tensor
        def _(pe):
            def product(use, stationary, moving, blocks):
                n, at = use
                need(pe, mm_empty, n + at - (MM_RING - 1))
                out = banks[at % MM_RING]
                for k in range(blocks):
                    last = nc.tensor.matmul(out[:, :], stationary(k), moving(k), start=(k == 0), stop=(k == blocks - 1))
                last.then_inc(mm_ready, 1)

            def turn(n, at, sources):
                need(pe, tr_empty, n + at - (TR_RING - 1))
                out = banks[MM_RING + at % TR_RING]
                for j, source in enumerate(sources):
                    last = nc.tensor.transpose(out[:, j * P:(j + 1) * P], source, ident[:, :])
                last.then_inc(tr_ready, 1)

            def body(b, prev, cur, more):
                if prev:
                    need(pe, tr_empty, tr_use(b - 1, "q") + NT)
                    need(pe, att_ready, 2 * b)
                    n = mm_use(b, "y")
                    for t in range(NT):
                        need(pe, mm_empty, n + t - (MM_RING - 1))
                        for i in range(KD):
                            last = nc.tensor.matmul(banks[t % MM_RING][:, i * P:(i + 1) * P], q_t[:, i, t * P:(t + 1) * P], g.att[:, i, :],
                                                    start=True, stop=True)
                        last.then_inc(mm_ready, 1)
                if cur:
                    n = tr_use(b, "z")
                    for half in range(2):
                        need(pe, z_ready, NT * (b - 1) + 4 * half + 4)
                        for i in range(KD):
                            turn(n, 4 * half + i, [z[:, 4 * half + j, i * P:(i + 1) * P] for j in range(4)])
                    need(pe, tr_empty, n + NT)
                    n = mm_use(b, "K")
                    for i in range(KD):
                        for half in range(2):
                            product((n, 2 * i + half), lambda k: g.w_qkv["k"][:, k, i * P:(i + 1) * P],
                                    lambda k: z_t[:, k, half * 512:(half + 1) * 512], KD)
                    n = mm_use(b, "V")
                    for t in range(NT):
                        product((n, t), lambda k: z_t[:, k, t * P:(t + 1) * P], lambda k: g.w_qkv["v"][:, k, :], KD)
                if not cur:
                    for i in range(2):
                        pe.wait_ge(ada_loaded[i], DMA)
                        rows_product(nc, g, 7 - i, w_ada_third[i]).then_inc(ada_ready, 1)
                if prev:
                    n = tr_use(b, "y")
                    for half in range(2):
                        need(pe, y_normed, NT * (b - 1) + 4 * half + 4)
                        for i in range(KD):
                            turn(n, 4 * half + i, [qy[:, 4 * half + j, i * P:(i + 1) * P] for j in range(4)])
                if cur:
                    n = mm_use(b, "Q")
                    for t in range(NT):
                        product((n, t), lambda k: z_t[:, k, t * P:(t + 1) * P], lambda k: g.w_qkv["q"][:, k, :], KD)
                if not cur:
                    pe.wait_ge(ada_kept, 2)
                    rows_turned(nc, g, 7, ada_rows).then_inc(ada_ready, 1)
                    pe.wait_ge(ada_loaded[2], DMA)
                    rows_product(nc, g, 6, w_ada_third[2]).then_inc(ada_ready, 1)
                if prev:
                    need(pe, tr_empty, tr_use(b, "y") + NT)
                    pe.wait_ge(w_out_loaded, DMA)
                    n = mm_use(b, "W")
                    for t in range(NT):
                        product((n, t), lambda k: h_t[:, k, t * P:(t + 1) * P], lambda k: g.w_out[:, k, :], KD)
                if cur:
                    n = tr_use(b, "q")
                    for half in range(2):
                        need(pe, q_exp_ready, NT * b + 4 * half + 4)
                        for i in range(KD):
                            turn(n, 4 * half + i, [qy[:, 4 * half + j, i * P:(i + 1) * P] for j in range(4)])
                    n = tr_use(b, "k")
                    need(pe, k_exp_ready, KD * b + KD)
                    for t in range(NT):
                        turn(n, t, [k_t[:, i, t * P:(t + 1) * P] for i in range(KD)])
                    need(pe, tr_empty, n + NT)
                    need(pe, att_ready, 2 * b)
                    for i in range(KD):
                        for t in range(NT):
                            last = nc.tensor.matmul(banks[6][:, i * P:(i + 1) * P], k_exp[:, t, i * P:(i + 1) * P], values[:, t, i * P:(i + 1) * P],
                                                    start=(t == 0), stop=(t == NT - 1))
                    last.then_inc(kv_ready, 1)

            iterations(pe, body)

        @block.scalar
        def _(act):
            def bank(at):
                return banks[MM_RING + at % TR_RING]

            def body(b, prev, cur, more):
                if cur:
                    n = tr_use(b, "z")
                    for half in range(2):
                        for i in range(KD):
                            need(act, tr_ready, n + 4 * half + i + 1)
                            nc.scalar.copy(z_t[:, i, half * 512:(half + 1) * 512], bank(i)[:, :]).then_inc(tr_empty, 1)
                    for i in range(KD):
                        need(act, k_top_ready, KD * b + i + 1)
                        nc.scalar.activation(k_t[:, i, :], k_t[:, i, :], ACT.Exp, bias=k_top[:, i:i + 1],
                                             accum_out=k_sum[:, i:i + 1]).then_inc(k_exp_ready, 1)
                if not cur:
                    for i in range(2):
                        act.wait_ge(ada_ready, i + 1)
                        nc.scalar.copy(ada_rows[:, i * DIM:(i + 1) * DIM], banks[7 - i][0:BATCH, :]).then_inc(ada_kept, 1)
                if prev:
                    need(act, mod_ready, b)
                    n = tr_use(b, "y")
                    for half in range(2):
                        for i in range(KD):
                            need(act, tr_ready, n + 4 * half + i + 1)
                            nc.scalar.activation(h_t[:, i, half * 512:(half + 1) * 512], bank(i)[:, :], ACT.Silu, scale=mod_cur[:, i:i + 1],
                                                 bias=mod_cur[:, KD + i:KD + i + 1]).then_inc(tr_empty, 1)
                if cur:
                    for t in range(NT):
                        need(act, q_shifted, NT * b + t + 1)
                        nc.scalar.activation(qy[:, t, :], qy[:, t, :], ACT.Exp).then_inc(q_exp_ready, 1)
                    n = tr_use(b, "q")
                    for half in range(2):
                        for i in range(KD):
                            need(act, tr_ready, n + 4 * half + i + 1)
                            nc.scalar.copy(q_t[:, i, half * 512:(half + 1) * 512], bank(i)[:, :]).then_inc(tr_empty, 1)
                    n = tr_use(b, "k")
                    need(act, mask_cur_ready, b + 1)
                    for t in range(NT):
                        need(act, tr_ready, n + t + 1)
                        nc.scalar.mul(k_exp[:, t, :], bank(t)[:, :], mask_cur[:, t:t + 1]).then_inc(tr_empty, 1)

            iterations(act, body)

        @block.gpsimd
        def _(pool):
            def body(b, prev, cur, more):
                if not cur:
                    pool.wait_ge(mm_ready, mm_use(b - 1, "Q") + NT)
                    pool.wait_ge(x1_stored, DMA)
                    gather_rows(nc, g, g.x1_dram[0:SEQ, :], 0)
                if prev:
                    need(pool, y_var_ready, b)
                    nc.gpsimd.tensor_tensor(y_rs[:, :], y_var[:, :], g.mhalf[:, :], ALU.pow).then_inc(y_rs_ready, 1)
                    need(pool, res_loaded, DMA * b)
                    for t in range(NT):
                        nc.gpsimd.tensor_tensor(res[:, t, :], res[:, t, :], g.out_bias[:, :], ALU.add).then_inc(res_ready, 1)
                if not cur:
                    rows_rsqrt(nc, g, 0)
                if more:
                    need(pool, x_var_ready, b + 1)
                    nc.gpsimd.tensor_tensor(x_rs[:, :], x_var[:, :], g.mhalf[:, :], ALU.pow).then_inc(x_rs_ready, 1)
                if cur:
                    for t in range(NT):
                        need(pool, q_top_ready, NT * b + t + 1)
                        heads = qy[:, t, :].rearrange("p (h d) -> p h d", h=HEADS)
                        nc.gpsimd.tensor_tensor(heads, heads, q_top[:, t, :].unsqueeze(2).to_broadcast([P, HEADS, HEAD]), ALU.add).then_inc(q_shifted, 1)

            iterations(pool, body)

        @block.vector
        def _(dve):
            def body(b, prev, cur, more):
                if prev:
                    need(dve, tr_empty, tr_use(b, "y") - 8)
                    dve.wait_ge(started, 1)
                    nc.vector.tensor_copy(mod_cur[:, :], g.mod_l0[:, bass.ds(b - 1, 1), 0:2 * KD].rearrange("p o i -> p (o i)")).then_inc(mod_ready, 1)
                if cur:
                    if not (isinstance(b, int) and b == 0):
                        need(dve, tr_empty, tr_use(b, "z"))
                    dve.wait_ge(started, 1)
                    nc.vector.tensor_copy(mask_cur[:, :], g.mod_l0[:, bass.ds(b, 1), 2 * KD:].rearrange("p o i -> p (o i)")).then_inc(mask_cur_ready, 1)
                if prev:
                    n = mm_use(b, "y")
                    need(dve, q_inv_ready, b)
                    for t in range(NT):
                        need(dve, mm_ready, n + t + 1)
                        nc.vector.tensor_tensor(qy[:, t, :].rearrange("p (h d) -> p h d", h=HEADS),
                                                banks[t % MM_RING][:, :].rearrange("p (h d) -> p h d", h=HEADS),
                                                q_inv[:, t, :].unsqueeze(2).to_broadcast([P, HEADS, HEAD]), ALU.mult).then_inc(mm_empty, 1)
                    need(dve, mm_empty, n + NT)
                    moments(nc, qy, y_raw, y_mv, y_var, y_stats, y_aggr, y_var_ready, b - 1, started)
                if cur:
                    need(dve, mask_loaded, DMA * (b + 1))
                    nc.vector.tensor_scalar(mask_add[:, :], mask_add[:, :], 1.0, MASKED, ALU.subtract, ALU.mult).then_inc(mask_ready, 1)
                    need(dve, mask_ready, b + 1)
                    n = mm_use(b, "K")
                    for i in range(KD):
                        for half in range(2):
                            need(dve, mm_ready, n + 2 * i + half + 1)
                            nc.vector.scalar_tensor_tensor(k_t[:, i, half * 512:(half + 1) * 512], banks[(2 * i + half) % MM_RING][:, :], g.k_bias[:, i:i + 1],
                                                           mask_add[:, half * 512:(half + 1) * 512], ALU.add, ALU.add).then_inc(mm_empty, 1)
                        need(dve, mm_empty, n + 2 * i + 2)
                        nc.vector.tensor_reduce(k_top[:, i:i + 1], k_t[:, i, :], AX.X, ALU.max, negate=True).then_inc(k_top_ready, 1)
                if prev:
                    need(dve, y_rs_ready, b)
                    normed(nc, qy, y_mv, y_rs, y_normed)
                if not cur:
                    rows_moments(nc, g, 0, started)
                    dve.wait_ge(ada_ready, 3)
                    turned_bias(nc, g, ada, 7, "L1_cond_b_ada").then_inc(ada_folded, 1)
                    dve.wait_ge(ada_folded, 1)
                    modulation(nc, g, g.mod_l1[:, :, :], ada, KD, 0, "L1_cond_gamma", "L1_cond_beta", ada_folded, 1)
                    dve.wait_ge(ada_ready, 4)
                    dve.wait_ge(gate_bias_loaded, DMA)
                    nc.vector.tensor_tensor(gate, banks[6][0:BATCH, :], gate_bias, ALU.add).then_inc(ada_folded, 1)
                    dve.wait_ge(ada_folded, 5)
                    rows_normed(nc, g, 0)
                if cur:
                    n = mm_use(b, "V")
                    for t in range(NT):
                        need(dve, mm_ready, n + t + 1)
                        nc.vector.tensor_tensor(values[:, t, :], banks[t % MM_RING][:, :], g.v_bias[:, :], ALU.add).then_inc(mm_empty, 1)
                if more:
                    need(dve, x_loaded, DMA * (b + 1))
                    moments(nc, z, x_raw, x_mv, x_var, x_stats, x_aggr, x_var_ready, b, started)
                if cur:
                    n = mm_use(b, "Q")
                    for t in range(NT):
                        need(dve, mm_ready, n + t + 1)
                        nc.vector.tensor_tensor(qy[:, t, :], banks[t % MM_RING][:, :], g.q_bias[:, :], ALU.add).then_inc(mm_empty, 1)
                        need(dve, mm_empty, n + t + 1)
                        nc.vector.tensor_reduce(q_top[:, t, :], qy[:, t, :].rearrange("p (h d) -> p h d", h=HEADS), AX.X, ALU.max,
                                                negate=True).then_inc(q_top_ready, 1)
                    need(dve, k_exp_ready, KD * b + KD)
                    nc.vector.reciprocal(k_inv[:, :], k_sum[:, :]).then_inc(k_inv_ready, 1)
                if more:
                    need(dve, x_rs_ready, b + 1)
                    normed(nc, z, x_mv, x_rs, z_ready)
                if prev:
                    n = mm_use(b, "W")
                    for t in range(NT):
                        need(dve, mm_ready, n + t + 1)
                        need(dve, res_ready, NT * (b - 1) + t + 1)
                        nc.vector.tensor_tensor(res[:, t, :], banks[t % MM_RING][:, :], res[:, t, :], ALU.add).then_inc(mm_empty, 1)
                if cur:
                    for t in range(NT):
                        need(dve, q_exp_ready, NT * b + t + 1)
                        nc.vector.tensor_reduce(q_sum[:, t, :], qy[:, t, :].rearrange("p (h d) -> p h d", h=HEADS), AX.X, ALU.add).then_inc(q_summed, 1)
                    need(dve, q_summed, NT * b + NT)
                    nc.vector.reciprocal(q_inv[:, :, :], q_sum[:, :, :]).then_inc(q_inv_ready, 1)
                    need(dve, kv_ready, b + 1)
                    need(dve, k_inv_ready, b + 1)
                    for h in range(2):
                        at = slice(h * HEAD, (h + 1) * HEAD)
                        nc.vector.tensor_tensor(g.att[at, :, at], banks[6][at, :].rearrange("p (i d) -> p i d", i=KD)[:, :, at],
                                                k_inv[at, :].unsqueeze(2).to_broadcast([HEAD, KD, HEAD]), ALU.mult).then_inc(att_ready, 1)

            nc.vector.memset(k_sum[:, :], 0.0).then_inc(started, 1)
            iterations(dve, body)


def layer1(nc, a, g):
    banks, ident = g.banks, g.ident
    x1_rows = g.x1_dram.rearrange("(b t p) d -> b t p d", p=P, t=NT)
    y_rows = g.y_dram.rearrange("(t p) d -> t p d", p=P)
    out_rows = a["out"].rearrange("b (t p) d -> b t p d", p=P)
    w_in_dram = a["L1_cond_W_in"].rearrange("(k p) n -> p k n", p=P)

    with ExitStack() as ctx:
        def sb(name, shape):
            return ctx.enter_context(nc.sbuf_tensor(name, shape, F32))

        def sem(name):
            return ctx.enter_context(nc.semaphore(name))

        w_xp = sb("w_xp", [P, KI, XD])
        w_dt = sb("w_dt", [RANK, INNER])
        w_y = sb("w_y", [P, KI, DIM])
        w_in = sb("w_in", [P, W_IN_RING, KD, P])
        d_diag = sb("d_diag", [P, KI, P])
        h_t = sb("h1_t", [P, 2, KD, CHUNK])
        xd = sb("xd", [XD, CHUNK])
        xm = sb("xm", [P, KI, CHUNK])
        zs = sb("zs", [P, KI, CHUNK])
        dt = sb("dt", [P, 2, KI, CHUNK])
        u = sb("u", [P, KI, CHUNK])
        acc = sb("acc", [P, CT, INNER])
        hs = sb("hs", [P, RING, 4, CHUNK])
        b_wide = sb("b_wide", [P, 2, CHUNK])
        c_t = sb("c_t", [P, 2, CT, STATE])
        gate = sb("gate_wide", [P, DIM])
        fin = sb("fin", [P, 2, DIM])
        mod_cur = sb("mod1_cur", [P, 2 * KD])
        halo = sb("halo", [P, KI, TAPS - 1])
        carry = sb("carry", [P, KI, STATE])
        state_banks, out_bank, work_banks = banks[0:2], banks[2], banks[6:8]

        weights_loaded, w_y_loaded, d_ready = sem("weights1_loaded"), sem("w_y_loaded"), sem("d_ready")
        last_loaded, last_stored = sem("last_loaded"), sem("last_stored")
        last_added = [sem(f"last_added{i}") for i in range(2)]
        w_in_loaded = [sem(f"w_in_loaded{i}") for i in range(W_IN_RING)]
        gate_loaded, b_stored = sem("gate_loaded"), sem("b_stored")
        b_loaded, y_stored = ([sem(f"{n}{i}") for i in range(2)] for n in ("b_loaded", "y_stored"))
        fin_loaded, fin_added, fin_stored = ([sem(f"fin_{n}{i}") for i in range(2)] for n in ("loaded", "added", "stored"))
        fin_free, idx_in_ready, mod_ready = (sem(n) for n in ("fin_free", "idx_in_ready", "mod1_ready"))
        work_ready, work_empty = ([sem(f"work_{n}{i}") for i in range(2)] for n in ("ready", "empty"))
        out_ready, out_empty = sem("out_ready"), sem("out_empty")
        first_tapped, tap_done, halo_done = sem("first_tapped"), sem("tap_done"), sem("halo_done")
        xm_ready, zs_ready, dt_exp, dt_log, dt_ready, u_ready = (sem(n) for n in ("xm_ready", "zs_ready", "dt_exp", "dt_log", "dt_ready", "u_ready"))
        da_ready, inputs_ready, scanned, turned, summed, carried = (sem(n) for n in ("da_ready", "inputs_ready", "scanned", "turned1", "summed", "carried"))
        passed = sem("passed1")
        block = ctx.enter_context(nc.Block())

        def decay_bank(k):
            return banks[3 + k % 3] if k < FOUR_BANKS else banks[2 + (k - FOUR_BANKS) % 4]

        def apart(eng, semaphore, value):
            need(eng, semaphore, value)
            if not isinstance(value, int):
                eng.sem_inc(passed, 1)

        def work_bank(place, stage, i):
            return work_banks[place[1][stage, i] % 2]

        def claimed(pe, place, stage, i):
            n = place[1][stage, i]
            need(pe, work_empty[n % 2], place[0] + n // 2)
            return work_banks[n % 2]

        def filled_by(place, stage, i):
            n = place[1][stage, i]
            return work_ready[n % 2], place[0] + n // 2 + 1

        def read_by(place, stage, i):
            n = place[1][stage, i]
            return work_empty[n % 2], place[0] + n // 2 + 1

        def last_z(place, m):
            n = (m - KI // 2) if m else -2 * KI // 2
            return work_ready[n % 2], place[0] + n // 2 + 1

        def fills(place, stage, i):
            return work_ready[place[1][stage, i] % 2]

        def empties(place, stage, i):
            return work_empty[place[1][stage, i] % 2]

        def either(eng, first_chunk, both_chunks):
            largest = eng.value_load(g.idx_max[0:1, 0:1], min_val=0, max_val=SEQ - 1)
            with eng.If(largest < CHUNK):
                first_chunk()
            with eng.Else():
                both_chunks()

        def batches(eng, body):
            body(0)
            with eng.Fori(1, BATCH) as b:
                body(b)

        def turns(eng, turn, end):
            turn(0, 0, False, True)
            with eng.Fori(0, BATCH // 2 - 1) as pair:
                turn(2 * pair + 1, 1, True, True)
                turn(2 * pair + 2, 0, True, True)
            turn(BATCH - 1, 1, True, False)
            end()

        front_place = (0, FRONT)
        end_place = (turn_place(BATCH - 1)[0] + len(LAST_TURN) // 2, END)

        def chunk_place(it):
            return len(CHUNK_ORDER) // 2 * it, CHUNK_ORDER

        def w_in_uses(b, stage):
            n = KI // W_IN_RING
            if stage == "xm":
                return 0 if isinstance(b, int) and b == 0 else n + 2 * n * (b - 1)
            return 2 * n * b + (n if isinstance(b, int) and b == BATCH - 1 else 2 * n)

        @block.sync
        def _(sp):
            def load_weights():
                sp.dma_start(w_xp[:, :, :], a["L1_cond_W_xp"].rearrange("(k p) n -> p k n", p=P)).then_inc(weights_loaded, DMA)
                sp.dma_start(w_dt[:, :], a["L1_cond_W_dt"]).then_inc(weights_loaded, DMA)

            def load_w_y():
                sp.dma_start(w_y[:, :, :], a["L1_cond_W_out"].rearrange("(k p) n -> p k n", p=P)).then_inc(w_y_loaded, DMA)

            def load_w_in(m, stage, before):
                if before is not None:
                    need(sp, *before)
                at = m if stage == "xm" else KI + m
                sp.dma_start(w_in[:, m % W_IN_RING, :, :], w_in_dram[:, :, at * P:(at + 1) * P]).then_inc(w_in_loaded[m % W_IN_RING], DMA)

            def store_b(it, place):
                apart(sp, *read_by(place, "xd", 0))
                sp.dma_start(g.b_dram[bass.ds(it, 1)].rearrange("o s t -> (o s) t"), xd[RANK:RANK + STATE, :]).then_inc(b_stored, DMA)

            def load_b(it, s):
                apart(sp, b_stored, DMA * (it + 1))
                apart(sp, inputs_ready, HALVES * it + 2 * (s - 1))
                sp.dma_start(b_wide[:, s % 2, :], g.b_dram[bass.ds(it, 1), s, :].rearrange("o t -> (o t)").partition_broadcast(P)).then_inc(b_loaded[s % 2], DMA)

            def load_gate(b):
                sp.dma_start(gate[:, :], g.gate_dram[bass.ds(b, 1)].rearrange("o d -> (o d)").partition_broadcast(P)).then_inc(gate_loaded, DMA)

            def store_y(it, c, t):
                need(sp, out_empty, CT * it + t + 1)
                sp.dma_start(y_rows[c * CT + t], fin[:, t % 2, :]).then_inc(y_stored[t % 2], DMA)

            def load_fin(b, k, stores):
                if k < 2:
                    apart(sp, y_stored[k % 2], DMA * CT // 2 * stores)
                else:
                    apart(sp, fin_stored[k % 2], DMA * (NT // 2 * b + k // 2))
                sp.dma_start(fin[:, k % 2, :], x1_rows[bass.ds(b, 1), k].rearrange("o p d -> (o p) d")).then_inc(fin_loaded[k % 2], DMA)

            def store_fin(b, k):
                apart(sp, fin_added[k % 2], DMA * (NT // 2 * b + k // 2 + 1))
                sp.dma_start(out_rows[bass.ds(b, 1), k].rearrange("o p d -> (o p) d"), fin[:, k % 2, :]).then_inc(fin_stored[k % 2], DMA)

            def batch_tiles(tiles, b):
                return tiles[b].rearrange("t p d -> p t d")

            def all_stored(b):
                for i in range(2):
                    apart(sp, fin_stored[i], DMA * NT // 2 * (b + 1))

            def finish(b, stores):
                for k in range(2):
                    load_fin(b, k, stores)
                for k in range(NT):
                    store_fin(b, k)
                    if k + 2 < NT:
                        load_fin(b, k + 2, stores)
                all_stored(b)

            def turn(b, par, prev, more):
                place = turn_place(b)
                for s in range(STATE):
                    if more:
                        if s == 0:
                            for m in range(W_IN_RING):
                                load_w_in(m, "xm", last_z(place, m) if prev else filled_by(front_place, "xm", m + W_IN_RING))
                        for m in {3: (4, 5), 4: (6, 7)}.get(s, ()):
                            load_w_in(m, "xm", filled_by(place, "xm", m - W_IN_RING))
                        if s == 8:
                            store_b(b + 1, place)
                    for m in {5: (0,), 6: (1, 2), 7: (3,)}.get(s, ()):
                        load_w_in(m, "z", filled_by(place, "xm", m + W_IN_RING) if more else last_z(place, m))
                    for m in {9: (4, 5), 12: (6, 7)}.get(s, ()):
                        load_w_in(m, "z", filled_by(place, "z", m - W_IN_RING))
                    if prev:
                        if s in (3, 5, 6, 7):
                            store_y(b - 1, 0, (3, 5, 6, 7).index(s))
                        if s == 9:
                            load_fin(b - 1, 0, b)
                            load_fin(b - 1, 1, b)
                        if 10 <= s < 14:
                            for k in (2 * (s - 10), 2 * (s - 10) + 1):
                                store_fin(b - 1, k)
                                if k + 2 < NT:
                                    load_fin(b - 1, k + 2, b)
                    if s == 8:
                        load_gate(b)
                    if s == 2 and not more:
                        sp.wait_ge(*filled_by(place, "init", KI - 1))
                        sp.dma_start(xm[:, :, :], batch_tiles(x1_rows, b)).then_inc(last_loaded, DMA)
                    if s + 2 < STATE:
                        load_b(b, s + 2)
                    elif more:
                        load_b(b + 1, s + 2 - STATE)
                if prev:
                    all_stored(b - 1)
                sp.sem_inc(fin_free, 1)

            def first_chunk():
                for m in range(KI):
                    if m == W_IN_RING:
                        load_weights()
                    load_w_in(m, "xm", filled_by(front_place, "xm", m - W_IN_RING) if m >= W_IN_RING else None)
                load_w_y()
                store_b(0, front_place)
                load_b(0, 0)
                load_b(0, 1)

                def end():
                    for t in range(CT):
                        store_y(BATCH - 1, 0, t)
                    for i in range(2):
                        sp.wait_ge(last_added[i], DMA * NT // 2)
                        half = slice(i * NT // 2, (i + 1) * NT // 2)
                        sp.dma_start(batch_tiles(out_rows, BATCH - 1)[:, half, :], xm[:, half, :]).then_inc(last_stored, DMA)
                    sp.wait_ge(last_stored, 2 * DMA)

                turns(sp, turn, end)

            def both_chunks():
                def body(b):
                    for c in range(CHUNKS):
                        it = CHUNKS * b + c
                        place = chunk_place(it)
                        for m in range(KI):
                            load_w_in(m, "xm", filled_by(place, "xm", m - W_IN_RING) if m >= W_IN_RING else None)
                        store_b(it, place)
                        for s in range(STATE):
                            load_b(it, s)
                        load_gate(b)
                        for m in range(KI):
                            load_w_in(m, "z", filled_by(place, "z", m - W_IN_RING) if m >= W_IN_RING else filled_by(place, "xm", m + W_IN_RING))
                        for t in range(CT):
                            store_y(it, c, t)
                    finish(b, CHUNKS * (b + 1))
                    sp.sem_inc(fin_free, 1)

                load_weights()
                load_w_y()
                batches(sp, body)

            either(sp, first_chunk, both_chunks)

        @block.tensor
        def _(pe):
            pe.wait_ge(d_ready, KI)

            def norm_turned(it, place, i):
                need(pe, g.normed, CT * it + CT)
                out = claimed(pe, place, "h", i)
                for t in range(CT):
                    last = nc.tensor.transpose(out[:, t * P:(t + 1) * P], g.rows[:, t, i * P:(i + 1) * P], ident[:, :])
                last.then_inc(fills(place, "h", i), 1)

            def project_in(par, place, loads, stage, m, ks, norm_place):
                if ks[0] == 0:
                    out = claimed(pe, place, stage, m)
                    need(pe, w_in_loaded[m % W_IN_RING], DMA * (loads + m // W_IN_RING + 1))
                    if norm_place is not None:
                        for i in (KD - 2, KD - 1):
                            need(pe, *read_by(norm_place, "h", i))
                for k in ks:
                    last = nc.tensor.matmul(work_bank(place, stage, m)[:, :], w_in[:, m % W_IN_RING, k, :], h_t[:, par, k, :],
                                            start=(k == 0), stop=(k == KD - 1))
                if ks[-1] == KD - 1:
                    last.then_inc(fills(place, stage, m), 1)

            def project_xd(it, place, js):
                if js[0] == 0:
                    pe.wait_ge(weights_loaded, 2 * DMA)
                    claimed(pe, place, "xd", 0)
                for j in js:
                    need(pe, xm_ready, KI // 2 * it + j // 2 + 1)
                    last = nc.tensor.matmul(work_bank(place, "xd", 0)[0:XD, :], w_xp[:, j, :], xm[:, j, :], start=(j == 0), stop=(j == KI - 1))
                if js[-1] == KI - 1:
                    last.then_inc(fills(place, "xd", 0), 1)

            def c_turned(place):
                out = claimed(pe, place, "C", 0)
                need(pe, *read_by(place, "xd", 0))
                for t in range(CT):
                    last = nc.tensor.transpose(out[:, t * XD:(t + 1) * XD], xd[:, t * P:(t + 1) * P], ident[0:XD, 0:XD])
                last.then_inc(fills(place, "C", 0), 1)

            def project_dt(place, j):
                out = claimed(pe, place, "dt", j)
                nc.tensor.matmul(out[:, :], w_dt[:, j * P:(j + 1) * P], xd[0:RANK, :], start=True, stop=True).then_inc(fills(place, "dt", j), 1)

            def x_turned(place, j):
                out = claimed(pe, place, "init", j)
                for t in range(CT):
                    last = nc.tensor.matmul(out[:, t * P:(t + 1) * P], xm[:, j, t * P:(t + 1) * P], d_diag[:, j, :], start=True, stop=True)
                last.then_inc(fills(place, "init", j), 1)

            def states_turned(it, q, t):
                n = CT * q + t
                if t == 0:
                    need(pe, scanned, BLOCKS * it + 4 * (q + 1))
                need(pe, summed, CT * HALVES * it + max(n - len(state_banks) + 1, 0))
                for j in range(4):
                    last = nc.tensor.transpose(state_banks[n % len(state_banks)][:, j * P:(j + 1) * P], hs[:, q % RING, j, t * P:(t + 1) * P], ident[:, :])
                last.then_inc(turned, 1)

            def y_turned(it, place, j):
                need(pe, summed, CT * HALVES * it + CT * HALVES)
                out = claimed(pe, place, "y", j)
                for t in range(CT):
                    last = nc.tensor.transpose(out[:, t * P:(t + 1) * P], acc[:, t, j * P:(j + 1) * P], ident[:, :])
                last.then_inc(fills(place, "y", j), 1)

            def project_out(it, place, t, js):
                if js[0] == 0:
                    need(pe, out_empty, CT * it + t)
                    if t == 0:
                        pe.wait_ge(w_y_loaded, DMA)
                        for j in (KI - 2, KI - 1):
                            apart(pe, *read_by(place, "y", j))
                for j in js:
                    last = nc.tensor.matmul(out_bank[:, :], zs[:, j, t * P:(t + 1) * P], w_y[:, j, :], start=(j == 0), stop=(j == KI - 1))
                if js[-1] == KI - 1:
                    last.then_inc(out_ready, 1)

            def turn(b, par, prev, more):
                place = turn_place(b)
                def swap_sums(j):
                    if prev:
                        y_turned(b - 1, place, j)
                    x_turned(place, j)

                for j in range(KI // 2):
                    swap_sums(j)
                for q in range(HALVES):
                    for t in range(CT):
                        states_turned(b, q, t)
                        if q == 0:
                            swap_sums(KI // 2 + t)
                        n = CT * q + t
                        if prev:
                            for tile, first in enumerate((4, 22, 32, 43)):
                                if first <= n < first + KI:
                                    project_out(b - 1, place, tile, [n - first])
                        if more:
                            if 12 <= n < 12 + KD:
                                norm_turned(b + 1, place, n - 12)
                            if 17 <= n < 17 + KI * KD:
                                project_in(1 - par, place, w_in_uses(b + 1, "xm"), "xm", (n - 17) // KD, [(n - 17) % KD], place)
                            if 53 <= n < 53 + KI:
                                project_xd(b + 1, place, [n - 53])
                            if n == 69:
                                c_turned(place)
                            for j, at in enumerate((70, 72, 73, 75, 90, 91, 93, 95)):
                                if n == at:
                                    project_dt(place, j)
                        for m, first in enumerate((49, 61, 65, 76, 80, 98, 102, 106)):
                            if first <= n < first + KD:
                                project_in(par, place, w_in_uses(b, "z"), "z", m, [n - first], None)

            def front(it, par, place, loads):
                for i in range(KD):
                    norm_turned(it, place, i)
                for m in range(KI):
                    project_in(par, place, loads, "xm", m, range(KD), place)
                project_xd(it, place, range(KI))
                c_turned(place)
                for j in range(KI):
                    project_dt(place, j)

            def first_chunk():
                def end():
                    for j in range(KI):
                        y_turned(BATCH - 1, end_place, j)
                    for t in range(CT):
                        project_out(BATCH - 1, end_place, t, range(KI))

                front(0, 0, front_place, 0)
                turns(pe, turn, end)

            def both_chunks():
                def body(b):
                    for c in range(CHUNKS):
                        it = CHUNKS * b + c
                        place, loads = chunk_place(it), 2 * KI // W_IN_RING * it
                        front(it, c, place, loads)
                        for j in range(KI):
                            x_turned(place, j)
                        for q in range(HALVES):
                            for t in range(CT):
                                states_turned(it, q, t)
                        for m in range(KI):
                            project_in(c, place, loads + KI // W_IN_RING, "z", m, range(KD), None)
                        for j in range(KI):
                            y_turned(it, place, j)
                        for t in range(CT):
                            project_out(it, place, t, range(KI))

                batches(pe, body)

            either(pe, first_chunk, both_chunks)

        @block.scalar
        def _(act):
            def filled(place, stage, i):
                need(act, *filled_by(place, stage, i))
                return work_bank(place, stage, i)

            def norm_modulated(it, par, place, i):
                need(act, mod_ready, it + 1)
                src = filled(place, "h", i)
                nc.scalar.activation(h_t[:, par, i, :], src[:, :], ACT.Identity, scale=mod_cur[:, i:i + 1],
                                     bias=mod_cur[:, KD + i:KD + i + 1]).then_inc(empties(place, "h", i), 1)

            def first_tap(place, m):
                src = filled(place, "xm", m)
                nc.scalar.activation(xm[:, m, :], src[:, :], ACT.Identity, scale=g.taps[:, m, TAPS - 1:TAPS],
                                     bias=column(g, "L1_cond_conv_b", m)).then_inc(first_tapped, 1)

            def silu_x(place, pair):
                for m in (2 * pair, 2 * pair + 1):
                    need(act, *read_by(place, "xm", m))
                part = xm[:, 2 * pair:2 * pair + 2, :]
                nc.scalar.activation(part, part, ACT.Silu).then_inc(xm_ready, 1)

            def keep_z(place, m):
                src = filled(place, "z", m)
                nc.scalar.copy(zs[:, m, :], src[:, :]).then_inc(empties(place, "z", m), 1)

            def silu_z(place, half):
                for m in (4 * half + 2, 4 * half + 3):
                    need(act, *read_by(place, "z", m))
                part = zs[:, 4 * half:4 * half + 4, :]
                nc.scalar.activation(part, part, ACT.Silu).then_inc(zs_ready, 1)

            def keep_xd(it, place):
                need(act, b_stored, DMA * it)
                src = filled(place, "xd", 0)
                nc.scalar.copy(xd[:, :], src[0:XD, :]).then_inc(empties(place, "xd", 0), 1)

            def keep_c(par, place):
                src = filled(place, "C", 0)
                nc.scalar.copy(c_t[:, par, :, :], src[:, 0:CT * XD].rearrange("p (t x) -> p t x", x=XD)[:, :, RANK + STATE:]).then_inc(empties(place, "C", 0), 1)

            def split_dt(it, par, place, j):
                if j == 4:
                    need(act, dt_ready, 2 * it + 1)
                src = filled(place, "dt", j)
                nc.scalar.activation(g.rows[:, j % 4, :], src[:, :], ACT.Relu, bias=column(g, "L1_cond_b_dt", j))
                nc.scalar.activation(dt[:, par, j, :], src[:, :], ACT.Abs, bias=column(g, "L1_cond_b_dt", j)).then_inc(empties(place, "dt", j), 1)

            def exp_dt(par, place, half):
                for j in (4 * half + 2, 4 * half + 3):
                    need(act, *read_by(place, "dt", j))
                part = dt[:, par, 4 * half:4 * half + 4, :]
                nc.scalar.activation(part, part, ACT.Exp, scale=-1.0).then_inc(dt_exp, 1)

            def log_dt(it, par, half):
                need(act, dt_exp, 2 * it + half + 1)
                part = dt[:, par, 4 * half:4 * half + 4, :]
                nc.scalar.activation(part, part, ACT.Ln, bias=1.0).then_inc(dt_log, 1)

            def start_sum(place, j):
                src = filled(place, "init", j)
                nc.scalar.copy(acc[:, :, j * P:(j + 1) * P], src[:, :].rearrange("p (t d) -> p t d", t=CT)).then_inc(empties(place, "init", j), 1)

            def decays(it, par, k):
                s, j = k // KI, k % KI
                if k < KI:
                    need(act, dt_ready, 2 * it + j // 4 + 1)
                need(act, scanned, BLOCKS * it + (k - 2 if k <= FOUR_BANKS else k - 3))
                nc.scalar.activation(decay_bank(k)[:, :], dt[:, par, j, :], ACT.Exp, scale=g.decay[:, j, s:s + 1]).then_inc(da_ready, 1)

            def turn(b, par, prev, more):
                place = turn_place(b)
                for k in range(3):
                    decays(b, par, k)
                for n in range(BLOCKS):
                    if more and 25 <= n < 25 + KI * TAPS and (n - 25) % TAPS == 0:
                        first_tap(place, (n - 25) // TAPS)
                    if n + 3 <= FOUR_BANKS:
                        decays(b, par, n + 3)
                    if FOUR_BANKS < n + 4 < BLOCKS:
                        decays(b, par, n + 4)
                    if n < KI:
                        start_sum(place, n)
                    if more:
                        if 17 <= n < 17 + KD:
                            norm_modulated(b + 1, 1 - par, place, n - 17)
                        if n in (33, 41, 49, 57):
                            silu_x(place, (n - 33) // 8)
                        if n == 65:
                            keep_xd(b + 1, place)
                        if n == 74:
                            keep_c(1 - par, place)
                        for j, at in enumerate((75, 77, 79, 81, 95, 97, 99, 101)):
                            if n == at:
                                split_dt(b + 1, 1 - par, place, j)
                        if n in (83, 103):
                            exp_dt(1 - par, place, n // 103)
                        if n in (86, 106):
                            log_dt(b + 1, 1 - par, n // 106)
                    for m, at in enumerate((58, 69, 73, 90, 91, 106, 110, 114)):
                        if n == at:
                            keep_z(place, m)
                    if n in (92, 121):
                        silu_z(place, n // 121)

            def front(it, par, place):
                for i in range(KD):
                    norm_modulated(it, par, place, i)
                for pair in range(KI // 2):
                    first_tap(place, 2 * pair)
                    first_tap(place, 2 * pair + 1)
                    silu_x(place, pair)
                keep_xd(it, place)
                keep_c(par, place)
                for half in range(2):
                    for j in range(4 * half, 4 * half + 4):
                        split_dt(it, par, place, j)
                    exp_dt(par, place, half)
                    log_dt(it, par, half)

            def first_chunk():
                front(0, 0, front_place)
                turns(act, turn, lambda: None)

            def both_chunks():
                def body(b):
                    for c in range(CHUNKS):
                        it = CHUNKS * b + c
                        place = chunk_place(it)
                        front(it, c, place)
                        for j in range(KI):
                            start_sum(place, j)
                        for k in range(BLOCKS):
                            decays(it, c, k)
                        for m in range(KI):
                            keep_z(place, m)
                        silu_z(place, 0)
                        silu_z(place, 1)

                batches(act, body)

            either(act, first_chunk, both_chunks)

        @block.gpsimd
        def _(pool):
            def gather(it, b, c):
                need(pool, dt_ready, 2 * it)
                apart(pool, idx_in_ready, b)
                gather_rows(nc, g, g.x1_dram, c)

            def add_dt(it, par, half):
                need(pool, dt_log, 2 * it + half + 1)
                part = dt[:, par, 4 * half:4 * half + 4, :]
                nc.gpsimd.tensor_tensor(part, part, g.rows[:, :, :], ALU.add).then_inc(dt_ready, 1)

            def dt_x(it, par, half):
                need(pool, dt_ready, 2 * it + half + 1)
                need(pool, xm_ready, KI // 2 * it + 2 * half + 2)
                need(pool, inputs_ready, HALVES * it - 2 + half + 1)
                part = slice(4 * half, 4 * half + 4)
                nc.gpsimd.tensor_tensor(u[:, part, :], dt[:, par, part, :], xm[:, part, :], ALU.mult).then_inc(u_ready, 1)

            def inputs(it, q):
                s, half = q // 2, q % 2
                if q < 2:
                    need(pool, u_ready, 2 * it + half + 1)
                if half == 0:
                    need(pool, b_loaded[s % 2], DMA * (STATE // 2 * it + s // 2 + 1))
                need(pool, turned, CT * HALVES * it + CT * (q - RING + 1))
                nc.gpsimd.tensor_tensor(hs[:, q % RING, :, :], u[:, 4 * half:4 * half + 4, :], b_wide[:, s % 2, :].unsqueeze(1).to_broadcast([P, 4, CHUNK]),
                                        ALU.mult).then_inc(inputs_ready, 1)

            def y_complete(stores):
                for i in range(2):
                    apart(pool, y_stored[i], DMA * CT // 2 * stores)

            def add_y(b, k, reach):
                apart(pool, fin_loaded[k % 2], DMA * (NT // 2 * b + k // 2 + 1))
                nc.gpsimd.indirect_dma_start(fin[:, k % 2, :], None, g.y_dram[0:reach, :], bass.IndirectOffsetOnAxis(g.idx_first[:, k:k + 1], axis=0),
                                             compute_op=ALU.add).then_inc(fin_added[k % 2], DMA)

            def turn(b, par, prev, more):
                for q in range(HALVES):
                    inputs(b, q)
                    if more and q >= HALVES - 2:
                        dt_x(b + 1, 1 - par, q - (HALVES - 2))
                    if more:
                        if q == 1:
                            gather(b + 1, b + 1, 0)
                        if q == 4:
                            rows_rsqrt(nc, g, b + 1)
                        if q == 24:
                            add_dt(b + 1, 1 - par, 0)
                        if q == 29:
                            add_dt(b + 1, 1 - par, 1)
                    if prev and 20 <= q < 20 + NT:
                        if q == 20:
                            y_complete(b)
                        add_y(b - 1, q - 20, CHUNK)

            def finish(b, stores, reach):
                y_complete(stores)
                for k in range(NT):
                    add_y(b, k, reach)

            def first_chunk():
                def end():
                    y_complete(BATCH)
                    pool.wait_ge(last_loaded, DMA)
                    for k in range(NT):
                        nc.gpsimd.indirect_dma_start(xm[:, k, :], None, g.y_dram[0:CHUNK, :], bass.IndirectOffsetOnAxis(g.idx_first[:, k:k + 1], axis=0),
                                                     compute_op=ALU.add).then_inc(last_added[k // (NT // 2)], DMA)

                turns(pool, turn, end)

            def both_chunks():
                def body(b):
                    for c in range(CHUNKS):
                        it = CHUNKS * b + c
                        if not (isinstance(it, int) and it == 0):
                            gather(it, b, c)
                            rows_rsqrt(nc, g, it)
                        for q in range(HALVES):
                            inputs(it, q)
                    finish(b, CHUNKS * (b + 1), SEQ)

                batches(pool, body)

            either(pool, first_chunk, both_chunks)

        @block.vector
        def _(dve):
            def modulate(b):
                dve.sem_inc(passed, 1)
                nc.vector.tensor_copy(mod_cur[:, :], g.mod_l1[:, bass.ds(b, 1), :].rearrange("p o i -> p (o i)")).then_inc(mod_ready, 1)

            def tap(it, place, m, back):
                bank, w = work_bank(place, "xm", m), g.taps[:, m, TAPS - 1 - back:TAPS - back]
                if back == 1:
                    need(dve, first_tapped, KI * it + m + 1)
                else:
                    need(dve, tap_done, (TAPS - 2) * (KI * it + m) + back - 1)
                last = back == TAPS - 1
                nc.vector.scalar_tensor_tensor(xm[:, m, back:], bank[:, 0:CHUNK - back], w, xm[:, m, back:], ALU.mult,
                                               ALU.add).then_inc(empties(place, "xm", m) if last else tap_done, 1)

            def halo_taps(it, m, done):
                need(dve, first_tapped, KI * it + m + 1)
                for back in range(1, TAPS):
                    need(dve, halo_done, done + back - 1)
                    nc.vector.scalar_tensor_tensor(xm[:, m, 0:back], halo[:, m, TAPS - 1 - back:], g.taps[:, m, TAPS - 1 - back:TAPS - back],
                                                   xm[:, m, 0:back], ALU.mult, ALU.add).then_inc(halo_done, 1)
                need(dve, halo_done, done + TAPS - 1)

            def add_dt(it, par, half):
                part = slice(4 * half, 4 * half + 4)
                need(dve, dt_log, 2 * it + half + 1)
                nc.vector.tensor_tensor(dt[:, par, part, :], dt[:, par, part, :], g.rows[:, :, :], ALU.add).then_inc(dt_ready, 1)

            def finish_dt(it, par, half):
                part = slice(4 * half, 4 * half + 4)
                add_dt(it, par, half)
                need(dve, dt_ready, 2 * it + half + 1)
                need(dve, xm_ready, KI // 2 * it + 2 * half + 2)
                nc.vector.tensor_tensor(u[:, part, :], dt[:, par, part, :], xm[:, part, :], ALU.mult).then_inc(u_ready, 1)

            def scan(it, k):
                need(dve, da_ready, BLOCKS * it + k + 1)
                if k % 4 == 0:
                    need(dve, inputs_ready, HALVES * it + k // 4 + 1)
                block = hs[:, k // 4 % RING, k % 4, :]
                nc.vector.tensor_tensor_scan(block, decay_bank(k)[:, :], block, 0.0, ALU.mult, ALU.add).then_inc(scanned, 1)

            def scan_on(it, b, c, q):
                for k in range(4 * q, 4 * q + 4):
                    s, j = k // KI, k % KI
                    need(dve, da_ready, BLOCKS * it + k + 1)
                    need(dve, inputs_ready, HALVES * it + q + 1)
                    need(dve, carried, BLOCKS * (b + c))
                    out = hs[:, q % RING, k % 4, :]
                    nc.vector.tensor_tensor_scan(out, decay_bank(k)[:, :], out, carry[:, j, s:s + 1] if c else 0.0,
                                                 ALU.mult, ALU.add).then_inc(scanned, 1)
                    if c == 0:
                        need(dve, scanned, BLOCKS * it + k + 1)
                        nc.vector.tensor_copy(carry[:, j, s:s + 1], out[:, CHUNK - 1:CHUNK]).then_inc(carried, 1)

            def add_states(it, par, place, q, t):
                s, jg = q // 2, q % 2
                if q < 2:
                    for j in (4 * jg + 2, 4 * jg + 3):
                        need(dve, *read_by(place, "init", j))
                else:
                    need(dve, summed, CT * HALVES * it + CT * (q - 2) + t + 1)
                need(dve, turned, CT * HALVES * it + CT * q + t + 1)
                part = acc[:, t, jg * 512:(jg + 1) * 512]
                nc.vector.scalar_tensor_tensor(part, state_banks[(CT * q + t) % len(state_banks)][:, :], c_t[:, par, t, s:s + 1], part, ALU.mult, ALU.add).then_inc(summed, 1)

            def gate_y(it, place, j):
                need(dve, zs_ready, 2 * it + j // 4 + 1)
                need(dve, *filled_by(place, "y", j))
                nc.vector.tensor_tensor(zs[:, j, :], work_bank(place, "y", j)[:, :], zs[:, j, :], ALU.mult).then_inc(empties(place, "y", j), 1)

            def gate_out(it, t, finals):
                if t == 0:
                    need(dve, gate_loaded, DMA * (it + 1))
                    need(dve, fin_free, finals)
                if t >= 2:
                    need(dve, y_stored[t % 2], DMA * (CT // 2 * it + t // 2))
                need(dve, out_ready, CT * it + t + 1)
                nc.vector.tensor_tensor(fin[:, t % 2, :], out_bank[:, :], gate[:, :], ALU.mult).then_inc(out_empty, 1)

            def next_rows():
                nc.vector.tensor_scalar(g.idx_in[:, :], g.idx_in[:, :], SEQ, None, ALU.add).then_inc(idx_in_ready, 1)

            def turn(b, par, prev, more):
                place = turn_place(b)
                for q in range(HALVES):
                    for t in range(CT):
                        n = CT * q + t
                        scan(b, n)
                        if q:
                            add_states(b, par, place, q - 1, t)
                        if prev:
                            if q < 2:
                                gate_y(b - 1, place, 4 * q + t)
                            for tile, at in enumerate((17, 35, 45, 56)):
                                if n == at:
                                    gate_out(b - 1, tile, b)
                        if more and 25 <= n < 25 + KI * TAPS:
                            for back in ((), (1,), (2, 3), ())[(n - 25) % TAPS]:
                                tap(b + 1, place, (n - 25) // TAPS, back)
                    if more:
                        if q == 2:
                            modulate(b + 1)
                            rows_moments(nc, g, b + 1, passed)
                        if q == 3:
                            rows_normed(nc, g, b + 1)
                        if q == 4:
                            next_rows()
                for t in range(CT):
                    add_states(b, par, place, HALVES - 1, t)

            def first_chunk():
                modulate(0)
                next_rows()
                for m in range(KI):
                    for back in range(1, TAPS):
                        tap(0, front_place, m, back)
                for half in range(2):
                    finish_dt(0, 0, half)

                def end():
                    for j in range(KI):
                        gate_y(BATCH - 1, end_place, j)
                    for t in range(CT):
                        gate_out(BATCH - 1, t, BATCH)

                turns(dve, turn, end)

            def both_chunks():
                def body(b):
                    for c in range(CHUNKS):
                        it = CHUNKS * b + c
                        place = chunk_place(it)
                        halos = KI * (1 + TAPS - 1) * b
                        modulate(b)
                        if not (isinstance(it, int) and it == 0):
                            rows_moments(nc, g, it, passed)
                            rows_normed(nc, g, it)
                        for m in range(KI):
                            if c:
                                halo_taps(it, m, halos + KI + (TAPS - 1) * m)
                            else:
                                apart(dve, first_tapped, KI * it + m + 1)
                                need(dve, halo_done, halos)
                                nc.vector.tensor_copy(halo[:, m, :], work_bank(place, "xm", m)[:, CHUNK - TAPS + 1:]).then_inc(halo_done, 1)
                            for back in range(1, TAPS):
                                tap(it, place, m, back)
                        for half in range(2):
                            finish_dt(it, c, half)
                        for q in range(HALVES):
                            scan_on(it, b, c, q)
                            for t in range(CT):
                                add_states(it, c, place, q, t)
                        for j in range(KI):
                            gate_y(it, place, j)
                        for t in range(CT):
                            gate_out(it, t, b)
                    next_rows()

                batches(dve, body)

            for j in range(KI):
                nc.vector.tensor_scalar(d_diag[:, j, :], ident[:, :], column(g, "L1_cond_D_param", j), None, ALU.mult).then_inc(d_ready, 1)
            dve.wait_ge(d_ready, KI)
            either(dve, first_chunk, both_chunks)


INPUTS = ["x", "cond_2048", "itok_S_0_1023", "mask_BxSx1_fk1"] + [
    f"L0_cond_{n}" for n in ("ln_w", "ln_b", "Wq", "bq", "Wk", "bk", "Wv", "bv", "W_emb", "b_emb", "ln2_w", "ln2_b", "W_out", "b_out")] + [
    f"L1_cond_{n}" for n in ("W_ada", "b_ada", "gamma", "beta", "W_in", "conv_w", "conv_b", "W_xp", "W_dt", "b_dt", "A_log", "D_param", "W_out")]


def kernel(**inputs):
    import numpy as np
    import concourse.bacc as bacc
    from concourse.bass_utils import run_bass_kernel_spmd

    nc = bacc.Bacc("TRN2", target_bir_lowering=False, num_devices=1)
    arrays, aps = {}, {}
    for name in INPUTS:
        arrays[f"in_{name}"] = np.ascontiguousarray(inputs[name])
        aps[name] = nc.dram_tensor(f"in_{name}", arrays[f"in_{name}"].shape, mybir.dt.from_np(arrays[f"in_{name}"].dtype), kind="ExternalInput").ap()
    aps["out"] = nc.dram_tensor("out", (BATCH, SEQ, DIM), F32, kind="ExternalOutput").ap()
    cond_mamba_kernel(nc, aps)
    result = run_bass_kernel_spmd(nc, [arrays], core_ids=[0])
    return result.results[0]["out"]
```
